# Optimizing a Trainium2 kernel written in Bass

```python
import numpy as np
import jax
import jax.numpy as jnp

def _softmax(x, axis=-1):
    return jax.nn.softmax(x, axis=axis)

def _gelu(x):
    return jax.nn.gelu(x, approximate=True)

def _silu(x):
    return jax.nn.silu(x)

def _sigmoid(x):
    return jax.nn.sigmoid(x)

def _layernorm(x, axis=-1, eps=1e-05):
    m = jnp.mean(x, axis=axis, keepdims=True)
    v = jnp.var(x, axis=axis, keepdims=True)
    return (x - m) / jnp.sqrt(v + eps)

def _scatter_add(tgt, idx, src, axis=0):
    return tgt.at[idx].add(src)

def _segment_sum(src, seg, n):
    return jax.ops.segment_sum(src, seg, n)
kernel_name = 'mk_adj_resnorm_d4_adj_r2_98d504'

def setup_inputs(seed: int=0):
    np.random.seed(seed)
    _w = jnp.asarray

    def _rec_inputs():
        import jax
        import jax.numpy as jnp
        _gk = jax.random.key(seed)
        x = 7.22e-05 + 1 * jax.random.normal(jax.random.fold_in(_gk, 1), (2048, 512), jnp.float32)
        _a = jax.random.bernoulli(jax.random.fold_in(_gk, 2), 0.000976562, (2048, 2048))
        _a = jnp.logical_or(_a, jnp.swapaxes(_a, -1, -2))
        _a = jnp.logical_or(_a, jnp.eye(2048, dtype=bool))
        _af = _a.astype(jnp.float32)
        _d = jnp.maximum(_af.sum(-1), 1.0) ** (-0.5)
        _af = _af * _d[..., :, None] * _d[..., None, :]
        adj = _af
        return (x, adj)
    x, adj = _rec_inputs()

    def _L0_gnn_setup():
        import jax, jax.numpy as jnp
        import numpy as np
        N = 4096
        D = 512

        def adjacent_mat(adj):
            adj = adj + jnp.eye(adj.shape[0], dtype=adj.dtype)
            deg = jnp.sum(adj, axis=1)
            dinv = jnp.where(deg > 0, deg ** (-0.5), 0.0).astype(adj.dtype)
            return dinv[:, None] * adj * dinv[None, :]
        key = jax.random.key(seed)
        k1, k2 = jax.random.split(key)
        x = jax.random.normal(k1, (N, D), dtype=jnp.float32)
        Coefficient2 = 1e-08 * jnp.ones((N, N), dtype=jnp.float32)
        A = jax.random.uniform(k2, (N, N), dtype=jnp.float32)
        return {'x': x, 'Coefficient2': Coefficient2, 'A': A}
    _L0_gnn_all = _L0_gnn_setup()
    _L0_gnn_in = {k: v for k, v in _L0_gnn_all.items() if k in ()}
    del _L0_gnn_all

    def _L1_gnn_setup():
        import jax, jax.numpy as jnp
        import numpy as np
        N, H, E, HEADS = (1500, 512, 10000, 8)
        DK = H // HEADS
        key = jax.random.key(seed)
        k1, k2, k3, k4 = jax.random.split(key, 4)
        inst_feature = jax.random.normal(k1, (N, H), dtype=jnp.float32)
        rel_pair_index = jax.random.randint(k2, (E, 2), 0, N, dtype=jnp.int64)
        agg = jnp.zeros((N, N), dtype=jnp.float32)
        agg = agg.at[rel_pair_index[:, 0], rel_pair_index[:, 1]].set(1.0)
        agg = agg.at[jnp.arange(N), jnp.arange(N)].set(1.0)
        std = float(np.sqrt(2.0 / (H + DK)))
        Wq = jax.random.normal(k3, (H, H), dtype=jnp.float32) * std
        Wk = jax.random.normal(k4, (H, H), dtype=jnp.float32) * std
        bq = jnp.zeros((H,), dtype=jnp.float32)
        bk = jnp.zeros((H,), dtype=jnp.float32)
        return {'inst_feature': inst_feature, 'aggregator_matrix': agg, 'rel_pair_index': rel_pair_index, 'Wq': Wq, 'bq': bq, 'Wk': Wk, 'bk': bk}
    _L1_gnn_all = _L1_gnn_setup()
    _L1_gnn_in = {k: v for k, v in _L1_gnn_all.items() if k in ('rel_pair_index', 'Wq', 'bq', 'Wk', 'bk')}
    del _L1_gnn_all

    def _L2_gnn_setup():
        import jax, jax.numpy as jnp
        import numpy as np
        NBITS = 4
        N_NODES = 4096
        IN_F = 512
        OUT_F = 512

        def _act_quant(x, alpha, b):
            n = float(2 ** b - 1)
            xd = x / alpha
            xc = jnp.minimum(xd, 1.0)
            xq = jnp.round(xc * n) / n
            return xq * alpha

        def _weight_quant(w, alpha, b):
            n = float(2 ** b - 1)
            wd = w / alpha
            wc = jnp.clip(wd, -1.0, 1.0)
            wq = jnp.round(jnp.abs(wc) * n) / n * jnp.sign(wc)
            return wq * alpha
        key = jax.random.key(seed)
        k1, k2, k3 = jax.random.split(key, 3)
        stdv = 1.0 / np.sqrt(OUT_F)
        inp = {'input': jax.random.uniform(k1, (N_NODES, IN_F), dtype=jnp.float32), 'adj': jax.random.uniform(k2, (N_NODES, N_NODES), dtype=jnp.float32), 'adj_scaling_factor': jnp.float32(2.0), 'weight': jax.random.uniform(k3, (IN_F, OUT_F), minval=-stdv, maxval=stdv, dtype=jnp.float32), 'wgt_alpha': jnp.float32(3.0), 'act_alpha': jnp.float32(1.0), 'act_alpha2': jnp.float32(1.0)}
        return inp
    _L2_gnn_all = _L2_gnn_setup()
    _L2_gnn_in = {k: v for k, v in _L2_gnn_all.items() if k in ('adj_scaling_factor', 'weight', 'wgt_alpha', 'act_alpha', 'act_alpha2')}
    del _L2_gnn_all

    def _L3_gnn_setup():
        import jax, jax.numpy as jnp
        import numpy as np
        import math
        SENT_DIM = 512
        N_SENT = 2048
        key = jax.random.key(seed)
        ks = jax.random.split(key, 8)
        D = SENT_DIM
        s = 1.0 / math.sqrt(D)
        return {'sent_embed': jax.random.normal(ks[0], (N_SENT, D), dtype=jnp.float32), 'adj_tensor': jax.random.randint(ks[1], (N_SENT, N_SENT), 0, 2).astype(jnp.float32), 'W_q': jax.random.uniform(ks[2], (D, D), jnp.float32, -s, s), 'b_q': jax.random.uniform(ks[3], (D,), jnp.float32, -s, s), 'W_k': jax.random.uniform(ks[4], (D, D), jnp.float32, -s, s), 'b_k': jax.random.uniform(ks[5], (D,), jnp.float32, -s, s), 'W_v': jax.random.uniform(ks[6], (D, D), jnp.float32, -s, s), 'b_v': jax.random.uniform(ks[7], (D,), jnp.float32, -s, s)}
    _L3_gnn_all = _L3_gnn_setup()
    _L3_gnn_in = {k: v for k, v in _L3_gnn_all.items() if k in ('W_q', 'b_q', 'W_k', 'b_k', 'W_v', 'b_v')}
    del _L3_gnn_all
    return {'x': x, 'adj': adj, 'L1_gnn_rel_pair_index': _L1_gnn_in['rel_pair_index'], 'L1_gnn_Wq': _L1_gnn_in['Wq'], 'L1_gnn_bq': _L1_gnn_in['bq'], 'L1_gnn_Wk': _L1_gnn_in['Wk'], 'L1_gnn_bk': _L1_gnn_in['bk'], 'L2_gnn_adj_scaling_factor': _L2_gnn_in['adj_scaling_factor'], 'L2_gnn_weight': _L2_gnn_in['weight'], 'L2_gnn_wgt_alpha': _L2_gnn_in['wgt_alpha'], 'L2_gnn_act_alpha': _L2_gnn_in['act_alpha'], 'L2_gnn_act_alpha2': _L2_gnn_in['act_alpha2'], 'L3_gnn_W_q': _L3_gnn_in['W_q'], 'L3_gnn_b_q': _L3_gnn_in['b_q'], 'L3_gnn_W_k': _L3_gnn_in['W_k'], 'L3_gnn_b_k': _L3_gnn_in['b_k'], 'L3_gnn_W_v': _L3_gnn_in['W_v'], 'L3_gnn_b_v': _L3_gnn_in['b_v']}

def reference(x, adj, L1_gnn_rel_pair_index, L1_gnn_Wq, L1_gnn_bq, L1_gnn_Wk, L1_gnn_bk, L2_gnn_adj_scaling_factor, L2_gnn_weight, L2_gnn_wgt_alpha, L2_gnn_act_alpha, L2_gnn_act_alpha2, L3_gnn_W_q, L3_gnn_b_q, L3_gnn_W_k, L3_gnn_b_k, L3_gnn_W_v, L3_gnn_b_v):
    import jax
    import jax.numpy as jnp

    def _L0_gnn_ref(x, Coefficient2, A):
        import jax, jax.numpy as jnp
        import numpy as np
        N = 4096
        D = 512

        def adjacent_mat(adj):
            adj = adj + jnp.eye(adj.shape[0], dtype=adj.dtype)
            deg = jnp.sum(adj, axis=1)
            dinv = jnp.where(deg > 0, deg ** (-0.5), 0.0).astype(adj.dtype)
            return dinv[:, None] * adj * dinv[None, :]
        A_c = jax.lax.stop_gradient(A)
        adj = adjacent_mat((A_c + A_c.T) * 0.5)
        y = Coefficient2 @ adj
        y = y @ x
        return y

    def _L1_gnn_ref(inst_feature, aggregator_matrix, rel_pair_index, Wq, bq, Wk, bk):
        import jax, jax.numpy as jnp
        import numpy as np
        N, H, E, HEADS = (1500, 512, 10000, 8)
        DK = H // HEADS
        n = inst_feature.shape[0]
        sub = rel_pair_index[:, 0]
        obj = rel_pair_index[:, 1]
        q = (inst_feature[sub] @ Wq.T + bq).reshape(-1, HEADS, DK)
        k = (inst_feature[obj] @ Wk.T + bk).reshape(-1, HEADS, DK)
        att = ((q * k).sum(-1) / np.sqrt(DK)).T.astype(inst_feature.dtype)
        scores = jnp.zeros((HEADS, n, n), dtype=inst_feature.dtype)
        scores = scores.at[:, sub, obj].set(att)
        mask = (1.0 - aggregator_matrix).astype(bool)
        scores = jnp.where(mask[None], -jnp.inf, scores)
        di = jnp.arange(n)
        scores = scores.at[:, di, di].set(1e-07)
        attn = jax.nn.softmax(scores, axis=2)
        aggregator_factor = attn.sum(axis=0) / HEADS
        return aggregator_factor @ inst_feature

    def _L2_gnn_ref(input, adj, adj_scaling_factor, weight, wgt_alpha, act_alpha, act_alpha2):
        import jax, jax.numpy as jnp
        import numpy as np
        NBITS = 4
        N_NODES = 4096
        IN_F = 512
        OUT_F = 512

        def _act_quant(x, alpha, b):
            n = float(2 ** b - 1)
            xd = x / alpha
            xc = jnp.minimum(xd, 1.0)
            xq = jnp.round(xc * n) / n
            return xq * alpha

        def _weight_quant(w, alpha, b):
            n = float(2 ** b - 1)
            wd = w / alpha
            wc = jnp.clip(wd, -1.0, 1.0)
            wq = jnp.round(jnp.abs(wc) * n) / n * jnp.sign(wc)
            return wq * alpha
        bit = NBITS
        wb = bit - 1
        mean = jax.lax.stop_gradient(jnp.mean(weight))
        std = jax.lax.stop_gradient(jnp.std(weight, ddof=1))
        w_norm = (weight - mean) / std
        weight_q = _weight_quant(w_norm, wgt_alpha, wb)
        x = _act_quant(input, act_alpha, bit)
        wgt_delta = wgt_alpha / (2 ** (bit - 1) - 1)
        act_delta = act_alpha / (2 ** bit - 1)
        support = jnp.matmul(x / act_delta, weight_q / wgt_delta)
        support = support * act_delta * wgt_delta
        support = jax.nn.relu(support)
        support_q = _act_quant(support, act_alpha2, bit)
        support_delta = act_alpha2 / (2 ** bit - 1)
        output = jnp.matmul(adj / adj_scaling_factor, support_q / support_delta)
        return output * adj_scaling_factor * support_delta

    def _L3_gnn_ref(sent_embed, adj_tensor, W_q, b_q, W_k, b_k, W_v, b_v):
        import jax, jax.numpy as jnp
        import numpy as np
        import math
        SENT_DIM = 512
        N_SENT = 2048
        q = sent_embed @ W_q.T + b_q
        k = sent_embed @ W_k.T + b_k
        v = sent_embed @ W_v.T + b_v
        scale = 1.0 / math.sqrt(sent_embed.shape[-1])
        z = scale * (q @ k.T)
        spare_z = z * adj_tensor
        spare_z = jnp.where(spare_z == 0.0, jnp.asarray(-10000.0, spare_z.dtype), spare_z)
        attn = jax.nn.softmax(spare_z, axis=1)
        out = attn @ v
        return jax.nn.relu(out)
    x = _layernorm(x + _L0_gnn_ref(x, adj, adj), axis=-1)
    x = _layernorm(x + _L1_gnn_ref(x, adj, L1_gnn_rel_pair_index, L1_gnn_Wq, L1_gnn_bq, L1_gnn_Wk, L1_gnn_bk), axis=-1)
    x = _layernorm(x + _L2_gnn_ref(x, adj, L2_gnn_adj_scaling_factor, L2_gnn_weight, L2_gnn_wgt_alpha, L2_gnn_act_alpha, L2_gnn_act_alpha2), axis=-1)
    x = _layernorm(x + _L3_gnn_ref(x, adj, L3_gnn_W_q, L3_gnn_b_q, L3_gnn_W_k, L3_gnn_b_k, L3_gnn_W_v, L3_gnn_b_v), axis=-1)
    return x

_drawn_inputs = setup_inputs


def setup_inputs(seed=0):
    import zlib

    import numpy as np

    out = dict(_drawn_inputs(seed))
    spreads = {'L1_gnn_bq': (0.0, 0.1), 'L1_gnn_bk': (0.0, 0.1)}
    factors = {'L3_gnn_W_q': 5.6,
     'L3_gnn_b_q': 34.905,
     'L3_gnn_W_k': 5.468,
     'L3_gnn_b_k': 64.0,
     'L3_gnn_b_v': 3.233}
    for name, (base, spread) in spreads.items():
        noise = np.random.default_rng([zlib.crc32(name.encode()), seed]).standard_normal(out[name].shape)
        drawn = base * np.exp(spread * noise) if base else spread * noise
        out[name] = jnp.asarray(drawn.astype(out[name].dtype))
    for name, factor in factors.items():
        out[name] = (out[name] * factor).astype(out[name].dtype)
    return out
```

```python
from contextlib import ExitStack

import numpy as np

import concourse.bass as bass
import concourse.mybir as mybir

FP32 = mybir.dt.float32
FP16 = mybir.dt.float16
INT32 = mybir.dt.int32
ALU = mybir.AluOpType
ACT = mybir.ActivationFunctionType
AX = mybir.AxisListType

P = 128
N = 2048
D = 512
T = N // P
K4 = D // P
HALF = N // 2
HT = HALF // P
HEADS = 8
DK = D // HEADS
EDGES = 10000
ET = -(-EDGES // P)
EPS = 1e-5
S64 = 64.0
PSCALE = 1024.0
ZS = 4.0
SCALE = ZS / float(np.sqrt(D))
MASKED = -10000.0
MAGIC = 12582912.0
ACT_STEPS = 15.0
WGT_STEPS = 7.0
ARENA = 79872


def ds(i, n):
    return bass.ds(i, n)


def pairs(eng, start, end):
    return eng.Fori(start, end - 1, 2)


def wait_apart(eng, semaphore, n, waited):
    eng.wait_ge(semaphore, n)
    eng.sem_inc(waited, 1)


class Memory:

    def __init__(self, nc, ctx):
        self.nc, self.ctx, self.sems = nc, ctx, {}
        self.big = ctx.enter_context(nc.sbuf_tensor("big", [P, T, 4096], FP16))
        self.arena = ctx.enter_context(nc.sbuf_tensor("arena", [P, ARENA // 4], FP32))
        self.psum = ctx.enter_context(nc.psum_tensor("psum", [P, 8, 512], FP32))
        self.ident = ctx.enter_context(nc.sbuf_tensor("ident", [P, P], FP16))
        self.mean_matrix = ctx.enter_context(nc.sbuf_tensor("mean_matrix", [P, P], FP32))
        self.scal = ctx.enter_context(nc.sbuf_tensor("scal", [P, 4], FP32))
        self.small = ctx.enter_context(nc.sbuf_tensor("small", [P, 240], FP32))
        self.at = 0
        self.minus_half = self.col()
        self.f_out = self.col()
        self.relation_cols = self.col(13)

    def sem(self, name):
        if name not in self.sems:
            self.sems[name] = self.ctx.enter_context(self.nc.semaphore(name))
        return self.sems[name]

    def col(self, n=1):
        self.at += n
        assert self.at <= 240
        return self.small[:, self.at - n:self.at]

    def carve(self, at, dims, dt):
        size = int(np.prod(dims)) * (2 if dt == FP16 else 4)
        assert at % 4 == 0 and at + size <= ARENA, (at, size)
        v = self.arena[:, at // 4:(at + size) // 4]
        if dt != FP32:
            v = v.bitcast(dt)
        if len(dims) > 1:
            n = "abcd"[:len(dims)]
            v = v.rearrange(f"p ({' '.join(n)}) -> p {' '.join(n)}", **dict(zip(n, dims)))
        return v

    def bank16(self, b, n=8):
        nb = n // 8
        return self.psum[:, b:b + nb, :].rearrange("p a b -> p (a b)").bitcast(FP16)\
            .rearrange("p (a b) -> p a b", a=n)


def propagation(nc, mem, a, x1_dram, x2_dram, flag):
    big, psum, ident, S, carve = mem.big, mem.psum, mem.ident, mem.sem, mem.carve
    u = carve(0, [2, T, D], FP16)
    rows = [carve(32768 + 8192 * b, [2, HALF], FP32) for b in range(2)]
    rows0 = [carve(8192, [2, HALF], FP32), carve(24576, [2, HALF], FP32)]
    mpair = [carve(49152 + 4096 * b, [2, HALF], FP16) for b in range(2)]
    zpair = [carve(57344 + 2048 * b, [2, D], FP16) for b in range(2)]
    xbuf = [carve(61440 + 2048 * b, [D], FP32) for b in range(2)]
    wq8 = carve(65536, [K4, D], FP16)
    wraw = carve(0, [K4, D], FP32)
    sup = carve(32768, [T, D], FP16)
    qpair = [carve(49152 + 2048 * b, [2, D], FP16) for b in range(2)]
    qT = [carve(53248 + 2048 * b, [2 * K4, P], FP16) for b in range(2)]
    hbuf = carve(57344, [D], FP32)
    qbuf = carve(59392, [D], FP32)
    x1buf = [carve(69632 + 2048 * b, [D], FP32) for b in range(2)]
    x2buf = [carve(73728 + 2048 * b, [D], FP32) for b in range(2)]
    sbuf2 = carve(77824, [D], FP32)

    col = mem.col
    sum_m, sum_a, sum_t = col(T), col(T), col(T)
    dz, dm = col(T), col(T)
    deg = [col() for _ in range(4)]
    stats, mv, mv2, rs1, rs2 = col(6), col(2), col(2), col(), col()
    wstats, wmv, wmean, wvar, wtmp = col(24), col(2), col(), col(), [col() for _ in range(4)]
    r_act, c_sup = col(), col()
    ones_seen, ones_diag, ones_tmp = col(2 * T), col(T), col(3)
    t_factor = col()

    def regions(part, half, k):
        if isinstance(k, int):
            at = slice((part * T + k) * P, (part * T + k + 1) * P)
        else:
            at = ds((k + part * T) * P, P)
        return big[:, HT * half:HT * half + HT, at]

    def blocks(v):
        return v.rearrange("p (a b) -> p a b", b=P)

    with nc.Block() as block:
        @block.sync
        def _(sp):
            sp.dma_start(mem.scal[:], a["scalars"]).then_inc(S("scalars_in"), 16)
            sp.dma_start(wraw, a["L2_w"].rearrange("(k p) d -> p k d", p=P)).then_inc(S("w_in"), 16)

            def load_first(k, b):
                r = ds(k * P, P)
                sp.wait_ge(S("rows_free"), k + 1)
                sp.dma_start(rows0[b][:, 0, :], a["adj"][r, 0:HALF]).then_inc(S(f"rows_in{b}"), 16)
                sp.dma_start(rows0[b][:, 1, :], a["adjT"][r, 0:HALF]).then_inc(S(f"rows_in{b}"), 16)
                sp.dma_start(rows[b][:, 0, :], a["adj"][r, HALF:N]).then_inc(S(f"rows_in{b}"), 16)
                sp.dma_start(rows[b][:, 1, :], a["adjT"][r, HALF:N]).then_inc(S(f"rows_in{b}"), 16)
                sp.wait_ge(S("x_free"), k + 1)
                sp.dma_start(xbuf[b], a["x"][r, :]).then_inc(S(f"x_in{b}"), 16)

            with pairs(sp, 0, T) as k:
                for b in range(2):
                    load_first(k + b, b)

            def load_second(k, b):
                r = ds(k * P, P)
                sp.wait_ge(S("rows_free"), k + T + 1)
                sp.dma_start(rows[b][:, 0, :], a["adj"][r, HALF:N]).then_inc(S(f"rows2_in{b}"), 16)
                sp.dma_start(rows[b][:, 1, :], a["adjT"][r, HALF:N]).then_inc(S(f"rows2_in{b}"), 16)
                sp.wait_ge(S("x_free"), k + T + 1)
                sp.dma_start(xbuf[b], a["x"][r, :]).then_inc(S(f"x_in{b}"), 16)

            with pairs(sp, 0, T) as k:
                for b in range(2):
                    load_second(k + b, b)

            with pairs(sp, 0, T) as m:
                for b in range(2):
                    r = ds((m + b) * P, P)
                    sp.wait_ge(S("x_free"), m + b + 2 * T + 1)
                    sp.dma_start(xbuf[b], a["x"][r, :]).then_inc(S(f"x_in{b}"), 16)
                    sp.wait_ge(S("x1_made"), m + b + 1)
                    sp.dma_start(x1_dram[r, :], x1buf[b]).then_inc(S(f"x1_kept{b}"), 16)
                    sp.wait_ge(S("x2_made"), m + b + 1)
                    sp.dma_start(x2_dram[r, :], x2buf[b]).then_inc(S(f"x2_kept{b}"), 16)
            for b in range(2):
                sp.wait_ge(S(f"x1_kept{b}"), 16 * (T // 2 + 1))
                sp.wait_ge(S(f"x2_kept{b}"), 16 * (T // 2 + 1))

        @block.gpsimd
        def _(pool):
            pool.memset(ident[:], 0.0).then_inc(S("setup"), 1)
            pool.memset(mem.mean_matrix[:], 1.0 / P).then_inc(S("setup"), 1)
            pool.memset(mem.minus_half, -0.5).then_inc(S("setup"), 1)
            pool.memset(t_factor, 0.5 / S64).then_inc(S("setup"), 1)
            pool.wait_ge(S("setup"), 4)
            pool.affine_select(out=ident[:], in_=ident[:], compare_op=ALU.not_equal, fill=1.0, base=0,
                               pattern=[[-1, P]], channel_multiplier=1).then_inc(S("setup"), 1)
            pool.wait_ge(S("w_var"), 1)
            pool.tensor_tensor(wtmp[2], wvar, mem.minus_half, ALU.pow).then_inc(S("w_rstd"), 1)

            def degree(k, b):
                c = ds(k, 1)
                pool.wait_ge(S("sum_m"), k + 1)
                pool.wait_ge(S("sums_at"), k + 1)
                pool.tensor_tensor(deg[0], sum_m[:, c], sum_a[:, c], ALU.add).then_inc(S("deg_a"), 1)
                pool.tensor_tensor(deg[1], sum_t[:, c], t_factor, ALU.mult).then_inc(S("deg_a"), 1)
                wait_apart(pool, S("deg_a"), k * 2 + 2, S("waited_pool"))
                pool.tensor_scalar(deg[2], deg[0], 0.5, 1.0, ALU.mult, ALU.add).then_inc(S("deg_b"), 1)
                pool.wait_ge(S("deg_b"), k + 1)
                pool.tensor_tensor(deg[3], deg[2], deg[1], ALU.add).then_inc(S("deg_c"), 1)
                wait_apart(pool, S("deg_c"), k + 1, S("waited_pool"))
                pool.tensor_scalar(deg[0], deg[3], 1e-37, None, ALU.max).then_inc(S("deg_d"), 1)
                pool.tensor_scalar(deg[1], deg[3], 0.0, S64, ALU.is_gt, ALU.mult).then_inc(S("deg_d"), 1)
                pool.wait_ge(S("deg_d"), k * 2 + 2)
                pool.tensor_tensor(deg[2], deg[0], mem.minus_half, ALU.pow).then_inc(S("deg_e"), 1)
                pool.wait_ge(S("deg_e"), k + 1)
                pool.tensor_tensor(dz[:, c], deg[2], deg[1], ALU.mult).then_inc(S("dz"), 1)

            with pairs(pool, 0, T) as k:
                for b in range(2):
                    degree(k + b, b)
            pool.wait_ge(S("dz"), T)
            pool.tensor_scalar(dm, dz, 0.5 / (S64 * S64), None, ALU.mult).then_inc(S("dm"), 1)

            with pool.Fori(0, T) as m:
                wait_apart(pool, S("aggr1"), m + 1, S("waited_pool"))
                pool.tensor_scalar(deg[0], mv[:, 1:2], EPS, None, ALU.add).then_inc(S("ve1"), 1)
                pool.wait_ge(S("ve1"), m + 1)
                pool.tensor_tensor(rs1, deg[0], mem.minus_half, ALU.pow).then_inc(S("rstd1"), 1)
                wait_apart(pool, S("aggr2"), m + 1, S("waited_pool"))
                pool.tensor_scalar(deg[1], mv2[:, 1:2], 4.0, EPS, ALU.mult, ALU.add).then_inc(S("ve2"), 1)
                pool.wait_ge(S("ve2"), m + 1)
                pool.tensor_tensor(deg[2], deg[1], mem.minus_half, ALU.pow).then_inc(S("pw2"), 1)
                wait_apart(pool, S("pw2"), m + 1, S("waited_pool"))
                pool.tensor_scalar(rs2, deg[2], 2.0, None, ALU.mult).then_inc(S("rstd2"), 1)

        @block.scalar
        def _(act):
            def rows_first(k, b):
                c = ds(k, 1)
                act.wait_ge(S(f"rows_in{b}"), (k - b) * 32 + 64)
                act.activation(regions(0, 0, k), blocks(rows0[b][:, 1, :]), ACT.Copy, scale=S64).then_inc(S("t_high"), 1)
                act.activation(regions(0, 1, k), blocks(rows[b][:, 1, :]), ACT.Copy, scale=S64,
                               accum_out=sum_t[:, c]).then_inc(S("t_high"), 1)
                act.activation(rows[b][:, 0, :], rows[b][:, 0, :], ACT.Copy,
                               accum_out=sum_a[:, c]).then_inc(S("sums_at"), 1)
                m_high(k, b, rows0[b], k + 1)

            def m_high(k, b, src, n):
                act.wait_ge(S("m_sum"), n)
                act.wait_ge(S("m_free"), n)
                act.activation(mpair[b][:, 0, :], src[:, 0, :], ACT.Copy, scale=S64).then_inc(S("m_high"), 1)

            def z_high(k, b, n, xn):
                act.wait_ge(S(f"x_in{b}"), xn)
                act.wait_ge(S("z_free"), n)
                act.activation(zpair[b][:, 0, :], xbuf[b], ACT.Copy, scale=dz[:, ds(k, 1)]).then_inc(S("z_high"), 1)

            def first(k, b):
                rows_first(k, b)
                act.wait_ge(S("dz"), k + 1)
                z_high(k, b, k + 1, (k - b) * 8 + 16)

            act.sem_inc(S("m_free"), 2)
            with pairs(act, 0, T) as k:
                for b in range(2):
                    first(k + b, b)

            def u_high(half):
                def one(j):
                    act.wait_ge(S("sweep_done"), half + 1)
                    act.activation(u[:, 0, HT * half + j, :], psum[:, j, :], ACT.Copy,
                                   scale=dm[:, HT * half + j:HT * half + j + 1]).then_inc(S("u_high"), 1)
                act.wait_ge(S("dm"), 1)
                for j in range(HT):
                    one(j)
            u_high(0)

            def second(k, b):
                act.wait_ge(S(f"rows2_in{b}"), (k - b) * 16 + 32)
                m_high(k, b, rows[b], k + T + 1)
                z_high(k, b, k + T + 1, (k - b) * 8 + 16 * (T // 2) + 16)
            with pairs(act, 0, T) as k:
                for b in range(2):
                    second(k + b, b)
            u_high(1)

            with pairs(act, 0, T) as m:
                for b in range(2):
                    act.wait_ge(S("qT_psum"), m + b + 1)
                    act.wait_ge(S("qT_free"), m + b + 1)
                    act.activation(qT[b], mem.bank16(2 + b), ACT.Copy).then_inc(S("qT_made"), 1)

        @block.vector
        def _(dve):
            dve.sem_inc(S("rows_free"), 2)
            dve.sem_inc(S("x_free"), 2)
            dve.sem_inc(S("z_free"), 2)
            dve.sem_inc(S("qT_free"), 2)
            dve.sem_inc(S("sup_free"), 2)
            dve.sem_inc(S("au_free"), 2)
            dve.sem_inc(S("q_free"), 2)
            for b in range(2):
                dve.sem_inc(S(f"x1_kept{b}"), 16)
                dve.sem_inc(S(f"x2_kept{b}"), 16)
            step = [0]

            def chained(ins):
                step[0] += 1
                ins.then_inc(S("w_chain"), 1)
                dve.wait_ge(S("w_chain"), step[0])

            dve.wait_ge(S("scalars_in"), 16)
            dve.wait_ge(S("w_in"), 16)
            for k in range(K4):
                last = dve.bn_stats(wstats[:, 6 * k:6 * k + 6], wraw[:, k, :])
            chained(last)
            chained(dve.bn_aggr(wmv, wstats))
            dve.engine_nop().then_inc(S("w_part_mean"), 1)
            dve.wait_ge(S("w_mean"), 1)
            chained(dve.tensor_copy(wmean, psum[:, 7, 0:1]))
            chained(dve.tensor_tensor(wtmp[0], wmv[:, 0:1], wmean, ALU.subtract))
            chained(dve.tensor_tensor(wtmp[1], wtmp[0], wtmp[0], ALU.mult))
            dve.tensor_tensor(wtmp[3], wtmp[1], wmv[:, 1:2], ALU.add).then_inc(S("w_part_var"), 1)
            dve.wait_ge(S("w_pvar"), 1)
            dve.tensor_scalar(wvar, psum[:, 7, 1:2], D * D / (D * D - 1.0), None, ALU.mult).then_inc(S("w_var"), 1)
            act_alpha, wgt_alpha, act_alpha2, adj_scale = (mem.scal[:, i:i + 1] for i in range(4))
            chained(dve.reciprocal(wtmp[1], wgt_alpha))
            dve.wait_ge(S("w_rstd"), 1)
            chained(dve.tensor_tensor(wtmp[0], wtmp[2], wtmp[1], ALU.mult))
            chained(dve.tensor_scalar(wraw, wraw, wmean, wtmp[0], ALU.subtract, ALU.mult))
            chained(dve.tensor_scalar(wraw, wraw, 1.0, -1.0, ALU.min, ALU.max))
            chained(dve.tensor_scalar(wraw, wraw, WGT_STEPS, MAGIC, ALU.mult, ALU.add))
            dve.tensor_scalar(wq8, wraw, MAGIC, None, ALU.subtract).then_inc(S("wq8"), 1)
            chained(dve.reciprocal(r_act, act_alpha))
            chained(dve.reciprocal(wtmp[1], act_alpha2))
            chained(dve.tensor_scalar(wtmp[0], act_alpha, 1.0 / ACT_STEPS, 1.0 / WGT_STEPS, ALU.mult, ALU.mult))
            chained(dve.tensor_tensor(wtmp[2], wtmp[0], wgt_alpha, ALU.mult))
            chained(dve.tensor_tensor(c_sup, wtmp[2], wtmp[1], ALU.mult))
            chained(dve.reciprocal(wtmp[0], adj_scale))
            chained(dve.tensor_tensor(wtmp[1], wtmp[0], adj_scale, ALU.mult))
            chained(dve.tensor_tensor(wtmp[2], wtmp[1], act_alpha2, ALU.mult))
            chained(dve.tensor_scalar(mem.f_out, wtmp[2], 1.0 / (ACT_STEPS * S64), None, ALU.mult))

            def m_rows(k, b, r, n, diag, accum):
                if accum:
                    dve.scalar_tensor_tensor(r[:, 0, :], r[:, 0, :], 1.0, r[:, 1, :], ALU.mult, ALU.add,
                                             accum_out=sum_m[:, ds(k, 1)]).then_inc(S("sum_m"), 1)
                else:
                    dve.tensor_tensor(r[:, 0, :], r[:, 0, :], r[:, 1, :], ALU.add).then_inc(S("sum_m"), 1)
                dve.wait_ge(S("sum_m"), n)
                if diag is not None:
                    d = r[:, 0, ds(diag * P, P)]
                    dve.scalar_tensor_tensor(d, ident[:], 2.0, d, ALU.mult, ALU.add).then_inc(S("m_sum"), 1)
                else:
                    dve.sem_inc(S("m_sum"), 1)

            def m_low(k, b, r, n):
                dve.wait_ge(S("m_high"), n)
                dve.wait_ge(S("m_sum"), n)
                dve.scalar_tensor_tensor(mpair[b][:, 1, :], r[:, 0, :], S64, mpair[b][:, 0, :],
                                         ALU.mult, ALU.subtract).then_inc(S("m_low"), 1)

            def z_low(k, b, n):
                dve.wait_ge(S("z_high"), n)
                dve.scalar_tensor_tensor(zpair[b][:, 1, :], xbuf[b], dz[:, ds(k, 1)], zpair[b][:, 0, :],
                                         ALU.mult, ALU.subtract).then_inc(S("z_low"), 1)

            def first(k, b, diag):
                dve.wait_ge(S(f"rows_in{b}"), (k - b) * 32 + 64)
                m_rows(k, b, rows0[b], k + 1, diag, True)
                dve.wait_ge(S("t_high"), k * 2 + 2)
                for half, r in ((0, rows0[b]), (1, rows[b])):
                    dve.scalar_tensor_tensor(regions(1, half, k), blocks(r[:, 1, :]), S64, regions(0, half, k),
                                             ALU.mult, ALU.subtract).then_inc(S("t_low"), 1)
                dve.wait_ge(S("sums_at"), k + 1)
                m_low(k, b, rows0[b], k + 1)
                dve.wait_ge(S("m_low"), k + 1)
                dve.sem_inc(S("rows_free"), 1)
                z_low(k, b, k + 1)
                dve.wait_ge(S("z_low"), k + 1)
                dve.sem_inc(S("x_free"), 1)

            dve.wait_ge(S("setup"), 5)
            with pairs(dve, 0, HT) as k:
                for b in range(2):
                    first(k + b, b, k + b)
            with pairs(dve, HT, T) as k:
                for b in range(2):
                    first(k + b, b, None)

            def u_low(half):
                for j in range(HT):
                    i = HT * half + j
                    dve.wait_ge(S("u_high"), i + 1)
                    dve.scalar_tensor_tensor(u[:, 1, i, :], psum[:, j, :], dm[:, i:i + 1], u[:, 0, i, :],
                                             ALU.mult, ALU.subtract).then_inc(S("u_low"), 1)
            u_low(0)

            def second(k, b, diag):
                dve.wait_ge(S(f"rows2_in{b}"), (k - b) * 16 + 32)
                m_rows(k, b, rows[b], k + T + 1, diag, False)
                m_low(k, b, rows[b], k + T + 1)
                dve.wait_ge(S("m_low"), k + T + 1)
                dve.sem_inc(S("rows_free"), 1)
                z_low(k, b, k + T + 1)
                dve.wait_ge(S("z_low"), k + T + 1)
                dve.sem_inc(S("x_free"), 1)

            with pairs(dve, 0, HT) as k:
                for b in range(2):
                    second(k + b, b, None)
            with pairs(dve, HT, T) as k:
                for b in range(2):
                    second(k + b, b, k + b - HT)
            u_low(1)

            def normed(m, b):
                n = m + 1
                dve.wait_ge(S("au_done"), n)
                dve.wait_ge(S(f"x_in{b}"), (m - b) * 8 + 16 * T + 16)
                dve.scalar_tensor_tensor(hbuf, psum[:, b, :], 1.0 / (S64 * S64), xbuf[b], ALU.mult,
                                         ALU.add).then_inc(S("h1"), 1)
                dve.wait_ge(S("h1"), n)
                dve.sem_inc(S("x_free"), 1)
                dve.sem_inc(S("au_free"), 1)
                dve.bn_stats(stats, hbuf).then_inc(S("stats1"), 1)
                wait_apart(dve, S("stats1"), n, S("waited_dve"))
                dve.bn_aggr(mv, stats).then_inc(S("aggr1"), 1)
                for h in range(2):
                    dve.tensor_scalar(psum[:, 6:8, :].rearrange("p a b -> p (a b)"),
                                      big[:, ds(m, 1), HALF * h:HALF * (h + 1)].rearrange("p a b -> p (a b)"),
                                      S64, 0.0, ALU.is_equal, ALU.add,
                                      accum_out=ones_seen[:, ds(m + h * T, 1)]).then_inc(S("ones"), 1)
                    dve.wait_ge(S("ones"), m * 3 + (1 + h))
                dve.scalar_tensor_tensor(psum[:, 6, 0:P], big[:, ds(m, 1), ds(m * P, P)].rearrange("p a b -> p (a b)"),
                                         S64, ident[:], ALU.is_equal, ALU.mult,
                                         accum_out=ones_diag[:, ds(m, 1)]).then_inc(S("ones"), 1)
                dve.wait_ge(S("ones"), n * 3)
                dve.wait_ge(S("rstd1"), n)
                dve.wait_ge(S(f"x1_kept{b}"), (m - b) * 8 + 16)
                dve.tensor_scalar(x1buf[b], hbuf, mv[:, 0:1], rs1, ALU.subtract, ALU.mult).then_inc(S("x1_made"), 1)
                dve.wait_ge(S("x1_made"), n)
                dve.bn_stats(stats, x1buf[b]).then_inc(S("stats2"), 1)
                wait_apart(dve, S("stats2"), n, S("waited_dve"))
                dve.bn_aggr(mv2, stats).then_inc(S("aggr2"), 1)

            def quantised(m, b):
                n = m + 1
                dve.wait_ge(S("rstd2"), n)
                dve.wait_ge(S(f"x2_kept{b}"), (m - b) * 8 + 16)
                dve.tensor_scalar(x2buf[b], x1buf[b], mv2[:, 0:1], rs2, ALU.subtract, ALU.mult).then_inc(S("x2_made"), 1)
                dve.wait_ge(S("x2_made"), n)
                dve.tensor_scalar(qbuf, x2buf[b], r_act, 1.0, ALU.mult, ALU.min).then_inc(S("q_a"), 1)
                dve.wait_ge(S("q_a"), n)
                dve.tensor_scalar(qbuf, qbuf, ACT_STEPS, MAGIC, ALU.mult, ALU.add).then_inc(S("q_b"), 1)
                dve.wait_ge(S("q_b"), n)
                dve.wait_ge(S("q_free"), n)
                dve.tensor_scalar(qpair[b][:, 0, :], qbuf, MAGIC, None, ALU.subtract).then_inc(S("q_c"), 1)
                dve.wait_ge(S("q_c"), n)
                dve.scalar_tensor_tensor(qpair[b][:, 1, :], qbuf, MAGIC, qpair[b][:, 0, :], ALU.subtract,
                                         ALU.subtract).then_inc(S("q_made"), 1)

            def support(m, b):
                n = m + 1
                dve.wait_ge(S("sup_psum"), n)
                dve.tensor_scalar(sbuf2, psum[:, 4 + b, :], c_sup, 0.0, ALU.mult, ALU.max).then_inc(S("s_a"), 1)
                dve.wait_ge(S("s_a"), n)
                dve.sem_inc(S("sup_free"), 1)
                dve.tensor_scalar(sbuf2, sbuf2, 1.0, ACT_STEPS, ALU.min, ALU.mult).then_inc(S("s_b"), 1)
                dve.wait_ge(S("s_b"), n)
                dve.tensor_scalar(sup[:, ds(m, 1), :].rearrange("p a b -> p (a b)"), sbuf2, MAGIC, MAGIC, ALU.add,
                                  ALU.subtract).then_inc(S("sup_made"), 1)
                dve.wait_ge(S("sup_made"), n)

            normed(0, 0)
            quantised(0, 0)
            with pairs(dve, 1, T - 1) as m:
                for j in range(2):
                    normed(m + j, 1 - j)
                    support(m + j - 1, j)
                    quantised(m + j, 1 - j)
            normed(T - 1, 1)
            support(T - 2, 0)
            quantised(T - 1, 1)
            support(T - 1, 1)
            dve.reduce_sum(ones_tmp[:, 0:1], ones_seen, axis=AX.X).then_inc(S("ones_sums"), 1)
            dve.reduce_sum(ones_tmp[:, 1:2], ones_diag, axis=AX.X).then_inc(S("ones_sums"), 1)
            dve.wait_ge(S("ones_sums"), 2)
            dve.tensor_tensor(ones_tmp[:, 2:3], ones_tmp[:, 0:1], ones_tmp[:, 1:2], ALU.subtract)\
                .then_inc(S("ones_row"), 1)
            dve.wait_ge(S("ones_all"), 1)
            dve.tensor_scalar(flag[0:1, 0:1], psum[0:1, 7, 0:1], float(P), None, ALU.mult).then_inc(S("flag"), 1)
            dve.wait_ge(S("flag"), 1)

        @block.tensor
        def _(pe):
            pe.wait_ge(S("setup"), 5)
            pe.wait_ge(S("w_part_mean"), 1)
            pe.matmul(psum[:, 7, 0:1], mem.mean_matrix[:], wmv[:, 0:1], start=True, stop=True).then_inc(S("w_mean"), 1)
            pe.wait_ge(S("w_part_var"), 1)
            pe.matmul(psum[:, 7, 1:2], mem.mean_matrix[:], wtmp[3], start=True, stop=True).then_inc(S("w_pvar"), 1)
            pe.wait_ge(S("w_var"), 1)

            def sweep(half):
                def body(k, b, start=False, stop=False):
                    n = k + (T * half + 1)
                    pe.wait_ge(S("m_low"), n)
                    pe.wait_ge(S("z_low"), n)
                    for j in range(HT):
                        if start and half:
                            pe.wait_ge(S("u_low"), j + 1)
                        high, low = (mpair[b][:, h, j * P:(j + 1) * P] for h in range(2))
                        pe.matmul(psum[:, j, :], high, zpair[b][:, 0, :], start=start, stop=False)
                        pe.matmul(psum[:, j, :], high, zpair[b][:, 1, :], start=False, stop=False)
                        last = pe.matmul(psum[:, j, :], low, zpair[b][:, 0, :], start=False, stop=stop)
                    last.then_inc(S("m_free"), 1)
                    pe.wait_ge(S("m_free"), n + 2)
                    last = pe.sem_inc(S("z_free"), 1)

                body(0, 0, start=True)
                body(1, 1)
                with pairs(pe, 2, T - 2) as k:
                    for b in range(2):
                        body(k + b, b)
                body(T - 2, 0)
                body(T - 1, 1, stop=True)
                pe.sem_inc(S("sweep_done"), 1)
            sweep(0)
            sweep(1)

            def transposes(m, b):
                pe.wait_ge(S("q_made"), m + 1)
                for h in range(2):
                    for k in range(K4):
                        last = pe.transpose(mem.bank16(2 + b)[:, h * K4 + k, :], qpair[b][:, h, k * P:(k + 1) * P],
                                            ident[:])
                last.then_inc(S("qT_psum"), 1)
                pe.wait_ge(S("qT_psum"), m + 1)
                pe.sem_inc(S("q_free"), 1)

            def au(m, b, prev, first=False):
                pe.wait_ge(S("au_free"), m + 1)
                for k in range(T):
                    if first:
                        pe.wait_ge(S("u_low"), k + 1 if k >= b + 1 else HT + b + 1)
                    if k == T // 2 and prev:
                        transposes(m - 1, 1 - b)
                    high, low = (big[:, ds(m, 1), (h * T + k) * P:(h * T + k + 1) * P].rearrange("p a b -> p (a b)")
                                 for h in range(2))
                    pe.matmul(psum[:, b, :], high, u[:, 0, k, :], start=(k == 0), stop=False, skip_group_check=True)
                    pe.matmul(psum[:, b, :], high, u[:, 1, k, :], start=False, stop=False, skip_group_check=True)
                    last = pe.matmul(psum[:, b, :], low, u[:, 0, k, :], start=False, stop=(k == T - 1),
                                     skip_group_check=True)
                last.then_inc(S("au_done"), 1)

            def support(m, b):
                pe.wait_ge(S("qT_made"), m + 1)
                pe.wait_ge(S("sup_free"), m + 1)
                for h in range(2):
                    for k in range(K4):
                        last = pe.matmul(psum[:, 4 + b, :], qT[b][:, h * K4 + k, :], wq8[:, k, :],
                                         start=(h == 0 and k == 0), stop=(h == 1 and k == K4 - 1))
                last.then_inc(S("sup_psum"), 1)
                pe.wait_ge(S("sup_psum"), m + 1)
                pe.sem_inc(S("qT_free"), 1)

            pe.wait_ge(S("u_low"), HT + 6)
            pe.wait_ge(S("wq8"), 1)
            au(0, 0, False, first=True)
            with pairs(pe, 1, T - 1) as m:
                for j in range(2):
                    au(m + j, 1 - j, True)
                    support(m + j - 1, j)
            au(T - 1, 1, True)
            support(T - 2, 0)
            transposes(T - 1, 1)
            support(T - 1, 1)
            pe.wait_ge(S("ones_row"), 1)
            pe.matmul(psum[0:1, 7, 0:1], ones_tmp[:, 2:3], mem.mean_matrix[:, 0:1], start=True,
                      stop=True).then_inc(S("ones_all"), 1)
    return r_act, c_sup


def relation_attention(nc, mem, a, x1_dram, x2_dram, r_act, c_sup):
    big, psum, ident, S, carve = mem.big, mem.psum, mem.ident, mem.sem, mem.carve
    floats = big[:].rearrange("p a b -> p (a b)").bitcast(FP32)

    def room(at, dims):
        v = floats[:, at:at + int(np.prod(dims))]
        return v.rearrange("p (a b) -> p a b", a=dims[0]) if len(dims) > 1 else v

    x1 = room(0, [T, D])
    x1T = room(T * D, [K4, N])
    related, masked, score, shares = (room(T * D + N * i, [N]) for i in range(4))
    q, k_ = room(2 * T * D, [K4, N]), room(3 * T * D, [K4, N])
    w = [carve(8192 * i, [K4, D], FP32) for i in range(2)]
    iota = carve(0, [N], FP32)
    edge_one, node_one = carve(8192, [N], FP16), carve(12288, [P], FP16)
    q_tile = carve(12544, [K4, P], FP32)
    sharesT = carve(14592, [T, P], FP32)
    edges, edges_f = carve(22784, [2 * ET], FP32).bitcast(INT32), carve(24064, [2 * ET], FP32)
    ident_f, not_ident = carve(25344, [P], FP32), carve(25856, [P], FP32)
    biases = carve(26368, [2 * K4], FP32)
    hbuf, qbuf = carve(49152, [D], FP32), carve(51200, [D], FP32)
    qpair, qT, sbuf = carve(53248, [2, D], FP16), carve(55296, [2 * K4, P], FP16), carve(57344, [D], FP32)
    x2buf = carve(59392, [D], FP32)
    sup = carve(32768, [T, D], FP16)
    wq8 = carve(65536, [K4, D], FP16)
    rows = carve(0, [N], FP32)
    top, total, inv, stats, mv, ve, rstd = (mem.relation_cols[:, i:j] for i, j in
                                            ((0, 1), (1, 2), (2, 3), (3, 9), (9, 11), (11, 12), (12, 13)))

    EDGE, MASKS, HEAD, AFTER = 2, 2 + 3 * ET, 8 + 3 * ET, 8 + 3 * ET + 9 * HEADS
    TILE = AFTER + 20
    START = 9
    END = START + T * TILE

    def at(i, step):
        return i * TILE + (START + step)

    with nc.Block() as block:
        @block.sync
        def _(sp):
            loads = [(x1, x1_dram.rearrange("(t p) d -> p t d", p=P)),
                     (w[0], a["L1_wqT"].rearrange("(k p) d -> p k d", p=P)),
                     (w[1], a["L1_wkT"].rearrange("(k p) d -> p k d", p=P)),
                     (biases[:, 0:K4], a["L1_bq"]), (biases[:, K4:2 * K4], a["L1_bk"]), (edges, a["edges"])]
            for dst, src in loads:
                sp.dma_start(dst, src).then_inc(S("relation_in"), 16)
            sp.wait_ge(S("relation_in"), 16 * len(loads))
            sp.sem_inc(S("turn"), 1)
            sp.wait_ge(S("turn"), 8)
            sp.dma_start(iota, a["iota"]).then_inc(S("relation_in"), 16)
            sp.wait_ge(S("relation_in"), 16 * len(loads) + 16)
            sp.sem_inc(S("turn"), 1)
            with sp.Fori(0, T) as i:
                r = ds(i * P, P)
                sp.wait_ge(S("turn"), at(i, 0))
                sp.dma_start(masked, a["adj"][r, :]).then_inc(S("relation_adj"), 16)
                sp.wait_ge(S("relation_adj"), i * 16 + 16)
                sp.sem_inc(S("turn"), 1)
                sp.wait_ge(S("turn"), at(i, AFTER + 9))
                sp.dma_start(x2_dram[r, :], x2buf).then_inc(S("relation_x2"), 16)
                sp.wait_ge(S("relation_x2"), i * 16 + 16)
                sp.sem_inc(S("turn"), 1)
            with sp.Fori(0, T) as k:
                sp.wait_ge(S("turn"), k * 3 + END)
                sp.dma_start(rows, a["adjT"][ds(k * P, P), :]).then_inc(S("relation_rows"), 16)
                sp.wait_ge(S("relation_rows"), k * 16 + 16)
                sp.sem_inc(S("turn"), 1)

        @block.gpsimd
        def _(pool):
            with pool.Fori(0, T) as i:
                wait_apart(pool, S("turn"), at(i, AFTER + 6), S("waited_pool"))
                pool.tensor_scalar(ve, mv[:, 1:2], EPS, None, ALU.add).then_inc(S("turn"), 1)
                pool.wait_ge(S("turn"), at(i, AFTER + 7))
                pool.tensor_tensor(rstd, ve, mem.minus_half, ALU.pow).then_inc(S("turn"), 1)

        @block.scalar
        def _(act):
            act.wait_ge(S("turn"), 5)
            for k in range(K4):
                for b in range(2):
                    act.wait_ge(S("relation_x1T"), 2 * k + b + 1)
                    last = act.activation(x1T[:, k, HALF * b:HALF * (b + 1)],
                                          psum[:, 2 * b:2 * b + 2, :].rearrange("p a b -> p (a b)"), ACT.Copy)
                    last.then_inc(S("relation_x1T_out"), 1)
            act.wait_ge(S("relation_x1T_out"), 2 * K4)
            act.sem_inc(S("turn"), 1)
            with act.Fori(0, T) as i:
                for h in range(HEADS):
                    act.wait_ge(S("turn"), at(i, HEAD + 9 * h + 5))
                    act.activation(score, score, ACT.Exp, bias=top, accum_out=total).then_inc(S("turn"), 1)
                act.wait_ge(S("turn"), at(i, AFTER + 1))
                act.activation(sharesT.rearrange("p a b -> p (a b)"),
                               psum[:, 4:8, :].rearrange("p a b -> p (a b)"), ACT.Copy).then_inc(S("turn"), 1)
                act.wait_ge(S("turn"), at(i, AFTER + 15))
                act.activation(qT, mem.bank16(2), ACT.Copy).then_inc(S("turn"), 1)
            with act.Fori(0, T) as k:
                act.wait_ge(S("turn"), k * 3 + (END + 1))
                act.activation(big[:, :, ds(k * P, P)], rows.rearrange("p (a b) -> p a b", b=P), ACT.Copy,
                               scale=S64).then_inc(S("turn"), 1)

        @block.vector
        def _(dve):
            dve.wait_ge(S("turn"), 1)
            dve.tensor_copy(edges_f, edges).then_inc(S("turn"), 1)
            dve.tensor_copy(ident_f, ident[:]).then_inc(S("turn"), 1)
            dve.wait_ge(S("turn"), 3)
            dve.tensor_scalar(not_ident, ident_f, -1.0, 1.0, ALU.mult, ALU.add).then_inc(S("turn"), 1)
            dve.wait_ge(S("turn"), 4)
            dve.sem_inc(S("turn"), 1)
            for n in range(2 * K4 * 4):
                side, d, c = n // (K4 * 4), n // 4 % K4, n % 4
                dve.wait_ge(S("relation_qk"), n + 1)
                dve.tensor_scalar((q, k_)[side][:, d, c * 512:(c + 1) * 512], psum[:, 4 + n % 4, :],
                                  biases[:, side * K4 + d:side * K4 + d + 1], None, ALU.add)\
                    .then_inc(S("relation_qk_out"), 1)
            dve.wait_ge(S("relation_qk_out"), 8 * K4)
            dve.sem_inc(S("turn"), 1)
            dve.sem_inc(S("turn"), 1)
            with dve.Fori(0, T) as i:
                diag = ds(i * P, P)
                dve.wait_ge(S("turn"), at(i, 1))
                dve.tensor_copy(q_tile, q[:, :, diag]).then_inc(S("turn"), 1)
                with dve.Fori(0, ET) as e:
                    dve.wait_ge(S("turn"), i * TILE + e * 3 + (START + EDGE))
                    dve.tensor_scalar(node_one, iota[:, diag], edges_f[:, ds(e, 1)], None, ALU.is_equal)\
                        .then_inc(S("turn"), 1)
                    dve.tensor_scalar(edge_one, iota, edges_f[:, ds(e + ET, 1)], None, ALU.is_equal)\
                        .then_inc(S("turn"), 1)
                dve.wait_ge(S("turn"), at(i, MASKS))
                dve.tensor_scalar(related, psum[:, 0:4, :].rearrange("p a b -> p (a b)"), 1.0, float(DK) ** -0.5,
                                  ALU.min, ALU.mult).then_inc(S("turn"), 1)
                dve.wait_ge(S("turn"), at(i, MASKS + 1))
                dve.tensor_tensor(related[:, diag], related[:, diag], not_ident, ALU.mult).then_inc(S("turn"), 1)
                dve.tensor_scalar(masked, masked, 1.0, 3.0e38, ALU.is_equal, ALU.mult).then_inc(S("turn"), 1)
                dve.wait_ge(S("turn"), at(i, MASKS + 3))
                dve.tensor_scalar(masked, masked, 3.0e38, None, ALU.subtract).then_inc(S("turn"), 1)
                dve.wait_ge(S("turn"), at(i, MASKS + 4))
                dve.tensor_tensor(masked[:, diag], masked[:, diag], not_ident, ALU.mult).then_inc(S("turn"), 1)
                dve.wait_ge(S("turn"), at(i, MASKS + 5))
                dve.scalar_tensor_tensor(masked[:, diag], ident_f, 1e-7, masked[:, diag], ALU.mult, ALU.add)\
                    .then_inc(S("turn"), 1)
                for h in range(HEADS):
                    first = HEAD + 9 * h
                    dve.wait_ge(S("turn"), at(i, first + 1))
                    dve.tensor_tensor(score, psum[:, 0:4, :].rearrange("p a b -> p (a b)"), related, ALU.mult)\
                        .then_inc(S("turn"), 1)
                    dve.wait_ge(S("turn"), at(i, first + 2))
                    dve.tensor_tensor(score, score, masked, ALU.add).then_inc(S("turn"), 1)
                    dve.wait_ge(S("turn"), at(i, first + 3))
                    dve.tensor_reduce(inv, score, axis=AX.X, op=ALU.max).then_inc(S("turn"), 1)
                    dve.wait_ge(S("turn"), at(i, first + 4))
                    dve.tensor_scalar(top, inv, -1.0, None, ALU.mult).then_inc(S("turn"), 1)
                    dve.wait_ge(S("turn"), at(i, first + 6))
                    dve.reciprocal(inv, total).then_inc(S("turn"), 1)
                    dve.wait_ge(S("turn"), at(i, first + 7))
                    dve.tensor_scalar(ve, inv, 1.0 / HEADS, None, ALU.mult).then_inc(S("turn"), 1)
                    dve.wait_ge(S("turn"), at(i, first + 8))
                    if h == 0:
                        dve.tensor_scalar(shares, score, ve, None, ALU.mult).then_inc(S("turn"), 1)
                    else:
                        dve.scalar_tensor_tensor(shares, score, ve, shares, ALU.mult, ALU.add).then_inc(S("turn"), 1)
                dve.wait_ge(S("turn"), at(i, AFTER + 3))
                dve.tensor_tensor(hbuf, psum[:, 0, :], x1[:, ds(i, 1), :].rearrange("p a b -> p (a b)"), ALU.add)\
                    .then_inc(S("turn"), 1)
                dve.wait_ge(S("turn"), at(i, AFTER + 4))
                dve.bn_stats(stats, hbuf).then_inc(S("turn"), 1)
                wait_apart(dve, S("turn"), at(i, AFTER + 5), S("waited_dve"))
                dve.bn_aggr(mv, stats).then_inc(S("turn"), 1)
                dve.wait_ge(S("turn"), at(i, AFTER + 8))
                dve.tensor_scalar(x2buf, hbuf, mv[:, 0:1], rstd, ALU.subtract, ALU.mult).then_inc(S("turn"), 1)
                dve.wait_ge(S("turn"), at(i, AFTER + 10))
                dve.tensor_scalar(qbuf, x2buf, r_act, 1.0, ALU.mult, ALU.min).then_inc(S("turn"), 1)
                dve.wait_ge(S("turn"), at(i, AFTER + 11))
                dve.tensor_scalar(qbuf, qbuf, ACT_STEPS, MAGIC, ALU.mult, ALU.add).then_inc(S("turn"), 1)
                dve.wait_ge(S("turn"), at(i, AFTER + 12))
                dve.tensor_scalar(qpair[:, 0, :], qbuf, MAGIC, None, ALU.subtract).then_inc(S("turn"), 1)
                dve.wait_ge(S("turn"), at(i, AFTER + 13))
                dve.scalar_tensor_tensor(qpair[:, 1, :], qbuf, MAGIC, qpair[:, 0, :], ALU.subtract, ALU.subtract)\
                    .then_inc(S("turn"), 1)
                dve.wait_ge(S("turn"), at(i, AFTER + 17))
                dve.tensor_scalar(sbuf, psum[:, 4, :], c_sup, 0.0, ALU.mult, ALU.max).then_inc(S("turn"), 1)
                dve.wait_ge(S("turn"), at(i, AFTER + 18))
                dve.tensor_scalar(sbuf, sbuf, 1.0, ACT_STEPS, ALU.min, ALU.mult).then_inc(S("turn"), 1)
                dve.wait_ge(S("turn"), at(i, AFTER + 19))
                dve.tensor_scalar(sup[:, ds(i, 1), :].rearrange("p a b -> p (a b)"), sbuf, MAGIC, MAGIC, ALU.add,
                                  ALU.subtract).then_inc(S("turn"), 1)
            with dve.Fori(0, T) as k:
                dve.wait_ge(S("turn"), k * 3 + (END + 2))
                dve.scalar_tensor_tensor(big[:, :, ds(k * P + N, P)], rows.rearrange("p (a b) -> p a b", b=P), S64,
                                         big[:, :, ds(k * P, P)], ALU.mult, ALU.subtract).then_inc(S("turn"), 1)

        @block.tensor
        def _(pe):
            pe.wait_ge(S("turn"), 5)
            for k in range(K4):
                for b in range(2):
                    if k:
                        pe.wait_ge(S("relation_x1T_out"), 2 * (k - 1) + b + 1)
                    for t in range(HT):
                        last = pe.transpose(psum[:, 2 * b + t // 4, t % 4 * P:(t % 4 + 1) * P],
                                            x1[:, HT * b + t, k * P:(k + 1) * P], ident_f)
                    last.then_inc(S("relation_x1T"), 1)
            pe.wait_ge(S("turn"), 6)
            for n in range(2 * K4 * 4):
                side, d, c = n // (K4 * 4), n // 4 % K4, n % 4
                if n >= 4:
                    pe.wait_ge(S("relation_qk_out"), n - 3)
                for k in range(K4):
                    last = pe.matmul(psum[:, 4 + n % 4, :], w[side][:, k, d * P:(d + 1) * P],
                                     x1T[:, k, c * 512:(c + 1) * 512], start=(k == 0), stop=(k == K4 - 1))
                last.then_inc(S("relation_qk"), 1)
            with pe.Fori(0, T) as i:
                def count(e, start=False, stop=False):
                    pe.wait_ge(S("turn"), i * TILE + e * 3 + (START + EDGE + 2))
                    for c in range(4):
                        last = pe.matmul(psum[:, c, :], node_one, edge_one[:, c * 512:(c + 1) * 512],
                                         start=start, stop=stop)
                    last.then_inc(S("turn"), 1)
                count(0, start=True)
                with pe.Fori(1, ET - 1) as e:
                    count(e)
                count(ET - 1, stop=True)
                for h in range(HEADS):
                    pe.wait_ge(S("turn"), at(i, HEAD + 9 * h))
                    r = slice(DK * (h % 2), DK * (h % 2) + DK)
                    for c in range(4):
                        last = pe.matmul(psum[:, c, :], q_tile[r, h // 2, :], k_[r, h // 2, c * 512:(c + 1) * 512],
                                         start=True, stop=True)
                    last.then_inc(S("turn"), 1)
                pe.wait_ge(S("turn"), at(i, AFTER))
                for t in range(T):
                    last = pe.transpose(psum[:, 4 + t // 4, t % 4 * P:(t % 4 + 1) * P], shares[:, t * P:(t + 1) * P],
                                        ident_f)
                last.then_inc(S("turn"), 1)
                pe.wait_ge(S("turn"), at(i, AFTER + 2))
                for t in range(T):
                    last = pe.matmul(psum[:, 0, :], sharesT[:, t, :], x1[:, t, :], start=(t == 0), stop=(t == T - 1))
                last.then_inc(S("turn"), 1)
                pe.wait_ge(S("turn"), at(i, AFTER + 14))
                for h in range(2):
                    for k in range(K4):
                        last = pe.transpose(mem.bank16(2)[:, h * K4 + k, :], qpair[:, h, k * P:(k + 1) * P], ident[:])
                last.then_inc(S("turn"), 1)
                pe.wait_ge(S("turn"), at(i, AFTER + 16))
                for h in range(2):
                    for k in range(K4):
                        last = pe.matmul(psum[:, 4, :], qT[:, h * K4 + k, :], wq8[:, k, :],
                                         start=(h == 0 and k == 0), stop=(h == 1 and k == K4 - 1))
                last.then_inc(S("turn"), 1)


def attention(nc, mem, a, x2_dram, out):
    big, psum, ident, S, carve = mem.big, mem.psum, mem.ident, mem.sem, mem.carve
    x3 = carve(0, [T, D], FP32)
    sup = carve(32768, [T, D], FP16)
    wq, wk, wvt = (carve(8192 * i, [K4, D], FP32) for i in range(3))
    g = carve(49152, [2, K4, D], FP16)
    wv = carve(57344, [2, K4, D], FP16)
    x2in = [carve(65536 + 2048 * b, [D], FP32) for b in range(2)]
    hbuf = carve(69632, [D], FP32)
    x3pair = carve(71680, [2, D], FP16)
    tmp = [carve(73728 + 2048 * b, [D], FP32) for b in range(2)]
    bv = carve(77824, [D], FP32)
    rows = [carve(32768 + 8192 * b, [N], FP32) for b in range(2)]
    mask = carve(49152, [N], FP16)
    ppair = [carve(53248 + 8192 * b, [2, N], FP16) for b in range(2)]
    attended = [carve(69632 + 2048 * b, [D], FP32) for b in range(2)]

    mem.at = 15
    col = mem.col
    bq, bk = col(K4), col(K4)
    gk, wc, wc_pair, c0, tmpc = col(K4), col(K4), col(K4), col(), col(K4)
    wc_high, wc_low = wc_pair[:, 0:2].bitcast(FP16), wc_pair[:, 2:4].bitcast(FP16)
    ci = col(T)
    stats, mv, ve, rstd = col(6), col(2), col(), col()
    top, bias, total, inv = col(2), col(2), col(2), col(2)

    def xT(tiles, part, k):
        return big[:, tiles, (part * K4 + k) * P:(part * K4 + k + 1) * P]

    def tT(tiles, part, k):
        return big[:, tiles, 1024 + (part * K4 + k) * P:1024 + (part * K4 + k + 1) * P]

    def value(tile, part):
        return big[:, tile, 2048 + part * D:2048 + (part + 1) * D].rearrange("p a b -> p (a b)")

    def pT(b, part, tiles):
        return big[:, tiles, 3072 + (2 * b + part) * P:3072 + (2 * b + part + 1) * P]

    with nc.Block() as block:
        @block.sync
        def _(sp):
            for v, n in ((wq, "W_q"), (wk, "W_k"), (wvt, "W_vT")):
                sp.dma_start(v, a[n].rearrange("(k p) d -> p k d", p=P)).then_inc(S("weights_in"), 16)
            sp.dma_start(bq, a["b_q"]).then_inc(S("weights_in"), 16)
            sp.dma_start(bk, a["b_k"]).then_inc(S("weights_in"), 16)
            sp.dma_start(bv, a["b_v"].to_broadcast([P, D])).then_inc(S("weights_in"), 16)
            with pairs(sp, 0, T) as m:
                for b in range(2):
                    sp.wait_ge(S("x2_free"), m + b + 1)
                    sp.dma_start(x2in[b], x2_dram[ds((m + b) * P, P), :]).then_inc(S(f"x2_in{b}"), 16)
            sp.wait_ge(S("t_made"), 4 * K4)
            with pairs(sp, 0, T) as i:
                for b in range(2):
                    sp.wait_ge(S("adj_free"), i + b + 1)
                    sp.dma_start(rows[b], a["adj"][ds((i + b) * P, P), :]).then_inc(S(f"adj_in{b}"), 16)
            with sp.Fori(0, T) as i:
                sp.wait_ge(S("out_made"), i + 1)
                sp.dma_start(out[ds(i * P, P), :], x3[:, ds(i, 1), :].rearrange("p a b -> p (a b)"))\
                    .then_inc(S("stored"), 16)
            sp.wait_ge(S("stored"), 16 * T)

        @block.gpsimd
        def _(pool):
            def inverse_deviation(n, made, ve_sem, rstd_sem):
                wait_apart(pool, S(made), n, S("waited_pool"))
                pool.tensor_scalar(ve, mv[:, 1:2], EPS, None, ALU.add).then_inc(S(ve_sem), 1)
                pool.wait_ge(S(ve_sem), n)
                pool.tensor_tensor(rstd, ve, mem.minus_half, ALU.pow).then_inc(S(rstd_sem), 1)

            with pool.Fori(0, T) as m:
                inverse_deviation(m + 1, "aggr3", "ve3", "rstd3")

            def masked(i, b):
                pool.wait_ge(S("scored"), i * 2 + 2)
                wait_apart(pool, S("mask_free"), i + 1, S("waited_pool"))
                pool.tensor_scalar(mask, rows[b], 0.0, ZS * MASKED, ALU.is_equal, ALU.mult).then_inc(S("mask"), 1)

            masked(0, 0)
            with pairs(pool, 1, T - 1) as i:
                for j in range(2):
                    masked(i + j, 1 - j)
                    inverse_deviation(i + j, "aggr4", "ve4", "rstd4")
            masked(T - 1, 1)
            inverse_deviation(T - 1, "aggr4", "ve4", "rstd4")
            inverse_deviation(T, "aggr4", "ve4", "rstd4")

        @block.scalar
        def _(act):
            for k in range(K4):
                act.wait_ge(S("g_psum"), k + 1)
                act.activation(g[:, 0, k, :], psum[:, k, :], ACT.Copy, scale=S64).then_inc(S("g_high"), 1)
            act.activation(wv[:, 0, :, :], wvt, ACT.Copy, scale=S64).then_inc(S("wv_high"), 1)

            def v_high(m, b):
                act.wait_ge(S("v_sum"), m + 1)
                act.activation(value(ds(m, 1), 0), tmp[0], ACT.Copy, scale=S64).then_inc(S("v_high"), 1)

            def x_side(m):
                act.wait_ge(S("x3_made"), m + 1)
                act.wait_ge(S("x3pair_free"), m + 1)
                act.activation(x3pair[:, 0, :], x3[:, ds(m, 1), :].rearrange("p a b -> p (a b)"),
                               ACT.Copy).then_inc(S("x3_high"), 1)

            def xT_out(m, b):
                act.wait_ge(S("xT_psum"), m + 1)
                act.activation(big[:, ds(m, 1), 0:1024].rearrange("p a (k c) -> p (a k) c", c=P),
                               mem.bank16(2), ACT.Copy).then_inc(S("xT_made"), 1)

            x_side(0)
            with act.Fori(1, T) as m:
                xT_out(m - 1, 0)
                x_side(m)
                v_high(m - 1, 0)
            xT_out(T - 1, 0)
            v_high(T - 1, 0)

            for c in range(4):
                for e in range(K4):
                    act.wait_ge(S("t_sum"), c * K4 + e + 1)
                    act.activation(tT(slice(4 * c, 4 * c + 4), 0, e),
                                   tmp[e % 2].rearrange("p (a b) -> p a b", b=P), ACT.Copy).then_inc(S("t_high4"), 1)

            def numerators(i, b):
                act.wait_ge(S("bias"), i + 1)
                act.activation(rows[b], rows[b], ACT.Exp, bias=bias[:, b:b + 1], scale=1.0 / ZS,
                               accum_out=total[:, b:b + 1]).then_inc(S("exp"), 1)
                act.wait_ge(S("exp"), i + 1)
                act.wait_ge(S("p_free"), i + 1)
                act.activation(ppair[b][:, 0, :], rows[b], ACT.Copy).then_inc(S("p_high"), 1)

            def evacuate(i, b):
                for q in range(2):
                    act.wait_ge(S("pT_h"), i * 2 + (q + 1))
                    if q == 0:
                        act.wait_ge(S("pT_free"), i + 1)
                    act.activation(pT(b, 0, slice(8 * q, 8 * q + 8)), mem.bank16(4 + q), ACT.Copy)\
                        .then_inc(S("pT_high"), 1)

            def weighted(i, b):
                act.wait_ge(S("pv"), i + 1)
                act.wait_ge(S("inv"), i + 1)
                act.activation(attended[b], psum[:, 7, :], ACT.Relu, scale=inv[:, b:b + 1]).then_inc(S("relu"), 1)

            numerators(0, 0)
            with pairs(act, 0, T - 2) as i:
                for b in range(2):
                    evacuate(i + b, b)
                    numerators(i + b + 1, 1 - b)
                    weighted(i + b, b)
            evacuate(T - 2, 0)
            numerators(T - 1, 1)
            weighted(T - 2, 0)
            evacuate(T - 1, 1)
            weighted(T - 1, 1)

        @block.vector
        def _(dve):
            dve.sem_inc(S("x2_free"), 2)
            dve.sem_inc(S("l3_free"), 2)
            dve.sem_inc(S("x3pair_free"), 1)
            dve.sem_inc(S("adj_free"), 2)
            dve.sem_inc(S("mask_free"), 1)
            dve.sem_inc(S("p_free"), 2)
            dve.sem_inc(S("pT_free"), 2)
            dve.wait_ge(S("weights_in"), 96)
            dve.wait_ge(S("small_psum"), 1)
            dve.tensor_scalar(gk, psum[:, 4, 0:K4], SCALE, None, ALU.mult).then_inc(S("gk"), 1)
            dve.tensor_scalar(wc, psum[:, 4, K4:2 * K4], S64, None, ALU.mult).then_inc(S("wc"), 1)
            dve.wait_ge(S("wc"), 1)
            dve.tensor_copy(wc_high, wc).then_inc(S("wc"), 1)
            dve.wait_ge(S("wc"), 2)
            dve.tensor_tensor(wc_low, wc, wc_high, ALU.subtract).then_inc(S("wc"), 1)
            dve.tensor_tensor(tmpc, bq, bk, ALU.mult).then_inc(S("bqk"), 1)
            dve.wait_ge(S("bqk"), 1)
            dve.reduce_sum(ve, tmpc, axis=AX.X).then_inc(S("bqk"), 1)
            dve.wait_ge(S("bqk_psum"), 1)
            dve.tensor_scalar(c0, psum[:, 5, 0:1], SCALE * P, None, ALU.mult).then_inc(S("c0"), 1)
            for k in range(K4):
                dve.wait_ge(S("g_high"), k + 1)
                dve.scalar_tensor_tensor(g[:, 1, k, :], psum[:, k, :], S64, g[:, 0, k, :], ALU.mult,
                                         ALU.subtract).then_inc(S("g_low"), 1)
            dve.wait_ge(S("wv_high"), 1)
            dve.scalar_tensor_tensor(wv[:, 1, :, :].rearrange("p a b -> p (a b)"), wvt.rearrange("p a b -> p (a b)"), S64,
                                     wv[:, 0, :, :].rearrange("p a b -> p (a b)"), ALU.mult, ALU.subtract)\
                .then_inc(S("wv_low"), 1)
            dve.wait_ge(S("wv_low"), 1)

            def convolved(m, b):
                n = m + 1
                xm = x3[:, ds(m, 1), :].rearrange("p a b -> p (a b)")
                dve.wait_ge(S("l3_psum"), n)
                dve.wait_ge(S(f"x2_in{b}"), (m - b) * 8 + 16)
                dve.scalar_tensor_tensor(hbuf, psum[:, b, :], mem.f_out, x2in[b], ALU.mult, ALU.add)\
                    .then_inc(S("h3"), 1)
                dve.wait_ge(S("h3"), n)
                dve.sem_inc(S("x2_free"), 1)
                dve.sem_inc(S("l3_free"), 1)
                dve.bn_stats(stats, hbuf).then_inc(S("stats3"), 1)
                wait_apart(dve, S("stats3"), n, S("waited_dve"))
                dve.bn_aggr(mv, stats).then_inc(S("aggr3"), 1)
                dve.wait_ge(S("rstd3"), n)
                dve.tensor_scalar(xm, hbuf, mv[:, 0:1], rstd, ALU.subtract, ALU.mult).then_inc(S("x3_made"), 1)
                dve.wait_ge(S("x3_high"), n)
                dve.tensor_tensor(x3pair[:, 1, :], xm, x3pair[:, 0, :], ALU.subtract).then_inc(S("x3_low"), 1)

            def valued(m):
                n = m + 1
                dve.wait_ge(S("v_psum"), n)
                dve.scalar_tensor_tensor(tmp[0], psum[:, 4, :], 1.0 / S64, bv, ALU.mult, ALU.add).then_inc(S("v_sum"), 1)
                dve.tensor_scalar(ci[:, ds(m, 1)], psum[:, 5, 0:1], SCALE / S64, c0, ALU.mult, ALU.add)\
                    .then_inc(S("ci"), 1)
                dve.wait_ge(S("v_high"), n)
                dve.scalar_tensor_tensor(value(ds(m, 1), 1), tmp[0], S64, value(ds(m, 1), 0), ALU.mult,
                                         ALU.subtract).then_inc(S("v_low"), 1)
                dve.wait_ge(S("v_low"), n)

            convolved(0, 0)
            with pairs(dve, 1, T - 1) as m:
                for j in range(2):
                    convolved(m + j, 1 - j)
                    valued(m + j - 1)
            convolved(T - 1, 1)
            valued(T - 2)
            valued(T - 1)

            for c in range(4):
                for e in range(K4):
                    n = c * K4 + e + 1
                    dve.wait_ge(S("t_psum"), n)
                    dve.tensor_scalar(tmp[e % 2], psum[:, e, :], SCALE / S64, gk[:, e:e + 1], ALU.mult, ALU.add)\
                        .then_inc(S("t_sum"), 1)
                    dve.wait_ge(S("t_high4"), n)
                    tiles = slice(4 * c, 4 * c + 4)
                    dve.tensor_tensor(tT(tiles, 1, e), tmp[e % 2].rearrange("p (a b) -> p a b", b=P),
                                      tT(tiles, 0, e), ALU.subtract).then_inc(S("t_made"), 1)

            def scored(i, b):
                dve.wait_ge(S(f"adj_in{b}"), (i - b) * 8 + 16)
                for h in range(2):
                    dve.wait_ge(S("z"), i * 2 + (h + 1))
                    part = rows[b][:, h * HALF:(h + 1) * HALF]
                    dve.scalar_tensor_tensor(part, psum[:, 2 * h:2 * h + 2, :].rearrange("p a b -> p (a b)"),
                                             ci[:, ds(i, 1)], part, ALU.add, ALU.mult).then_inc(S("scored"), 1)

            def maximum(i, b):
                wait_apart(dve, S("mask"), i + 1, S("waited_dve"))
                dve.tensor_tensor_reduce(out=rows[b], in0=rows[b], in1=mask, scale=1.0, scalar=-3.0e38,
                                         op0=ALU.add, op1=ALU.max, accum_out=top[:, b:b + 1]).then_inc(S("top"), 1)
                dve.wait_ge(S("top"), i + 1)
                dve.sem_inc(S("mask_free"), 1)
                dve.tensor_scalar(bias[:, b:b + 1], top[:, b:b + 1], -1.0 / ZS, float(np.log(PSCALE)), ALU.mult,
                                  ALU.add).then_inc(S("bias"), 1)

            def p_low(i, b):
                dve.wait_ge(S("p_high"), i + 1)
                dve.tensor_tensor(ppair[b][:, 1, :], rows[b], ppair[b][:, 0, :], ALU.subtract).then_inc(S("p_low"), 1)
                dve.reciprocal(top[:, b:b + 1], total[:, b:b + 1]).then_inc(S("recip"), 1)
                dve.wait_ge(S("recip"), i + 1)
                dve.tensor_scalar(inv[:, b:b + 1], top[:, b:b + 1], 1.0 / S64, None, ALU.mult).then_inc(S("inv"), 1)
                dve.wait_ge(S("p_low"), i + 1)
                dve.sem_inc(S("adj_free"), 1)

            def evacuate(i, b):
                for q in range(2):
                    dve.wait_ge(S("pT_l"), i * 2 + (q + 1))
                    if q == 0:
                        dve.wait_ge(S("pT_free"), i + 1)
                    dve.tensor_copy(pT(b, 1, slice(8 * q, 8 * q + 8)), mem.bank16(6 if q == 0 else 4))\
                        .then_inc(S("pT_low"), 1)

            def finished(i, b):
                n = i + 1
                xi = x3[:, ds(i, 1), :].rearrange("p a b -> p (a b)")
                dve.wait_ge(S("relu"), n)
                dve.tensor_tensor(attended[b], attended[b], xi, ALU.add).then_inc(S("h4"), 1)
                dve.wait_ge(S("h4"), n)
                dve.bn_stats(stats, attended[b]).then_inc(S("stats4"), 1)
                wait_apart(dve, S("stats4"), n, S("waited_dve"))
                dve.bn_aggr(mv, stats).then_inc(S("aggr4"), 1)
                dve.wait_ge(S("rstd4"), n)
                dve.tensor_scalar(xi, attended[b], mv[:, 0:1], rstd, ALU.subtract, ALU.mult).then_inc(S("out_made"), 1)

            scored(0, 0)
            maximum(0, 0)
            p_low(0, 0)
            with pairs(dve, 0, T - 2) as i:
                for b in range(2):
                    evacuate(i + b, b)
                    scored(i + b + 1, 1 - b)
                    maximum(i + b + 1, 1 - b)
                    p_low(i + b + 1, 1 - b)
                    finished(i + b, b)
            evacuate(T - 2, 0)
            scored(T - 1, 1)
            maximum(T - 1, 1)
            p_low(T - 1, 1)
            finished(T - 2, 0)
            evacuate(T - 1, 1)
            finished(T - 1, 1)

        @block.tensor
        def _(pe):
            pe.wait_ge(S("weights_in"), 96)
            for d in range(K4):
                for o in range(K4):
                    last = pe.matmul(psum[:, d, :], wq[:, o, d * P:(d + 1) * P], wk[:, o, :], start=(o == 0),
                                     stop=(o == K4 - 1))
                last.then_inc(S("g_psum"), 1)
            for i, (w, bias_col) in enumerate(((wk, bq), (wq, bk))):
                for d in range(K4):
                    for o in range(K4):
                        last = pe.matmul(psum[:, 4, i * K4 + d:i * K4 + d + 1], w[:, o, d * P:(d + 1) * P],
                                         bias_col[:, o:o + 1], start=(o == 0), stop=(o == K4 - 1))
            last.then_inc(S("small_psum"), 1)
            pe.wait_ge(S("bqk"), 2)
            pe.matmul(psum[:, 5, 0:1], mem.mean_matrix[:], ve, start=True, stop=True).then_inc(S("bqk_psum"), 1)
            pe.wait_ge(S("g_low"), K4)
            pe.wait_ge(S("c0"), 1)
            pe.wait_ge(S("wc"), 3)
            pe.wait_ge(S("wv_low"), 1)

            def convolve(m, b, prev):
                pe.wait_ge(S("l3_free"), m + 1)
                for k in range(T):
                    if k == T // 2 and prev:
                        transposes(m - 1)
                    for h in range(2):
                        w = big[:, ds(m, 1), (h * T + k) * P:(h * T + k + 1) * P].rearrange("p a b -> p (a b)")
                        last = pe.matmul(psum[:, b, :], w, sup[:, k, :], start=(k == 0 and h == 0),
                                         stop=(k == T - 1 and h == 1), skip_group_check=True)
                last.then_inc(S("l3_psum"), 1)

            def transposes(m):
                pe.wait_ge(S("x3_low"), m + 1)
                for h in range(2):
                    for k in range(K4):
                        last = pe.transpose(mem.bank16(2)[:, h * K4 + k, :], x3pair[:, h, k * P:(k + 1) * P], ident[:])
                last.then_inc(S("xT_psum"), 1)
                pe.wait_ge(S("xT_psum"), m + 1)
                pe.sem_inc(S("x3pair_free"), 1)

            def project(m):
                pe.wait_ge(S("xT_made"), m + 1)
                if not isinstance(m, int) or m > 0:
                    pe.wait_ge(S("v_low"), m)
                for part, other in ((0, 0), (0, 1), (1, 0)):
                    for k in range(K4):
                        w = xT(ds(m, 1), part, k).rearrange("p a b -> p (a b)")
                        first, end = (part, other, k) == (0, 0, 0), (part, k) == (1, K4 - 1)
                        pe.matmul(psum[:, 4, :], w, wv[:, other, k, :], start=first, stop=end)
                        last = pe.matmul(psum[:, 5, 0:1], w, (wc_high, wc_low)[other][:, k:k + 1],
                                         start=first, stop=end)
                last.then_inc(S("v_psum"), 1)

            convolve(0, 0, False)
            with pairs(pe, 1, T - 1) as m:
                for j in range(2):
                    convolve(m + j, 1 - j, True)
                    project(m + j - 1)
            convolve(T - 1, 1, True)
            project(T - 2)
            transposes(T - 1)
            project(T - 1)

            for c in range(4):
                for e in range(K4):
                    if c:
                        pe.wait_ge(S("t_sum"), (c - 1) * K4 + e + 1)
                    elif e < 2:
                        pe.wait_ge(S("h3"), T)
                    for part, other in ((0, 0), (0, 1), (1, 0)):
                        for k in range(K4):
                            last = pe.matmul(psum[:, e, :], g[:, part, k, e * P:(e + 1) * P],
                                             xT(slice(4 * c, 4 * c + 4), other, k),
                                             start=((part, other, k) == (0, 0, 0)), stop=((part, k) == (1, K4 - 1)))
                    last.then_inc(S("t_psum"), 1)

            def scores(i, first=False):
                for c in range(4):
                    if not first and c % 2 == 0:
                        pe.wait_ge(S("scored"), i * 2 - 1 + c // 2)
                    for part, other in ((0, 0), (0, 1), (1, 0)):
                        for k in range(K4):
                            last = pe.matmul(psum[:, c, :], tT(ds(i, 1), part, k).rearrange("p a b -> p (a b)"),
                                             xT(slice(4 * c, 4 * c + 4), other, k),
                                             start=((part, other, k) == (0, 0, 0)), stop=((part, k) == (1, K4 - 1)))
                    if c % 2:
                        last.then_inc(S("z"), 1)

            def weigh(i, b, first=False):
                def turn(part, q, bank, done):
                    for j in range(8):
                        last = pe.transpose(mem.bank16(bank)[:, j, :],
                                            ppair[b][:, part, (8 * q + j) * P:(8 * q + j + 1) * P], ident[:])
                    last.then_inc(S(done), 1)

                pe.wait_ge(S("p_high"), i + 1)
                turn(0, 0, 4, "pT_h")
                pe.wait_ge(S("p_low"), i + 1)
                turn(1, 0, 6, "pT_l")
                turn(0, 1, 5, "pT_h")
                pe.wait_ge(S("pT_high"), i * 2 + 1)
                turn(1, 1, 4, "pT_l")
                pe.wait_ge(S("pT_l"), i * 2 + 2)
                pe.sem_inc(S("p_free"), 1)
                if not first:
                    pe.wait_ge(S("relu"), i)
                for j in range(T):
                    if j % 8 == 0:
                        pe.wait_ge(S("pT_high"), i * 2 + (j // 8 + 1))
                        pe.wait_ge(S("pT_low"), i * 2 + (j // 8 + 1))
                    high, low = (pT(b, h, slice(j, j + 1)).rearrange("p a b -> p (a b)") for h in range(2))
                    pe.matmul(psum[:, 7, :], high, value(slice(j, j + 1), 0), start=(j == 0), stop=False)
                    pe.matmul(psum[:, 7, :], high, value(slice(j, j + 1), 1), start=False, stop=False)
                    last = pe.matmul(psum[:, 7, :], low, value(slice(j, j + 1), 0), start=False, stop=(j == T - 1))
                last.then_inc(S("pv"), 1)
                pe.wait_ge(S("pv"), i + 1)
                pe.sem_inc(S("pT_free"), 1)

            pe.wait_ge(S("t_made"), 4 * K4)
            scores(0, first=True)
            scores(1)
            weigh(0, 0, first=True)
            scores(2)
            with pairs(pe, 1, T - 3) as i:
                for j in range(2):
                    weigh(i + j, 1 - j)
                    scores(i + j + 2)
            weigh(T - 3, 1)
            scores(T - 1)
            weigh(T - 2, 0)
            weigh(T - 1, 1)


def gnn_stack(nc, a, out):
    with ExitStack() as ctx:
        mem = Memory(nc, ctx)
        x1_dram = nc.dram_tensor("x1_scratch", [N, D], FP32, kind="Internal").ap()
        x2_dram = nc.dram_tensor("x2_scratch", [N, D], FP32, kind="Internal").ap()
        flag = ctx.enter_context(nc.sbuf_tensor("flag", [1, 1], INT32))
        r_act, c_sup = propagation(nc, mem, a, x1_dram, x2_dram, flag)
        ones_off_diagonal = nc.values_load(flag[0:1, 0:1],
                                           skip_runtime_bounds_check_because="it is only compared with 0")
        with nc.If(ones_off_diagonal > 0):
            relation_attention(nc, mem, a, x1_dram, x2_dram, r_act, c_sup)
        attention(nc, mem, a, x2_dram, out)


def kernel(**inputs):
    import concourse.bacc as bacc
    from concourse.bass_utils import run_bass_kernel_spmd

    def column(v):
        return np.ascontiguousarray(np.asarray(v).reshape(K4, P).T)

    x, adj = np.asarray(inputs["x"]), np.asarray(inputs["adj"])
    pairs_in = np.asarray(inputs["L1_gnn_rel_pair_index"])
    padded = np.full((2, ET * P), -1, pairs_in.dtype)
    padded[:, :EDGES] = pairs_in.T
    edges = np.ascontiguousarray(padded.reshape(2 * ET, P).T)
    scalars = [inputs[n] for n in ("L2_gnn_act_alpha", "L2_gnn_wgt_alpha", "L2_gnn_act_alpha2",
                                   "L2_gnn_adj_scaling_factor")]
    arrays = {
        "x": x, "adj": adj, "adjT": np.ascontiguousarray(adj.T),
        "scalars": np.tile(np.stack([np.asarray(v).reshape(()) for v in scalars]), (P, 1)),
        "L2_w": np.asarray(inputs["L2_gnn_weight"]),
        "W_q": np.asarray(inputs["L3_gnn_W_q"]), "W_k": np.asarray(inputs["L3_gnn_W_k"]),
        "W_vT": np.ascontiguousarray(np.asarray(inputs["L3_gnn_W_v"]).T),
        "b_q": column(inputs["L3_gnn_b_q"]), "b_k": column(inputs["L3_gnn_b_k"]),
        "b_v": np.asarray(inputs["L3_gnn_b_v"]).reshape(1, D),
        "L1_wqT": np.ascontiguousarray(np.asarray(inputs["L1_gnn_Wq"]).T),
        "L1_wkT": np.ascontiguousarray(np.asarray(inputs["L1_gnn_Wk"]).T),
        "L1_bq": column(inputs["L1_gnn_bq"]), "L1_bk": column(inputs["L1_gnn_bk"]),
        "edges": edges, "iota": np.tile(np.arange(N, dtype=np.float32), (P, 1)),
    }
    nc = bacc.Bacc("TRN2", target_bir_lowering=False, num_devices=1)
    args = {n: nc.dram_tensor(f"in_{n}", v.shape, mybir.dt.from_np(v.dtype), kind="ExternalInput").ap()
            for n, v in arrays.items()}
    out = nc.dram_tensor("out_x", [N, D], FP32, kind="ExternalOutput").ap()
    gnn_stack(nc, args, out)
    result = run_bass_kernel_spmd(nc, [{f"in_{n}": v for n, v in arrays.items()}], core_ids=[0])
    return result.results[0]["out_x"]
```

```python
from contextlib import ExitStack

import numpy as np

import concourse.bass as bass
import concourse.mybir as mybir

FP32 = mybir.dt.float32
FP16 = mybir.dt.float16
INT32 = mybir.dt.int32
ALU = mybir.AluOpType
ACT = mybir.ActivationFunctionType
AX = mybir.AxisListType

P = 128
N = 2048
D = 512
T = N // P
K4 = D // P
HALF = N // 2
HT = HALF // P
HEADS = 8
DK = D // HEADS
EDGES = 10000
ET = -(-EDGES // P)
EPS = 1e-5
S64 = 64.0
PSCALE = 1024.0
ZS = 4.0
SCALE = ZS / float(np.sqrt(D))
MASKED = -10000.0
MAGIC = 12582912.0
ACT_STEPS = 15.0
WGT_STEPS = 7.0
ARENA = 79872


def ds(i, n):
    return bass.ds(i, n)


def pairs(eng, start, end):
    return eng.Fori(start, end - 1, 2)


def wait_apart(eng, semaphore, n, waited):
    eng.wait_ge(semaphore, n)
    eng.sem_inc(waited, 1)


def convolve(pe, mem, m, b, tiles):
    for k in tiles:
        for h in range(2):
            w = mem.big[:, ds(m, 1), (h * T + k) * P:(h * T + k + 1) * P].rearrange("p a b -> p (a b)")
            last = pe.matmul(mem.psum[:, b, :], w, mem.sup[:, k, :], start=(k == 0 and h == 0),
                             stop=(k == T - 1 and h == 1), skip_group_check=True)
    return last


def load_weights(eng, mem, a):
    for v, n in zip(mem.raw, ("W_q", "W_k", "W_vT")):
        eng.dma_start(v, a[n].rearrange("(k p) d -> p k d", p=P)).then_inc(mem.sem("weights_in"), 16)


def weights_high(act, mem, loaded):
    act.wait_ge(mem.sem("weights_in"), loaded)
    for v, pair in zip(mem.raw, mem.weight_pairs):
        act.activation(pair[:, 0], v, ACT.Copy, scale=S64).then_inc(mem.sem("weights_high"), 1)


def weights_low(dve, mem, pairs_before):
    for i, (v, pair) in enumerate(zip(mem.raw, mem.weight_pairs)):
        dve.wait_ge(mem.sem("weights_high"), pairs_before + i + 1)
        high, low = (pair[:, h].rearrange("p a b -> p (a b)") for h in range(2))
        dve.scalar_tensor_tensor(low, v.rearrange("p a b -> p (a b)"), S64, high, ALU.mult, ALU.subtract)\
            .then_inc(mem.sem("weights_low"), 1)


class Memory:

    def __init__(self, nc, ctx):
        self.nc, self.ctx, self.sems = nc, ctx, {}
        self.big = ctx.enter_context(nc.sbuf_tensor("big", [P, T, 4096], FP16))
        self.arena = ctx.enter_context(nc.sbuf_tensor("arena", [P, ARENA // 4], FP32))
        self.psum = ctx.enter_context(nc.psum_tensor("psum", [P, 8, 512], FP32))
        self.ident = ctx.enter_context(nc.sbuf_tensor("ident", [P, P], FP16))
        self.mean_matrix = ctx.enter_context(nc.sbuf_tensor("mean_matrix", [P, P], FP32))
        self.scal = ctx.enter_context(nc.sbuf_tensor("scal", [P, 4], FP32))
        self.small = ctx.enter_context(nc.sbuf_tensor("small", [P, 240], FP32))
        self.sup = self.carve(32768, [T, D], FP16)
        self.raw = [self.carve(8192 * i, [K4, D], FP32) for i in range(3)]
        self.weight_pairs = [self.carve(at, [2, K4, D], FP16) for at in (57344, 24576)]
        self.at = 0
        self.minus_half = self.col()
        self.f_out = self.col()
        self.relation_cols = self.col(13)

    def sem(self, name):
        if name not in self.sems:
            self.sems[name] = self.ctx.enter_context(self.nc.semaphore(name))
        return self.sems[name]

    def col(self, n=1):
        self.at += n
        assert self.at <= 240
        return self.small[:, self.at - n:self.at]

    def carve(self, at, dims, dt):
        size = int(np.prod(dims)) * (2 if dt == FP16 else 4)
        assert at % 4 == 0 and at + size <= ARENA, (at, size)
        v = self.arena[:, at // 4:(at + size) // 4]
        if dt != FP32:
            v = v.bitcast(dt)
        if len(dims) > 1:
            n = "abcd"[:len(dims)]
            v = v.rearrange(f"p ({' '.join(n)}) -> p {' '.join(n)}", **dict(zip(n, dims)))
        return v

    def bank16(self, b, n=8):
        nb = n // 8
        return self.psum[:, b:b + nb, :].rearrange("p a b -> p (a b)").bitcast(FP16)\
            .rearrange("p (a b) -> p a b", a=n)


def propagation(nc, mem, a, x1_dram, x2_dram, flag):
    big, psum, ident, S, carve = mem.big, mem.psum, mem.ident, mem.sem, mem.carve
    u = carve(0, [2, T, D], FP16)
    rows = [carve(32768 + 8192 * b, [2, HALF], FP32) for b in range(2)]
    rows0 = [carve(8192, [2, HALF], FP32), carve(24576, [2, HALF], FP32)]
    mpair = [carve(49152 + 4096 * b, [2, HALF], FP16) for b in range(2)]
    zpair = [carve(57344 + 2048 * b, [2, D], FP16) for b in range(2)]
    xbuf = [carve(61440 + 2048 * b, [D], FP32) for b in range(2)]
    wq8 = carve(65536, [K4, D], FP16)
    wraw = carve(69632, [K4, D], FP32)
    sup = mem.sup
    qpair = [carve(49152 + 2048 * b, [2, D], FP16) for b in range(2)]
    qT = [carve(53248 + 2048 * b, [2 * K4, P], FP16) for b in range(2)]
    hbuf = carve(57344, [D], FP32)
    qbuf = carve(59392, [D], FP32)
    x1buf = [carve(69632 + 2048 * b, [D], FP32) for b in range(2)]
    x2buf = [carve(73728 + 2048 * b, [D], FP32) for b in range(2)]
    sbuf2 = carve(77824, [D], FP32)

    col = mem.col
    sum_m, sum_a, sum_t = col(T), col(T), col(T)
    dz, dm = col(T), col(T)
    deg = [col() for _ in range(4)]
    stats, mv, mv2, rs1, rs2 = col(6), col(2), col(2), col(), col()
    wstats, wmv, wmean, wvar, wscale, wtmp = col(24), col(2), col(), col(), col(), [col() for _ in range(4)]
    r_act, c_sup = col(), col()
    ones_seen, ones_diag, ones_tmp = col(2 * T), col(T), col(4)
    below_one = col()
    t_factor = col()

    def regions(part, half, k):
        if isinstance(k, int):
            at = slice((part * T + k) * P, (part * T + k + 1) * P)
        else:
            at = ds((k + part * T) * P, P)
        return big[:, HT * half:HT * half + HT, at]

    def blocks(v):
        return v.rearrange("p (a b) -> p a b", b=P)

    with nc.Block() as block:
        @block.sync
        def _(sp):
            sp.dma_start(mem.scal[:], a["scalars"]).then_inc(S("scalars_in"), 16)
            def load_first(k, b, with_weight=False):
                r = ds(k * P, P)
                sp.wait_ge(S("rows0_free"), k + 1)
                sp.dma_start(rows0[b][:, 0, :], a["adj"][r, 0:HALF]).then_inc(S(f"rows0_in{b}"), 16)
                sp.dma_start(rows0[b][:, 1, :], a["adjT"][r, 0:HALF]).then_inc(S(f"rows0_in{b}"), 16)
                if with_weight:
                    sp.dma_start(wraw, a["L2_w"].rearrange("(k p) d -> p k d", p=P)).then_inc(S("w_in"), 16)
                sp.wait_ge(S("rows_free"), k + 1)
                sp.dma_start(rows[b][:, 0, :], a["adj"][r, HALF:N]).then_inc(S(f"rows_in{b}"), 16)
                sp.dma_start(rows[b][:, 1, :], a["adjT"][r, HALF:N]).then_inc(S(f"rows_in{b}"), 16)
                sp.wait_ge(S("x_free"), k + 1)
                sp.dma_start(xbuf[b], a["x"][r, :]).then_inc(S(f"x_in{b}"), 16)

            load_first(0, 0, True)
            with pairs(sp, 1, T - 1) as k:
                for j in range(2):
                    load_first(k + j, 1 - j)
            load_first(T - 1, 1)

            def load_second(k, b):
                r = ds(k * P, P)
                sp.wait_ge(S("rows_free"), k + T + 1)
                sp.dma_start(rows[b][:, 0, :], a["adj"][r, HALF:N]).then_inc(S(f"rows_in{b}"), 16)
                sp.dma_start(rows[b][:, 1, :], a["adjT"][r, HALF:N]).then_inc(S(f"rows_in{b}"), 16)
                sp.wait_ge(S("x_free"), k + T + 1)
                sp.dma_start(xbuf[b], a["x"][r, :]).then_inc(S(f"x_in{b}"), 16)

            with pairs(sp, 0, T) as k:
                for b in range(2):
                    load_second(k + b, b)

            with pairs(sp, 0, T) as m:
                for b in range(2):
                    r = ds((m + b) * P, P)
                    sp.wait_ge(S("x_free"), m + b + 2 * T + 1)
                    sp.dma_start(xbuf[b], a["x"][r, :]).then_inc(S(f"x_in{b}"), 16)
                    sp.wait_ge(S("x1_made"), m + b + 1)
                    sp.dma_start(x1_dram[r, :], x1buf[b]).then_inc(S(f"x1_kept{b}"), 16)
                    sp.wait_ge(S("x2_made"), m + b + 1)
                    sp.dma_start(x2_dram[r, :], x2buf[b]).then_inc(S(f"x2_kept{b}"), 16)
            for b in range(2):
                sp.wait_ge(S(f"x1_kept{b}"), 16 * (T // 2 + 1))
                sp.wait_ge(S(f"x2_kept{b}"), 16 * (T // 2 + 1))

        @block.gpsimd
        def _(pool):
            pool.memset(ident[:], 0.0).then_inc(S("setup"), 1)
            pool.memset(mem.mean_matrix[:], 1.0 / P).then_inc(S("setup"), 1)
            pool.memset(mem.minus_half, -0.5).then_inc(S("setup"), 1)
            pool.memset(t_factor, 0.5 / S64).then_inc(S("setup"), 1)
            pool.memset(below_one, -(S64 - 2.0 ** -6)).then_inc(S("setup"), 1)
            pool.wait_ge(S("setup"), 5)
            pool.affine_select(out=ident[:], in_=ident[:], compare_op=ALU.not_equal, fill=1.0, base=0,
                               pattern=[[-1, P]], channel_multiplier=1).then_inc(S("setup"), 1)
            pool.wait_ge(S("w_var"), 1)
            pool.tensor_tensor(wtmp[2], wvar, mem.minus_half, ALU.pow).then_inc(S("w_rstd"), 1)

            def degree(k, b):
                c = ds(k, 1)
                pool.wait_ge(S("sum_m"), k + 1)
                pool.wait_ge(S("sums_at"), k + 1)
                pool.tensor_tensor(deg[0], sum_m[:, c], sum_a[:, c], ALU.add).then_inc(S("deg_a"), 1)
                pool.tensor_tensor(deg[1], sum_t[:, c], t_factor, ALU.mult).then_inc(S("deg_a"), 1)
                wait_apart(pool, S("deg_a"), k * 2 + 2, S("waited_pool"))
                pool.tensor_scalar(deg[2], deg[0], 0.5, 1.0, ALU.mult, ALU.add).then_inc(S("deg_b"), 1)
                pool.wait_ge(S("deg_b"), k + 1)
                pool.tensor_tensor(deg[3], deg[2], deg[1], ALU.add).then_inc(S("deg_c"), 1)
                wait_apart(pool, S("deg_c"), k + 1, S("waited_pool"))
                pool.tensor_scalar(deg[0], deg[3], 1e-37, None, ALU.max).then_inc(S("deg_d"), 1)
                pool.tensor_scalar(deg[1], deg[3], 0.0, S64, ALU.is_gt, ALU.mult).then_inc(S("deg_d"), 1)
                pool.wait_ge(S("deg_d"), k * 2 + 2)
                pool.tensor_tensor(deg[2], deg[0], mem.minus_half, ALU.pow).then_inc(S("deg_e"), 1)
                pool.wait_ge(S("deg_e"), k + 1)
                pool.tensor_tensor(dz[:, c], deg[2], deg[1], ALU.mult).then_inc(S("dz"), 1)

            with pairs(pool, 0, T) as k:
                for b in range(2):
                    degree(k + b, b)
            pool.wait_ge(S("dz"), T)
            pool.tensor_scalar(dm, dz, 0.5 / (S64 * S64), None, ALU.mult).then_inc(S("dm"), 1)

            pool.wait_ge(S("w_scale"), 1)
            pool.tensor_scalar(wraw, wraw, wmean, wscale, ALU.subtract, ALU.mult).then_inc(S("w_steps"), 1)
            pool.wait_ge(S("w_steps"), 1)
            pool.tensor_scalar(wraw, wraw, 1.0, -1.0, ALU.min, ALU.max).then_inc(S("w_steps"), 1)
            pool.wait_ge(S("w_steps"), 2)
            pool.tensor_scalar(wraw, wraw, WGT_STEPS, MAGIC, ALU.mult, ALU.add).then_inc(S("w_steps"), 1)
            pool.wait_ge(S("w_steps"), 3)
            pool.tensor_scalar(wq8, wraw, MAGIC, None, ALU.subtract).then_inc(S("wq8"), 1)

            with pool.Fori(0, T) as m:
                wait_apart(pool, S("aggr1"), m + 1, S("waited_pool"))
                pool.tensor_scalar(deg[0], mv[:, 1:2], EPS, None, ALU.add).then_inc(S("ve1"), 1)
                pool.wait_ge(S("ve1"), m + 1)
                pool.tensor_tensor(rs1, deg[0], mem.minus_half, ALU.pow).then_inc(S("rstd1"), 1)
                wait_apart(pool, S("aggr2"), m + 1, S("waited_pool"))
                pool.tensor_scalar(deg[1], mv2[:, 1:2], 4.0, EPS, ALU.mult, ALU.add).then_inc(S("ve2"), 1)
                pool.wait_ge(S("ve2"), m + 1)
                pool.tensor_tensor(deg[2], deg[1], mem.minus_half, ALU.pow).then_inc(S("pw2"), 1)
                wait_apart(pool, S("pw2"), m + 1, S("waited_pool"))
                pool.tensor_scalar(rs2, deg[2], 2.0, None, ALU.mult).then_inc(S("rstd2"), 1)

        @block.scalar
        def _(act):
            def m_high(k, b, src, n):
                act.wait_ge(S("m_sum"), n)
                act.wait_ge(S("m_free"), n)
                act.activation(mpair[b][:, 0, :], src[:, 0, :], ACT.Copy, scale=S64).then_inc(S("m_high"), 1)

            def z_high(k, b, n, xn):
                act.wait_ge(S(f"x_in{b}"), xn)
                act.wait_ge(S("m_free"), n)
                act.activation(zpair[b][:, 0, :], xbuf[b], ACT.Copy, scale=dz[:, ds(k, 1)]).then_inc(S("z_high"), 1)

            def z_first(k, b):
                act.wait_ge(S("dz"), k + 1)
                z_high(k, b, k + 1, (k - b) * 8 + 16)

            def rows_first(k, b, z_before=True):
                c = ds(k, 1)
                act.wait_ge(S(f"rows0_in{b}"), (k - b) * 16 + 32)
                act.activation(regions(0, 0, k), blocks(rows0[b][:, 1, :]), ACT.Copy, scale=S64).then_inc(S("t_high"), 1)
                if z_before:
                    z_first(k - 1, 1 - b)
                m_high(k, b, rows0[b], k + 1)
                act.wait_ge(S(f"rows_in{b}"), (k - b) * 16 + 32)
                act.activation(regions(0, 1, k), blocks(rows[b][:, 1, :]), ACT.Copy, scale=S64,
                               accum_out=sum_t[:, c]).then_inc(S("t_high"), 1)
                act.activation(rows[b][:, 0, :], rows[b][:, 0, :], ACT.Copy,
                               accum_out=sum_a[:, c]).then_inc(S("sums_at"), 1)

            act.sem_inc(S("m_free"), 2)
            rows_first(0, 0, False)
            with pairs(act, 1, T - 1) as k:
                for j in range(2):
                    rows_first(k + j, 1 - j)
            rows_first(T - 1, 1)
            z_first(T - 1, 1)

            def u_high(half):
                def one(j):
                    if j < HT - 1:
                        act.wait_ge(S("sweep_done"), half * (HT - 1) + j + 1)
                    else:
                        act.wait_ge(S("m_free"), (half + 1) * T + 2)
                    act.activation(u[:, 0, HT * half + j, :], psum[:, j, :], ACT.Copy,
                                   scale=dm[:, HT * half + j:HT * half + j + 1]).then_inc(S("u_high"), 1)
                act.wait_ge(S("dm"), 1)
                for j in range(HT):
                    one(j)

            def second(k, b):
                z_high(k, b, k + T + 1, (k - b) * 8 + 16 * (T // 2) + 16)
                act.wait_ge(S(f"rows_in{b}"), (k - b) * 16 + (16 * T + 32))
                m_high(k, b, rows[b], k + T + 1)
            second(0, 0)
            u_high(0)
            with pairs(act, 1, T - 1) as k:
                for j in range(2):
                    second(k + j, 1 - j)
            second(T - 1, 1)
            u_high(1)

            def ones(m):
                for h in range(2):
                    act.activation(psum[:, 6:8, :].rearrange("p a b -> p (a b)"),
                                   big[:, ds(m, 1), HALF * h:HALF * (h + 1)].rearrange("p a b -> p (a b)"), ACT.Sign,
                                   bias=below_one, accum_out=ones_seen[:, ds(m + h * T, 1)]).then_inc(S("ones"), 1)
                    act.wait_ge(S("ones"), m * 2 + (h + 1))

            def qT_out(m, b):
                act.wait_ge(S("qT_psum"), m + 3)
                act.wait_ge(S("sup_psum"), m + 1)
                act.activation(qT[b], mem.bank16(2 + b), ACT.Copy).then_inc(S("qT_made"), 1)

            act.wait_ge(S("u_low"), T)
            ones(0)
            ones(1)
            with pairs(act, 2, T) as m:
                for b in range(2):
                    ones(m + b)
                    qT_out(m + b - 2, b)
            act.wait_ge(S("au_done"), T)
            load_weights(act, mem, a)
            qT_out(T - 2, 0)
            act.wait_ge(S("q_made"), T)
            weights_high(act, mem, 48)
            qT_out(T - 1, 1)

        @block.vector
        def _(dve):
            dve.sem_inc(S("rows0_free"), 2)
            dve.sem_inc(S("rows_free"), 2)
            dve.sem_inc(S("x_free"), 2)
            dve.sem_inc(S("qT_psum"), 2)
            dve.sem_inc(S("sup_psum"), 2)
            dve.sem_inc(S("sup_free"), 2)
            dve.sem_inc(S("au_free"), 2)
            for b in range(2):
                dve.sem_inc(S(f"x1_kept{b}"), 16)
                dve.sem_inc(S(f"x2_kept{b}"), 16)
            step = [0]

            def chained(ins):
                step[0] += 1
                ins.then_inc(S("w_chain"), 1)
                dve.wait_ge(S("w_chain"), step[0])

            act_alpha, wgt_alpha, act_alpha2, adj_scale = (mem.scal[:, i:i + 1] for i in range(4))

            def weight_moments():
                dve.wait_ge(S("scalars_in"), 16)
                dve.wait_ge(S("w_in"), 16)
                for k in range(K4):
                    last = dve.bn_stats(wstats[:, 6 * k:6 * k + 6], wraw[:, k, :])
                chained(last)
                chained(dve.bn_aggr(wmv, wstats))
                dve.engine_nop().then_inc(S("w_part_mean"), 1)
                dve.wait_ge(S("w_mean"), 1)
                chained(dve.tensor_copy(wmean, psum[:, 7, 0:1]))
                chained(dve.tensor_tensor(wtmp[0], wmv[:, 0:1], wmean, ALU.subtract))
                chained(dve.tensor_tensor(wtmp[1], wtmp[0], wtmp[0], ALU.mult))
                dve.tensor_tensor(wtmp[3], wtmp[1], wmv[:, 1:2], ALU.add).then_inc(S("w_part_var"), 1)
                dve.wait_ge(S("w_pvar"), 1)
                dve.tensor_scalar(wvar, psum[:, 7, 1:2], D * D / (D * D - 1.0), None, ALU.mult).then_inc(S("w_var"), 1)
                chained(dve.reciprocal(wtmp[1], wgt_alpha))
                dve.wait_ge(S("w_rstd"), 1)
                dve.tensor_tensor(wscale, wtmp[2], wtmp[1], ALU.mult).then_inc(S("w_scale"), 1)
                dve.wait_ge(S("w_scale"), 1)

            def constants():
                chained(dve.reciprocal(r_act, act_alpha))
                chained(dve.reciprocal(wtmp[1], act_alpha2))
                chained(dve.tensor_scalar(wtmp[0], act_alpha, 1.0 / ACT_STEPS, 1.0 / WGT_STEPS, ALU.mult, ALU.mult))
                chained(dve.tensor_tensor(wtmp[2], wtmp[0], wgt_alpha, ALU.mult))
                chained(dve.tensor_tensor(c_sup, wtmp[2], wtmp[1], ALU.mult))
                chained(dve.reciprocal(wtmp[0], adj_scale))
                chained(dve.tensor_tensor(wtmp[1], wtmp[0], adj_scale, ALU.mult))
                chained(dve.tensor_tensor(wtmp[2], wtmp[1], act_alpha2, ALU.mult))
                chained(dve.tensor_scalar(mem.f_out, wtmp[2], 1.0 / (ACT_STEPS * S64), None, ALU.mult))

            def m_rows(k, b, r, n, diag, accum):
                if accum:
                    dve.scalar_tensor_tensor(r[:, 0, :], r[:, 0, :], 1.0, r[:, 1, :], ALU.mult, ALU.add,
                                             accum_out=sum_m[:, ds(k, 1)]).then_inc(S("sum_m"), 1)
                else:
                    dve.tensor_tensor(r[:, 0, :], r[:, 0, :], r[:, 1, :], ALU.add).then_inc(S("sum_m"), 1)
                dve.wait_ge(S("sum_m"), n)
                if diag is not None:
                    d = r[:, 0, ds(diag * P, P)]
                    dve.scalar_tensor_tensor(d, ident[:], 2.0, d, ALU.mult, ALU.add).then_inc(S("m_sum"), 1)
                else:
                    dve.sem_inc(S("m_sum"), 1)

            def m_low(k, b, r, n):
                dve.wait_ge(S("m_high"), n)
                dve.wait_ge(S("m_sum"), n)
                dve.scalar_tensor_tensor(mpair[b][:, 1, :], r[:, 0, :], S64, mpair[b][:, 0, :],
                                         ALU.mult, ALU.subtract).then_inc(S("m_low"), 1)

            def z_low(k, b, n):
                dve.wait_ge(S("z_high"), n)
                dve.scalar_tensor_tensor(zpair[b][:, 1, :], xbuf[b], dz[:, ds(k, 1)], zpair[b][:, 0, :],
                                         ALU.mult, ALU.subtract).then_inc(S("z_low"), 1)

            def z_ready(k, b, n):
                z_low(k, b, n)
                dve.wait_ge(S("z_low"), n)
                dve.sem_inc(S("x_free"), 1)

            def t_low(k, half, r):
                dve.wait_ge(S("t_high"), k * 2 + (half + 1))
                dve.scalar_tensor_tensor(regions(1, half, k), blocks(r[:, 1, :]), S64, regions(0, half, k),
                                         ALU.mult, ALU.subtract).then_inc(S("t_low"), 1)

            def rows_first(k, b, diag, z_before=True):
                dve.wait_ge(S(f"rows0_in{b}"), (k - b) * 16 + 32)
                m_rows(k, b, rows0[b], k + 1, diag, True)
                if not z_before:
                    weight_moments()
                t_low(k, 0, rows0[b])
                if z_before:
                    z_ready(k - 1, 1 - b, k)
                m_low(k, b, rows0[b], k + 1)
                dve.wait_ge(S("m_low"), k + 1)
                dve.wait_ge(S("t_low"), k * 2 + 1)
                dve.sem_inc(S("rows0_free"), 1)
                dve.wait_ge(S(f"rows_in{b}"), (k - b) * 16 + 32)
                t_low(k, 1, rows[b])
                dve.wait_ge(S("sums_at"), k + 1)
                dve.wait_ge(S("t_low"), k * 2 + 2)
                dve.sem_inc(S("rows_free"), 1)

            dve.wait_ge(S("setup"), 6)
            rows_first(0, 0, 0, False)
            with pairs(dve, 1, HT - 1) as k:
                for j in range(2):
                    rows_first(k + j, 1 - j, k + j)
            rows_first(HT - 1, 1, HT - 1)
            with pairs(dve, HT, T) as k:
                for b in range(2):
                    rows_first(k + b, b, None)
            z_ready(T - 1, 1, T)
            constants()

            def u_low(half):
                for j in range(HT):
                    i = HT * half + j
                    dve.wait_ge(S("u_high"), i + 1)
                    dve.scalar_tensor_tensor(u[:, 1, i, :], psum[:, j, :], dm[:, i:i + 1], u[:, 0, i, :],
                                             ALU.mult, ALU.subtract).then_inc(S("u_low"), 1)
            def rows_second(k, b, diag):
                dve.wait_ge(S(f"rows_in{b}"), (k - b) * 16 + (16 * T + 32))
                m_rows(k, b, rows[b], k + T + 1, diag, False)
                z_ready(k, b, k + T + 1)
                m_low(k, b, rows[b], k + T + 1)
                dve.wait_ge(S("m_low"), k + T + 1)
                dve.sem_inc(S("rows_free"), 1)

            rows_second(0, 0, None)
            u_low(0)
            with pairs(dve, 1, HT - 1) as k:
                for j in range(2):
                    rows_second(k + j, 1 - j, None)
            rows_second(HT - 1, 1, None)
            with pairs(dve, HT, T) as k:
                for b in range(2):
                    rows_second(k + b, b, k + b - HT)
            u_low(1)

            def normed(m, b):
                n = m + 1
                dve.wait_ge(S("au_done"), n)
                dve.wait_ge(S(f"x_in{b}"), (m - b) * 8 + 16 * T + 16)
                dve.scalar_tensor_tensor(hbuf, psum[:, b, :], 1.0 / (S64 * S64), xbuf[b], ALU.mult,
                                         ALU.add).then_inc(S("h1"), 1)
                dve.wait_ge(S("h1"), n)
                dve.sem_inc(S("x_free"), 1)
                dve.sem_inc(S("au_free"), 1)
                dve.bn_stats(stats, hbuf).then_inc(S("stats1"), 1)
                wait_apart(dve, S("stats1"), n, S("waited_dve"))
                dve.bn_aggr(mv, stats).then_inc(S("aggr1"), 1)
                dve.scalar_tensor_tensor(sbuf2[:, 0:P], big[:, ds(m, 1), ds(m * P, P)].rearrange("p a b -> p (a b)"),
                                         S64, ident[:], ALU.is_ge, ALU.mult,
                                         accum_out=ones_diag[:, ds(m, 1)]).then_inc(S("ones_diag"), 1)
                dve.wait_ge(S("ones_diag"), n)
                dve.wait_ge(S("rstd1"), n)
                dve.wait_ge(S(f"x1_kept{b}"), (m - b) * 8 + 16)
                dve.tensor_scalar(x1buf[b], hbuf, mv[:, 0:1], rs1, ALU.subtract, ALU.mult).then_inc(S("x1_made"), 1)
                dve.wait_ge(S("x1_made"), n)
                dve.bn_stats(stats, x1buf[b]).then_inc(S("stats2"), 1)
                wait_apart(dve, S("stats2"), n, S("waited_dve"))
                dve.bn_aggr(mv2, stats).then_inc(S("aggr2"), 1)

            def quantised(m, b):
                n = m + 1
                dve.wait_ge(S("rstd2"), n)
                dve.wait_ge(S(f"x2_kept{b}"), (m - b) * 8 + 16)
                dve.tensor_scalar(x2buf[b], x1buf[b], mv2[:, 0:1], rs2, ALU.subtract, ALU.mult).then_inc(S("x2_made"), 1)
                dve.wait_ge(S("x2_made"), n)
                dve.tensor_scalar(qbuf, x2buf[b], r_act, 1.0, ALU.mult, ALU.min).then_inc(S("q_a"), 1)
                dve.wait_ge(S("q_a"), n)
                dve.tensor_scalar(qbuf, qbuf, ACT_STEPS, MAGIC, ALU.mult, ALU.add).then_inc(S("q_b"), 1)
                dve.wait_ge(S("q_b"), n)
                dve.wait_ge(S("qT_psum"), n)
                dve.tensor_scalar(qpair[b][:, 0, :], qbuf, MAGIC, None, ALU.subtract).then_inc(S("q_c"), 1)
                dve.wait_ge(S("q_c"), n)
                dve.scalar_tensor_tensor(qpair[b][:, 1, :], qbuf, MAGIC, qpair[b][:, 0, :], ALU.subtract,
                                         ALU.subtract).then_inc(S("q_made"), 1)

            def support(m, b):
                n = m + 1
                dve.wait_ge(S("sup_psum"), n + 2)
                dve.tensor_scalar(sbuf2, psum[:, 4 + b, :], c_sup, 0.0, ALU.mult, ALU.max).then_inc(S("s_a"), 1)
                dve.wait_ge(S("s_a"), n)
                dve.sem_inc(S("sup_free"), 1)
                dve.tensor_scalar(sbuf2, sbuf2, 1.0, ACT_STEPS, ALU.min, ALU.mult).then_inc(S("s_b"), 1)
                dve.wait_ge(S("s_b"), n)
                dve.tensor_scalar(sup[:, ds(m, 1), :].rearrange("p a b -> p (a b)"), sbuf2, MAGIC, MAGIC, ALU.add,
                                  ALU.subtract).then_inc(S("sup_made"), 1)
                dve.wait_ge(S("sup_made"), n)

            normed(0, 0)
            quantised(0, 0)
            normed(1, 1)
            quantised(1, 1)
            with pairs(dve, 2, T) as m:
                for b in range(2):
                    normed(m + b, b)
                    support(m + b - 2, b)
                    quantised(m + b, b)
            dve.wait_ge(S("ones"), 2 * T)
            dve.reduce_sum(ones_tmp[:, 0:1], ones_seen, axis=AX.X).then_inc(S("ones_sums"), 1)
            dve.reduce_sum(ones_tmp[:, 1:2], ones_diag, axis=AX.X).then_inc(S("ones_sums"), 1)
            dve.wait_ge(S("ones_sums"), 2)
            dve.tensor_scalar(ones_tmp[:, 3:4], ones_tmp[:, 0:1], 0.5, 0.5 * T * N, ALU.mult, ALU.add)\
                .then_inc(S("ones_sums"), 1)
            dve.wait_ge(S("ones_sums"), 3)
            dve.tensor_tensor(ones_tmp[:, 2:3], ones_tmp[:, 3:4], ones_tmp[:, 1:2], ALU.subtract)\
                .then_inc(S("ones_row"), 1)
            support(T - 2, 0)
            weights_low(dve, mem, 0)
            dve.wait_ge(S("ones_all"), 1)
            dve.tensor_scalar(flag[0:1, 0:1], psum[0:1, 7, 0:1], float(P), None, ALU.mult).then_inc(S("flag"), 1)
            support(T - 1, 1)
            dve.wait_ge(S("flag"), 1)

        @block.tensor
        def _(pe):
            pe.wait_ge(S("setup"), 6)
            pe.wait_ge(S("w_part_mean"), 1)
            pe.matmul(psum[:, 7, 0:1], mem.mean_matrix[:], wmv[:, 0:1], start=True, stop=True).then_inc(S("w_mean"), 1)
            pe.wait_ge(S("w_part_var"), 1)
            pe.matmul(psum[:, 7, 1:2], mem.mean_matrix[:], wtmp[3], start=True, stop=True).then_inc(S("w_pvar"), 1)
            pe.wait_ge(S("w_var"), 1)

            def sweep(half):
                def body(k, b, start=False, stop=False):
                    n = k + (T * half + 1)
                    pe.wait_ge(S("m_low"), n)
                    pe.wait_ge(S("z_low"), n)
                    for j in range(HT):
                        if start and half:
                            pe.wait_ge(S("u_low"), j + 1)
                        high, low = (mpair[b][:, h, j * P:(j + 1) * P] for h in range(2))
                        pe.matmul(psum[:, j, :], high, zpair[b][:, 0, :], start=start, stop=False)
                        pe.matmul(psum[:, j, :], high, zpair[b][:, 1, :], start=False, stop=False)
                        last = pe.matmul(psum[:, j, :], low, zpair[b][:, 0, :], start=False, stop=stop)
                        if stop and j < HT - 1:
                            last.then_inc(S("sweep_done"), 1)
                    last.then_inc(S("m_free"), 1)

                body(0, 0, start=True)
                body(1, 1)
                with pairs(pe, 2, T - 2) as k:
                    for b in range(2):
                        body(k + b, b)
                body(T - 2, 0)
                body(T - 1, 1, stop=True)
            sweep(0)
            sweep(1)

            def transposes(m, b):
                pe.wait_ge(S("q_made"), m + 1)
                for h in range(2):
                    for k in range(K4):
                        last = pe.transpose(mem.bank16(2 + b)[:, h * K4 + k, :], qpair[b][:, h, k * P:(k + 1) * P],
                                            ident[:])
                last.then_inc(S("qT_psum"), 1)

            def au(m, b, prev, first=False):
                pe.wait_ge(S("au_free"), m + 1)
                for k in range(T):
                    if first:
                        pe.wait_ge(S("u_low"), k + 1 if k >= b + 1 else HT + b + 1)
                    if k == T // 2 and prev:
                        transposes(m - 2, b)
                    high, low = (big[:, ds(m, 1), (h * T + k) * P:(h * T + k + 1) * P].rearrange("p a b -> p (a b)")
                                 for h in range(2))
                    pe.matmul(psum[:, b, :], high, u[:, 0, k, :], start=(k == 0), stop=False, skip_group_check=True)
                    pe.matmul(psum[:, b, :], high, u[:, 1, k, :], start=False, stop=False, skip_group_check=True)
                    last = pe.matmul(psum[:, b, :], low, u[:, 0, k, :], start=False, stop=(k == T - 1),
                                     skip_group_check=True)
                last.then_inc(S("au_done"), 1)

            def support(m, b):
                pe.wait_ge(S("qT_made"), m + 1)
                pe.wait_ge(S("sup_free"), m + 1)
                for h in range(2):
                    for k in range(K4):
                        last = pe.matmul(psum[:, 4 + b, :], qT[b][:, h * K4 + k, :], wq8[:, k, :],
                                         start=(h == 0 and k == 0), stop=(h == 1 and k == K4 - 1))
                last.then_inc(S("sup_psum"), 1)

            pe.wait_ge(S("u_low"), HT + 6)
            pe.wait_ge(S("wq8"), 1)
            au(0, 0, False, first=True)
            au(1, 1, False)
            with pairs(pe, 2, T) as m:
                for b in range(2):
                    au(m + b, b, True)
                    support(m + b - 2, b)
            transposes(T - 2, 0)
            pe.wait_ge(S("sup_made"), T - 3)
            pe.wait_ge(S("au_free"), T + 1)
            convolve(pe, mem, 0, 0, range(T - 3))
            support(T - 2, 0)
            pe.wait_ge(S("sup_made"), T - 2)
            convolve(pe, mem, 0, 0, range(T - 3, T - 2))
            pe.wait_ge(S("au_free"), T + 2)
            convolve(pe, mem, 1, 1, range(T - 2))
            pe.wait_ge(S("ones_row"), 1)
            pe.matmul(psum[0:1, 7, 0:1], ones_tmp[:, 2:3], mem.mean_matrix[:, 0:1], start=True,
                      stop=True).then_inc(S("ones_all"), 1)
            transposes(T - 1, 1)
            pe.wait_ge(S("sup_made"), T - 1)
            for m in range(2):
                convolve(pe, mem, m, m, range(T - 2, T - 1))
            support(T - 1, 1)
    return r_act, c_sup


def relation_attention(nc, mem, a, x1_dram, x2_dram, r_act, c_sup):
    big, psum, ident, S, carve = mem.big, mem.psum, mem.ident, mem.sem, mem.carve
    floats = big[:].rearrange("p a b -> p (a b)").bitcast(FP32)

    def room(at, dims):
        v = floats[:, at:at + int(np.prod(dims))]
        return v.rearrange("p (a b) -> p a b", a=dims[0]) if len(dims) > 1 else v

    x1 = room(0, [T, D])
    x1T = room(T * D, [K4, N])
    related, masked, score, shares = (room(T * D + N * i, [N]) for i in range(4))
    q, k_ = room(2 * T * D, [K4, N]), room(3 * T * D, [K4, N])
    w = [carve(8192 * i, [K4, D], FP32) for i in range(2)]
    iota = carve(0, [N], FP32)
    edge_one, node_one = carve(8192, [N], FP16), carve(12288, [P], FP16)
    q_tile = carve(12544, [K4, P], FP32)
    sharesT = carve(14592, [T, P], FP32)
    edges, edges_f = carve(22784, [2 * ET], FP32).bitcast(INT32), carve(24064, [2 * ET], FP32)
    ident_f, not_ident = carve(25344, [P], FP32), carve(25856, [P], FP32)
    biases = carve(26368, [2 * K4], FP32)
    hbuf, qbuf = carve(49152, [D], FP32), carve(51200, [D], FP32)
    qpair, qT, sbuf = carve(53248, [2, D], FP16), carve(55296, [2 * K4, P], FP16), carve(57344, [D], FP32)
    x2buf = carve(59392, [D], FP32)
    sup = mem.sup
    wq8 = carve(65536, [K4, D], FP16)
    rows = carve(0, [N], FP32)
    top, total, inv, stats, mv, ve, rstd = (mem.relation_cols[:, i:j] for i, j in
                                            ((0, 1), (1, 2), (2, 3), (3, 9), (9, 11), (11, 12), (12, 13)))

    EDGE, MASKS, HEAD, AFTER = 2, 2 + 3 * ET, 8 + 3 * ET, 8 + 3 * ET + 9 * HEADS
    TILE = AFTER + 20
    START = 9
    END = START + T * TILE

    def at(i, step):
        return i * TILE + (START + step)

    with nc.Block() as block:
        @block.sync
        def _(sp):
            sp.wait_ge(S("weights_in"), 48)
            loads = [(x1, x1_dram.rearrange("(t p) d -> p t d", p=P)),
                     (w[0], a["L1_wqT"].rearrange("(k p) d -> p k d", p=P)),
                     (w[1], a["L1_wkT"].rearrange("(k p) d -> p k d", p=P)),
                     (biases[:, 0:K4], a["L1_bq"]), (biases[:, K4:2 * K4], a["L1_bk"]), (edges, a["edges"])]
            for dst, src in loads:
                sp.dma_start(dst, src).then_inc(S("relation_in"), 16)
            sp.wait_ge(S("relation_in"), 16 * len(loads))
            sp.sem_inc(S("turn"), 1)
            sp.wait_ge(S("turn"), 8)
            sp.dma_start(iota, a["iota"]).then_inc(S("relation_in"), 16)
            sp.wait_ge(S("relation_in"), 16 * len(loads) + 16)
            sp.sem_inc(S("turn"), 1)
            with sp.Fori(0, T) as i:
                r = ds(i * P, P)
                sp.wait_ge(S("turn"), at(i, 0))
                sp.dma_start(masked, a["adj"][r, :]).then_inc(S("relation_adj"), 16)
                sp.wait_ge(S("relation_adj"), i * 16 + 16)
                sp.sem_inc(S("turn"), 1)
                sp.wait_ge(S("turn"), at(i, AFTER + 9))
                sp.dma_start(x2_dram[r, :], x2buf).then_inc(S("relation_x2"), 16)
                sp.wait_ge(S("relation_x2"), i * 16 + 16)
                sp.sem_inc(S("turn"), 1)
            with sp.Fori(0, T) as k:
                sp.wait_ge(S("turn"), k * 3 + END)
                sp.dma_start(rows, a["adjT"][ds(k * P, P), :]).then_inc(S("relation_rows"), 16)
                sp.wait_ge(S("relation_rows"), k * 16 + 16)
                sp.sem_inc(S("turn"), 1)
            sp.wait_ge(S("turn"), END + 3 * T)
            load_weights(sp, mem, a)
            sp.wait_ge(S("weights_in"), 96)

        @block.gpsimd
        def _(pool):
            with pool.Fori(0, T) as i:
                wait_apart(pool, S("turn"), at(i, AFTER + 6), S("waited_pool"))
                pool.tensor_scalar(ve, mv[:, 1:2], EPS, None, ALU.add).then_inc(S("turn"), 1)
                pool.wait_ge(S("turn"), at(i, AFTER + 7))
                pool.tensor_tensor(rstd, ve, mem.minus_half, ALU.pow).then_inc(S("turn"), 1)

        @block.scalar
        def _(act):
            act.wait_ge(S("turn"), 5)
            for k in range(K4):
                for b in range(2):
                    act.wait_ge(S("relation_x1T"), 2 * k + b + 1)
                    last = act.activation(x1T[:, k, HALF * b:HALF * (b + 1)],
                                          psum[:, 2 * b:2 * b + 2, :].rearrange("p a b -> p (a b)"), ACT.Copy)
                    last.then_inc(S("relation_x1T_out"), 1)
            act.wait_ge(S("relation_x1T_out"), 2 * K4)
            act.sem_inc(S("turn"), 1)
            with act.Fori(0, T) as i:
                for h in range(HEADS):
                    act.wait_ge(S("turn"), at(i, HEAD + 9 * h + 5))
                    act.activation(score, score, ACT.Exp, bias=top, accum_out=total).then_inc(S("turn"), 1)
                act.wait_ge(S("turn"), at(i, AFTER + 1))
                act.activation(sharesT.rearrange("p a b -> p (a b)"),
                               psum[:, 4:8, :].rearrange("p a b -> p (a b)"), ACT.Copy).then_inc(S("turn"), 1)
                act.wait_ge(S("turn"), at(i, AFTER + 15))
                act.activation(qT, mem.bank16(2), ACT.Copy).then_inc(S("turn"), 1)
            with act.Fori(0, T) as k:
                act.wait_ge(S("turn"), k * 3 + (END + 1))
                act.activation(big[:, :, ds(k * P, P)], rows.rearrange("p (a b) -> p a b", b=P), ACT.Copy,
                               scale=S64).then_inc(S("turn"), 1)
            weights_high(act, mem, 96)

        @block.vector
        def _(dve):
            dve.wait_ge(S("turn"), 1)
            dve.tensor_copy(edges_f, edges).then_inc(S("turn"), 1)
            dve.tensor_copy(ident_f, ident[:]).then_inc(S("turn"), 1)
            dve.wait_ge(S("turn"), 3)
            dve.tensor_scalar(not_ident, ident_f, -1.0, 1.0, ALU.mult, ALU.add).then_inc(S("turn"), 1)
            dve.wait_ge(S("turn"), 4)
            dve.sem_inc(S("turn"), 1)
            for n in range(2 * K4 * 4):
                side, d, c = n // (K4 * 4), n // 4 % K4, n % 4
                dve.wait_ge(S("relation_qk"), n + 1)
                dve.tensor_scalar((q, k_)[side][:, d, c * 512:(c + 1) * 512], psum[:, 4 + n % 4, :],
                                  biases[:, side * K4 + d:side * K4 + d + 1], None, ALU.add)\
                    .then_inc(S("relation_qk_out"), 1)
            dve.wait_ge(S("relation_qk_out"), 8 * K4)
            dve.sem_inc(S("turn"), 1)
            dve.sem_inc(S("turn"), 1)
            with dve.Fori(0, T) as i:
                diag = ds(i * P, P)
                dve.wait_ge(S("turn"), at(i, 1))
                dve.tensor_copy(q_tile, q[:, :, diag]).then_inc(S("turn"), 1)
                with dve.Fori(0, ET) as e:
                    dve.wait_ge(S("turn"), i * TILE + e * 3 + (START + EDGE))
                    dve.tensor_scalar(node_one, iota[:, diag], edges_f[:, ds(e, 1)], None, ALU.is_equal)\
                        .then_inc(S("turn"), 1)
                    dve.tensor_scalar(edge_one, iota, edges_f[:, ds(e + ET, 1)], None, ALU.is_equal)\
                        .then_inc(S("turn"), 1)
                dve.wait_ge(S("turn"), at(i, MASKS))
                dve.tensor_scalar(related, psum[:, 0:4, :].rearrange("p a b -> p (a b)"), 1.0, float(DK) ** -0.5,
                                  ALU.min, ALU.mult).then_inc(S("turn"), 1)
                dve.wait_ge(S("turn"), at(i, MASKS + 1))
                dve.tensor_tensor(related[:, diag], related[:, diag], not_ident, ALU.mult).then_inc(S("turn"), 1)
                dve.tensor_scalar(masked, masked, 1.0, 3.0e38, ALU.is_equal, ALU.mult).then_inc(S("turn"), 1)
                dve.wait_ge(S("turn"), at(i, MASKS + 3))
                dve.tensor_scalar(masked, masked, 3.0e38, None, ALU.subtract).then_inc(S("turn"), 1)
                dve.wait_ge(S("turn"), at(i, MASKS + 4))
                dve.tensor_tensor(masked[:, diag], masked[:, diag], not_ident, ALU.mult).then_inc(S("turn"), 1)
                dve.wait_ge(S("turn"), at(i, MASKS + 5))
                dve.scalar_tensor_tensor(masked[:, diag], ident_f, 1e-7, masked[:, diag], ALU.mult, ALU.add)\
                    .then_inc(S("turn"), 1)
                for h in range(HEADS):
                    first = HEAD + 9 * h
                    dve.wait_ge(S("turn"), at(i, first + 1))
                    dve.tensor_tensor(score, psum[:, 0:4, :].rearrange("p a b -> p (a b)"), related, ALU.mult)\
                        .then_inc(S("turn"), 1)
                    dve.wait_ge(S("turn"), at(i, first + 2))
                    dve.tensor_tensor(score, score, masked, ALU.add).then_inc(S("turn"), 1)
                    dve.wait_ge(S("turn"), at(i, first + 3))
                    dve.tensor_reduce(inv, score, axis=AX.X, op=ALU.max).then_inc(S("turn"), 1)
                    dve.wait_ge(S("turn"), at(i, first + 4))
                    dve.tensor_scalar(top, inv, -1.0, None, ALU.mult).then_inc(S("turn"), 1)
                    dve.wait_ge(S("turn"), at(i, first + 6))
                    dve.reciprocal(inv, total).then_inc(S("turn"), 1)
                    dve.wait_ge(S("turn"), at(i, first + 7))
                    dve.tensor_scalar(ve, inv, 1.0 / HEADS, None, ALU.mult).then_inc(S("turn"), 1)
                    dve.wait_ge(S("turn"), at(i, first + 8))
                    if h == 0:
                        dve.tensor_scalar(shares, score, ve, None, ALU.mult).then_inc(S("turn"), 1)
                    else:
                        dve.scalar_tensor_tensor(shares, score, ve, shares, ALU.mult, ALU.add).then_inc(S("turn"), 1)
                dve.wait_ge(S("turn"), at(i, AFTER + 3))
                dve.tensor_tensor(hbuf, psum[:, 0, :], x1[:, ds(i, 1), :].rearrange("p a b -> p (a b)"), ALU.add)\
                    .then_inc(S("turn"), 1)
                dve.wait_ge(S("turn"), at(i, AFTER + 4))
                dve.bn_stats(stats, hbuf).then_inc(S("turn"), 1)
                wait_apart(dve, S("turn"), at(i, AFTER + 5), S("waited_dve"))
                dve.bn_aggr(mv, stats).then_inc(S("turn"), 1)
                dve.wait_ge(S("turn"), at(i, AFTER + 8))
                dve.tensor_scalar(x2buf, hbuf, mv[:, 0:1], rstd, ALU.subtract, ALU.mult).then_inc(S("turn"), 1)
                dve.wait_ge(S("turn"), at(i, AFTER + 10))
                dve.tensor_scalar(qbuf, x2buf, r_act, 1.0, ALU.mult, ALU.min).then_inc(S("turn"), 1)
                dve.wait_ge(S("turn"), at(i, AFTER + 11))
                dve.tensor_scalar(qbuf, qbuf, ACT_STEPS, MAGIC, ALU.mult, ALU.add).then_inc(S("turn"), 1)
                dve.wait_ge(S("turn"), at(i, AFTER + 12))
                dve.tensor_scalar(qpair[:, 0, :], qbuf, MAGIC, None, ALU.subtract).then_inc(S("turn"), 1)
                dve.wait_ge(S("turn"), at(i, AFTER + 13))
                dve.scalar_tensor_tensor(qpair[:, 1, :], qbuf, MAGIC, qpair[:, 0, :], ALU.subtract, ALU.subtract)\
                    .then_inc(S("turn"), 1)
                dve.wait_ge(S("turn"), at(i, AFTER + 17))
                dve.tensor_scalar(sbuf, psum[:, 4, :], c_sup, 0.0, ALU.mult, ALU.max).then_inc(S("turn"), 1)
                dve.wait_ge(S("turn"), at(i, AFTER + 18))
                dve.tensor_scalar(sbuf, sbuf, 1.0, ACT_STEPS, ALU.min, ALU.mult).then_inc(S("turn"), 1)
                dve.wait_ge(S("turn"), at(i, AFTER + 19))
                dve.tensor_scalar(sup[:, ds(i, 1), :].rearrange("p a b -> p (a b)"), sbuf, MAGIC, MAGIC, ALU.add,
                                  ALU.subtract).then_inc(S("turn"), 1)
            with dve.Fori(0, T) as k:
                dve.wait_ge(S("turn"), k * 3 + (END + 2))
                dve.scalar_tensor_tensor(big[:, :, ds(k * P + N, P)], rows.rearrange("p (a b) -> p a b", b=P), S64,
                                         big[:, :, ds(k * P, P)], ALU.mult, ALU.subtract).then_inc(S("turn"), 1)
            weights_low(dve, mem, 2)

        @block.tensor
        def _(pe):
            pe.wait_ge(S("turn"), 5)
            for k in range(K4):
                for b in range(2):
                    if k:
                        pe.wait_ge(S("relation_x1T_out"), 2 * (k - 1) + b + 1)
                    for t in range(HT):
                        last = pe.transpose(psum[:, 2 * b + t // 4, t % 4 * P:(t % 4 + 1) * P],
                                            x1[:, HT * b + t, k * P:(k + 1) * P], ident_f)
                    last.then_inc(S("relation_x1T"), 1)
            pe.wait_ge(S("turn"), 6)
            for n in range(2 * K4 * 4):
                side, d, c = n // (K4 * 4), n // 4 % K4, n % 4
                if n >= 4:
                    pe.wait_ge(S("relation_qk_out"), n - 3)
                for k in range(K4):
                    last = pe.matmul(psum[:, 4 + n % 4, :], w[side][:, k, d * P:(d + 1) * P],
                                     x1T[:, k, c * 512:(c + 1) * 512], start=(k == 0), stop=(k == K4 - 1))
                last.then_inc(S("relation_qk"), 1)
            with pe.Fori(0, T) as i:
                def count(e, start=False, stop=False):
                    pe.wait_ge(S("turn"), i * TILE + e * 3 + (START + EDGE + 2))
                    for c in range(4):
                        last = pe.matmul(psum[:, c, :], node_one, edge_one[:, c * 512:(c + 1) * 512],
                                         start=start, stop=stop)
                    last.then_inc(S("turn"), 1)
                count(0, start=True)
                with pe.Fori(1, ET - 1) as e:
                    count(e)
                count(ET - 1, stop=True)
                for h in range(HEADS):
                    pe.wait_ge(S("turn"), at(i, HEAD + 9 * h))
                    r = slice(DK * (h % 2), DK * (h % 2) + DK)
                    for c in range(4):
                        last = pe.matmul(psum[:, c, :], q_tile[r, h // 2, :], k_[r, h // 2, c * 512:(c + 1) * 512],
                                         start=True, stop=True)
                    last.then_inc(S("turn"), 1)
                pe.wait_ge(S("turn"), at(i, AFTER))
                for t in range(T):
                    last = pe.transpose(psum[:, 4 + t // 4, t % 4 * P:(t % 4 + 1) * P], shares[:, t * P:(t + 1) * P],
                                        ident_f)
                last.then_inc(S("turn"), 1)
                pe.wait_ge(S("turn"), at(i, AFTER + 2))
                for t in range(T):
                    last = pe.matmul(psum[:, 0, :], sharesT[:, t, :], x1[:, t, :], start=(t == 0), stop=(t == T - 1))
                last.then_inc(S("turn"), 1)
                pe.wait_ge(S("turn"), at(i, AFTER + 14))
                for h in range(2):
                    for k in range(K4):
                        last = pe.transpose(mem.bank16(2)[:, h * K4 + k, :], qpair[:, h, k * P:(k + 1) * P], ident[:])
                last.then_inc(S("turn"), 1)
                pe.wait_ge(S("turn"), at(i, AFTER + 16))
                for h in range(2):
                    for k in range(K4):
                        last = pe.matmul(psum[:, 4, :], qT[:, h * K4 + k, :], wq8[:, k, :],
                                         start=(h == 0 and k == 0), stop=(h == 1 and k == K4 - 1))
                last.then_inc(S("turn"), 1)
            pe.wait_ge(S("turn"), END + 3 * T)
            for m in range(2):
                convolve(pe, mem, m, m, range(T - 1))


def attention(nc, mem, a, x2_dram, out):
    big, psum, ident, S, carve = mem.big, mem.psum, mem.ident, mem.sem, mem.carve
    x3 = carve(0, [T, D], FP32)
    sup = mem.sup
    wvt = mem.raw[2]
    (wq, wk) = mem.weight_pairs
    g = carve(49152, [2, K4, D], FP16)
    wv = carve(57344, [2, K4, D], FP16)
    x2in = [carve(65536 + 2048 * b, [D], FP32) for b in range(2)]
    hbuf = carve(69632, [D], FP32)
    x3pair = [carve(71680, [2, D], FP16), carve(75776, [2, D], FP16)]
    v_sum = carve(73728, [D], FP32)
    t_sum = [v_sum, hbuf]
    T_BANK = (6, 7, 0, 1)
    bv = carve(77824, [D], FP32)
    rows = [carve(32768 + 8192 * b, [N], FP32) for b in range(2)]
    mask = carve(49152, [N], FP16)
    ppair = [carve(53248 + 8192 * b, [2, N], FP16) for b in range(2)]
    attended = [carve(69632 + 2048 * b, [D], FP32) for b in range(2)]

    mem.at = 15
    col = mem.col
    biases = col(2 * K4)
    bias_high, bias_low = (col(K4).bitcast(FP16) for _ in range(2))
    gk, wc, wc_pair, c0, tmpc = col(K4), col(K4), col(K4), col(), col(K4)
    wc_high, wc_low = wc_pair[:, 0:2].bitcast(FP16), wc_pair[:, 2:4].bitcast(FP16)
    ci = col(T)
    bqk_sum = col()
    stats, mv, ve, rstd = col(6), col(2), col(), col()
    top, bias, total, inv = col(2), col(2), col(2), col(2)

    def xT(tiles, part, k):
        return big[:, tiles, (part * K4 + k) * P:(part * K4 + k + 1) * P]

    def tT(tiles, part, k):
        return big[:, tiles, 1024 + (part * K4 + k) * P:1024 + (part * K4 + k + 1) * P]

    def value(tile, part):
        return big[:, tile, 2048 + part * D:2048 + (part + 1) * D].rearrange("p a b -> p (a b)")

    def pT(b, part, tiles):
        return big[:, tiles, 3072 + (2 * b + part) * P:3072 + (2 * b + part + 1) * P]

    with nc.Block() as block:
        @block.sync
        def _(sp):
            def load_x2(m, b):
                sp.wait_ge(S("x2_free"), m + 1)
                sp.dma_start(x2in[b], x2_dram[ds(m * P, P), :]).then_inc(S(f"x2_in{b}"), 16)

            load_x2(0, 0)
            load_x2(1, 1)
            sp.dma_start(biases[:, 0:K4], a["b_q"]).then_inc(S("biases_in"), 16)
            sp.dma_start(biases[:, K4:2 * K4], a["b_k"]).then_inc(S("biases_in"), 16)
            sp.dma_start(bv, a["b_v"].to_broadcast([P, D])).then_inc(S("biases_in"), 16)
            with pairs(sp, 2, T) as m:
                for b in range(2):
                    load_x2(m + b, b)
            sp.wait_ge(S("l3_psum"), T)
            with pairs(sp, 0, T) as i:
                for b in range(2):
                    sp.wait_ge(S("adj_free"), i + b + 1)
                    sp.dma_start(rows[b], a["adj"][ds((i + b) * P, P), :]).then_inc(S(f"adj_in{b}"), 16)
            with sp.Fori(0, T) as i:
                sp.wait_ge(S("out_made"), i + 1)
                sp.dma_start(out[ds(i * P, P), :], x3[:, ds(i, 1), :].rearrange("p a b -> p (a b)"))\
                    .then_inc(S("stored"), 16)
            sp.wait_ge(S("stored"), 16 * T)

        @block.gpsimd
        def _(pool):
            def inverse_deviation(n, made, ve_sem, rstd_sem):
                wait_apart(pool, S(made), n, S("waited_pool"))
                pool.tensor_scalar(ve, mv[:, 1:2], EPS, None, ALU.add).then_inc(S(ve_sem), 1)
                pool.wait_ge(S(ve_sem), n)
                pool.tensor_tensor(rstd, ve, mem.minus_half, ALU.pow).then_inc(S(rstd_sem), 1)

            with pool.Fori(0, T) as m:
                inverse_deviation(m + 1, "aggr3", "ve3", "rstd3")

            with pool.Fori(0, T) as i:
                inverse_deviation(i + 1, "aggr4", "ve4", "rstd4")

        @block.scalar
        def _(act):
            def x_side(m, b):
                act.wait_ge(S("x3_made"), m + 1)
                act.wait_ge(S("xT_psum"), m + 1)
                act.activation(x3pair[b][:, 0, :], x3[:, ds(m, 1), :].rearrange("p a b -> p (a b)"),
                               ACT.Copy).then_inc(S("x3_high"), 1)

            x_side(0, 0)
            x_side(1, 1)
            for k in range(K4):
                act.wait_ge(S("g_psum"), k + 1)
                act.activation(g[:, 0, k, :], psum[:, 4 + k, :], ACT.Copy, scale=1.0 / S64).then_inc(S("g_high"), 1)
            act.wait_ge(S("small_psum"), 1)
            act.activation(wv[:, 0, :, :], wvt, ACT.Copy, scale=S64).then_inc(S("wv_high"), 1)

            def v_high(m):
                act.wait_ge(S("v_sum"), m + 1)
                act.activation(value(ds(m, 1), 0), v_sum, ACT.Copy, scale=S64).then_inc(S("v_high"), 1)

            def xT_out(m):
                act.wait_ge(S("xT_psum"), m + 3)
                act.activation(big[:, ds(m, 1), 0:1024].rearrange("p a (k c) -> p (a k) c", c=P),
                               mem.bank16(2), ACT.Copy).then_inc(S("xT_made"), 1)

            with pairs(act, 2, T) as m:
                for b in range(2):
                    xT_out(m + b - 2)
                    x_side(m + b, b)
                    v_high(m + b - 2)
            def turned_out(c):
                for e in range(K4):
                    act.wait_ge(S("t_sum"), c * K4 + e + 1)
                    act.activation(tT(slice(4 * c, 4 * c + 4), 0, e),
                                   t_sum[e % 2].rearrange("p (a b) -> p a b", b=P), ACT.Copy).then_inc(S("t_high4"), 1)

            xT_out(T - 2)
            turned_out(0)
            v_high(T - 2)
            xT_out(T - 1)
            turned_out(1)
            v_high(T - 1)
            turned_out(2)
            turned_out(3)

            def numerators(i, b):
                act.wait_ge(S("bias"), i + 1)
                act.activation(rows[b], rows[b], ACT.Exp, bias=bias[:, b:b + 1], scale=1.0 / ZS,
                               accum_out=total[:, b:b + 1]).then_inc(S("exp"), 1)
                act.wait_ge(S("exp"), i + 1)
                act.wait_ge(S("pT_l"), i * 2 + 2)
                act.activation(ppair[b][:, 0, :], rows[b], ACT.Copy).then_inc(S("p_high"), 1)

            def evacuate(i, b):
                for q in range(2):
                    act.wait_ge(S("pT_h"), i * 2 + (q + 1))
                    if q == 0:
                        act.wait_ge(S("pv"), i + 1)
                    act.activation(pT(b, 0, slice(8 * q, 8 * q + 8)), mem.bank16(4 + q), ACT.Copy)\
                        .then_inc(S("pT_high"), 1)

            def weighted(i, b):
                act.wait_ge(S("pv"), i + 3)
                act.wait_ge(S("inv"), i + 1)
                act.activation(attended[b], psum[:, 7, :], ACT.Relu, scale=inv[:, b:b + 1]).then_inc(S("relu"), 1)

            numerators(0, 0)
            evacuate(0, 0)
            with pairs(act, 0, T - 2) as i:
                for b in range(2):
                    numerators(i + b + 1, 1 - b)
                    weighted(i + b, b)
                    evacuate(i + b + 1, 1 - b)
            numerators(T - 1, 1)
            weighted(T - 2, 0)
            evacuate(T - 1, 1)
            weighted(T - 1, 1)

        @block.vector
        def _(dve):
            dve.sem_inc(S("x2_free"), 2)
            dve.sem_inc(S("l3_free"), 2)
            dve.sem_inc(S("xT_psum"), 2)
            dve.sem_inc(S("adj_free"), 2)
            dve.sem_inc(S("pT_l"), 4)
            dve.sem_inc(S("pv"), 2)
            def convolved(m, b):
                n = m + 1
                xm = x3[:, ds(m, 1), :].rearrange("p a b -> p (a b)")
                dve.wait_ge(S("l3_psum"), n)
                dve.wait_ge(S(f"x2_in{b}"), (m - b) * 8 + 16)
                dve.scalar_tensor_tensor(hbuf, psum[:, b, :], mem.f_out, x2in[b], ALU.mult, ALU.add)\
                    .then_inc(S("h3"), 1)
                dve.wait_ge(S("h3"), n)
                dve.sem_inc(S("x2_free"), 1)
                dve.sem_inc(S("l3_free"), 1)
                dve.bn_stats(stats, hbuf).then_inc(S("stats3"), 1)
                wait_apart(dve, S("stats3"), n, S("waited_dve"))
                dve.bn_aggr(mv, stats).then_inc(S("aggr3"), 1)
                dve.wait_ge(S("rstd3"), n)
                dve.tensor_scalar(xm, hbuf, mv[:, 0:1], rstd, ALU.subtract, ALU.mult).then_inc(S("x3_made"), 1)
                dve.wait_ge(S("x3_high"), n)
                dve.tensor_tensor(x3pair[b][:, 1, :], xm, x3pair[b][:, 0, :], ALU.subtract).then_inc(S("x3_low"), 1)

            def valued(m):
                n = m + 1
                dve.wait_ge(S("v_psum"), n)
                dve.scalar_tensor_tensor(v_sum, psum[:, 4, :], 1.0 / S64, bv, ALU.mult, ALU.add).then_inc(S("v_sum"), 1)
                dve.tensor_scalar(ci[:, ds(m, 1)], psum[:, 5, 0:1], SCALE / S64, c0, ALU.mult, ALU.add)\
                    .then_inc(S("ci"), 1)
                dve.wait_ge(S("v_high"), n)
                dve.scalar_tensor_tensor(value(ds(m, 1), 1), v_sum, S64, value(ds(m, 1), 0), ALU.mult,
                                         ALU.subtract).then_inc(S("v_low"), 1)
                dve.wait_ge(S("v_low"), n)

            convolved(0, 0)
            convolved(1, 1)
            dve.wait_ge(S("biases_in"), 48)
            dve.tensor_scalar(bias_high, biases, S64, None, ALU.mult).then_inc(S("bias_pairs"), 1)
            dve.wait_ge(S("bias_pairs"), 1)
            dve.scalar_tensor_tensor(bias_low, biases, S64, bias_high, ALU.mult, ALU.subtract)\
                .then_inc(S("bias_pairs"), 1)
            dve.tensor_tensor(tmpc, biases[:, 0:K4], biases[:, K4:2 * K4], ALU.mult).then_inc(S("bqk"), 1)
            dve.wait_ge(S("bqk"), 1)
            dve.reduce_sum(bqk_sum, tmpc, axis=AX.X).then_inc(S("bqk"), 1)
            for k in range(K4):
                dve.wait_ge(S("g_high"), k + 1)
                dve.scalar_tensor_tensor(g[:, 1, k, :], psum[:, 4 + k, :], 1.0 / S64, g[:, 0, k, :], ALU.mult,
                                         ALU.subtract).then_inc(S("g_low"), 1)
            dve.wait_ge(S("small_psum"), 1)
            dve.tensor_scalar(gk, psum[:, 2, 0:K4], SCALE / (S64 * S64), None, ALU.mult).then_inc(S("gk"), 1)
            dve.tensor_scalar(wc, psum[:, 2, K4:2 * K4], 1.0 / S64, None, ALU.mult).then_inc(S("wc"), 1)
            dve.wait_ge(S("wc"), 1)
            dve.tensor_copy(wc_high, wc).then_inc(S("wc"), 1)
            dve.wait_ge(S("wc"), 2)
            dve.tensor_tensor(wc_low, wc, wc_high, ALU.subtract).then_inc(S("wc"), 1)
            dve.wait_ge(S("bqk_psum"), 1)
            dve.tensor_scalar(c0, psum[:, 3, 0:1], SCALE * P, None, ALU.mult).then_inc(S("c0"), 1)
            dve.wait_ge(S("wv_high"), 1)
            dve.scalar_tensor_tensor(wv[:, 1, :, :].rearrange("p a b -> p (a b)"), wvt.rearrange("p a b -> p (a b)"), S64,
                                     wv[:, 0, :, :].rearrange("p a b -> p (a b)"), ALU.mult, ALU.subtract)\
                .then_inc(S("wv_low"), 1)
            dve.wait_ge(S("wv_low"), 1)

            with pairs(dve, 2, T) as m:
                for b in range(2):
                    convolved(m + b, b)
                    valued(m + b - 2)
            def turned_out(c):
                for e in range(K4):
                    n = c * K4 + e + 1
                    dve.wait_ge(S("t_psum"), n)
                    dve.tensor_scalar(t_sum[e % 2], psum[:, T_BANK[e], :], SCALE / S64, gk[:, e:e + 1], ALU.mult,
                                      ALU.add).then_inc(S("t_sum"), 1)
                    dve.wait_ge(S("t_high4"), n)
                    tiles = slice(4 * c, 4 * c + 4)
                    dve.tensor_tensor(tT(tiles, 1, e), t_sum[e % 2].rearrange("p (a b) -> p a b", b=P),
                                      tT(tiles, 0, e), ALU.subtract).then_inc(S("t_made"), 1)

            turned_out(0)
            valued(T - 2)
            turned_out(1)
            valued(T - 1)
            turned_out(2)
            turned_out(3)

            def scored(i, b):
                dve.wait_ge(S(f"adj_in{b}"), (i - b) * 8 + 16)
                for h in range(2):
                    dve.wait_ge(S("z"), i * 2 + (h + 1))
                    part = rows[b][:, h * HALF:(h + 1) * HALF]
                    dve.scalar_tensor_tensor(part, psum[:, 2 * h:2 * h + 2, :].rearrange("p a b -> p (a b)"),
                                             ci[:, ds(i, 1)], part, ALU.add, ALU.mult).then_inc(S("scored"), 1)

            def maximum(i, b):
                dve.wait_ge(S("scored"), i * 2 + 2)
                dve.tensor_scalar(mask, rows[b], 0.0, ZS * MASKED, ALU.is_equal, ALU.mult).then_inc(S("mask"), 1)
                wait_apart(dve, S("mask"), i + 1, S("waited_dve"))
                dve.tensor_tensor_reduce(out=rows[b], in0=rows[b], in1=mask, scale=1.0, scalar=-3.0e38,
                                         op0=ALU.add, op1=ALU.max, accum_out=top[:, b:b + 1]).then_inc(S("top"), 1)
                dve.wait_ge(S("top"), i + 1)
                dve.tensor_scalar(bias[:, b:b + 1], top[:, b:b + 1], -1.0 / ZS, float(np.log(PSCALE)), ALU.mult,
                                  ALU.add).then_inc(S("bias"), 1)

            def p_low(i, b):
                dve.wait_ge(S("p_high"), i + 1)
                dve.tensor_tensor(ppair[b][:, 1, :], rows[b], ppair[b][:, 0, :], ALU.subtract).then_inc(S("p_low"), 1)
                dve.reciprocal(top[:, b:b + 1], total[:, b:b + 1]).then_inc(S("recip"), 1)
                dve.wait_ge(S("recip"), i + 1)
                dve.tensor_scalar(inv[:, b:b + 1], top[:, b:b + 1], 1.0 / S64, None, ALU.mult).then_inc(S("inv"), 1)
                dve.wait_ge(S("p_low"), i + 1)
                dve.sem_inc(S("adj_free"), 1)

            def evacuate(i, b):
                for q in range(2):
                    dve.wait_ge(S("pT_l"), i * 2 + (q + 5))
                    if q == 0:
                        dve.wait_ge(S("pv"), i + 1)
                    dve.tensor_copy(pT(b, 1, slice(8 * q, 8 * q + 8)), mem.bank16(6 if q == 0 else 4))\
                        .then_inc(S("pT_low"), 1)

            def finished(i, b):
                n = i + 1
                xi = x3[:, ds(i, 1), :].rearrange("p a b -> p (a b)")
                dve.wait_ge(S("relu"), n)
                dve.tensor_tensor(attended[b], attended[b], xi, ALU.add).then_inc(S("h4"), 1)
                dve.wait_ge(S("h4"), n)
                dve.bn_stats(stats, attended[b]).then_inc(S("stats4"), 1)
                wait_apart(dve, S("stats4"), n, S("waited_dve"))
                dve.bn_aggr(mv, stats).then_inc(S("aggr4"), 1)
                dve.wait_ge(S("rstd4"), n)
                dve.tensor_scalar(xi, attended[b], mv[:, 0:1], rstd, ALU.subtract, ALU.mult).then_inc(S("out_made"), 1)

            scored(0, 0)
            maximum(0, 0)
            p_low(0, 0)
            evacuate(0, 0)
            with pairs(dve, 0, T - 2) as i:
                for b in range(2):
                    scored(i + b + 1, 1 - b)
                    maximum(i + b + 1, 1 - b)
                    p_low(i + b + 1, 1 - b)
                    finished(i + b, b)
                    evacuate(i + b + 1, 1 - b)
            scored(T - 1, 1)
            maximum(T - 1, 1)
            p_low(T - 1, 1)
            finished(T - 2, 0)
            evacuate(T - 1, 1)
            finished(T - 1, 1)

        @block.tensor
        def _(pe):
            def sums(m, b):
                pe.wait_ge(S("l3_free"), m + 1)
                convolve(pe, mem, m, b, range(T // 2))
                transposes(m - 2, b)
                convolve(pe, mem, m, b, range(T // 2, T)).then_inc(S("l3_psum"), 1)

            def transposes(m, b):
                pe.wait_ge(S("x3_low"), m + 1)
                for h in range(2):
                    for k in range(K4):
                        last = pe.transpose(mem.bank16(2)[:, h * K4 + k, :], x3pair[b][:, h, k * P:(k + 1) * P], ident[:])
                last.then_inc(S("xT_psum"), 1)

            def project(m):
                pe.wait_ge(S("xT_made"), m + 1)
                if not isinstance(m, int) or m > 0:
                    pe.wait_ge(S("v_low"), m)
                for part, other in ((0, 0), (0, 1), (1, 0)):
                    for k in range(K4):
                        w = xT(ds(m, 1), part, k).rearrange("p a b -> p (a b)")
                        first, end = (part, other, k) == (0, 0, 0), (part, k) == (1, K4 - 1)
                        pe.matmul(psum[:, 4, :], w, wv[:, other, k, :], start=first, stop=end)
                        last = pe.matmul(psum[:, 5, 0:1], w, (wc_high, wc_low)[other][:, k:k + 1],
                                         start=first, stop=end)
                last.then_inc(S("v_psum"), 1)

            for m in range(2):
                convolve(pe, mem, m, m, range(T - 1, T)).then_inc(S("l3_psum"), 1)
            pe.wait_ge(S("weights_low"), 2)
            for d in range(K4):
                for part, other in ((0, 0), (0, 1), (1, 0)):
                    for o in range(K4):
                        last = pe.matmul(psum[:, 4 + d, :], wq[:, part, o, d * P:(d + 1) * P], wk[:, other, o, :],
                                         start=((part, other, o) == (0, 0, 0)), stop=((part, o) == (1, K4 - 1)))
                last.then_inc(S("g_psum"), 1)
            pe.wait_ge(S("bias_pairs"), 2)
            for i, w in enumerate((wk, wq)):
                for d in range(K4):
                    for part, bias_col in ((0, bias_high), (0, bias_low), (1, bias_high)):
                        for o in range(K4):
                            last = pe.matmul(psum[:, 2, i * K4 + d:i * K4 + d + 1], w[:, part, o, d * P:(d + 1) * P],
                                             bias_col[:, i * K4 + o:i * K4 + o + 1],
                                             start=((part, o) == (0, 0) and bias_col is bias_high),
                                             stop=((part, o) == (1, K4 - 1)))
            last.then_inc(S("small_psum"), 1)
            pe.wait_ge(S("bqk"), 2)
            pe.matmul(psum[:, 3, 0:1], mem.mean_matrix[:], bqk_sum, start=True, stop=True).then_inc(S("bqk_psum"), 1)

            pe.wait_ge(S("gk"), 1)
            pe.wait_ge(S("wc"), 3)
            sums(2, 0)
            pe.wait_ge(S("g_low"), K4)
            pe.wait_ge(S("wv_low"), 1)
            project(0)
            sums(3, 1)
            project(1)
            with pairs(pe, 4, T) as m:
                for b in range(2):
                    sums(m + b, b)
                    project(m + b - 2)
            def turn_x(c):
                for e in range(K4):
                    if c:
                        pe.wait_ge(S("t_sum"), (c - 1) * K4 + e + 1)
                    elif e == 2:
                        pe.wait_ge(S("h3"), T)
                    for part, other in ((0, 0), (0, 1), (1, 0)):
                        for k in range(K4):
                            last = pe.matmul(psum[:, T_BANK[e], :], g[:, part, k, e * P:(e + 1) * P],
                                             xT(slice(4 * c, 4 * c + 4), other, k),
                                             start=((part, other, k) == (0, 0, 0)), stop=((part, k) == (1, K4 - 1)))
                    last.then_inc(S("t_psum"), 1)

            transposes(T - 2, 0)
            turn_x(0)
            project(T - 2)
            transposes(T - 1, 1)
            turn_x(1)
            project(T - 1)
            turn_x(2)
            turn_x(3)

            def scores(i, first=False, turning=None):
                for c in range(4):
                    if c == 3 and turning is not None:
                        turned(i - 1, turning)
                    if first:
                        if c < 2:
                            pe.wait_ge(S("t_sum"), 3 * K4 + T_BANK.index(c) + 1)
                    elif c % 2 == 0:
                        pe.wait_ge(S("scored"), i * 2 - 1 + c // 2)
                    for part, other in ((0, 0), (0, 1), (1, 0)):
                        for k in range(K4):
                            last = pe.matmul(psum[:, c, :], tT(ds(i, 1), part, k).rearrange("p a b -> p (a b)"),
                                             xT(slice(4 * c, 4 * c + 4), other, k),
                                             start=((part, other, k) == (0, 0, 0)), stop=((part, k) == (1, K4 - 1)))
                    if c % 2:
                        last.then_inc(S("z"), 1)

            def turn(b, part, q, bank, done):
                for j in range(8):
                    last = pe.transpose(mem.bank16(bank)[:, j, :],
                                        ppair[b][:, part, (8 * q + j) * P:(8 * q + j + 1) * P], ident[:])
                last.then_inc(S(done), 1)

            def turned(i, b):
                pe.wait_ge(S("p_high"), i + 1)
                turn(b, 0, 0, 4, "pT_h")
                pe.wait_ge(S("p_low"), i + 1)
                turn(b, 1, 0, 6, "pT_l")
                turn(b, 0, 1, 5, "pT_h")

            def weigh(i, b, first=False):
                pe.wait_ge(S("pT_high"), i * 2 + 1)
                turn(b, 1, 1, 4, "pT_l")
                if not first:
                    pe.wait_ge(S("relu"), i)
                for j in range(T):
                    if j % 8 == 0:
                        pe.wait_ge(S("pT_high"), i * 2 + (j // 8 + 1))
                        pe.wait_ge(S("pT_low"), i * 2 + (j // 8 + 1))
                    high, low = (pT(b, h, slice(j, j + 1)).rearrange("p a b -> p (a b)") for h in range(2))
                    pe.matmul(psum[:, 7, :], high, value(slice(j, j + 1), 0), start=(j == 0), stop=False)
                    pe.matmul(psum[:, 7, :], high, value(slice(j, j + 1), 1), start=False, stop=False)
                    last = pe.matmul(psum[:, 7, :], low, value(slice(j, j + 1), 0), start=False, stop=(j == T - 1))
                last.then_inc(S("pv"), 1)

            pe.wait_ge(S("t_made"), K4)
            scores(0, first=True)
            pe.wait_ge(S("t_made"), 4 * K4)
            scores(1)
            turned(0, 0)
            weigh(0, 0, first=True)
            scores(2, turning=1)
            with pairs(pe, 1, T - 3) as i:
                for j in range(2):
                    weigh(i + j, 1 - j)
                    scores(i + j + 2, turning=j)
            weigh(T - 3, 1)
            scores(T - 1, turning=0)
            weigh(T - 2, 0)
            turned(T - 1, 1)
            weigh(T - 1, 1)


def gnn_stack(nc, a, out):
    with ExitStack() as ctx:
        mem = Memory(nc, ctx)
        x1_dram = nc.dram_tensor("x1_scratch", [N, D], FP32, kind="Internal").ap()
        x2_dram = nc.dram_tensor("x2_scratch", [N, D], FP32, kind="Internal").ap()
        flag = ctx.enter_context(nc.sbuf_tensor("flag", [1, 1], INT32))
        r_act, c_sup = propagation(nc, mem, a, x1_dram, x2_dram, flag)
        ones_off_diagonal = nc.values_load(flag[0:1, 0:1],
                                           skip_runtime_bounds_check_because="it is only compared with 0")
        with nc.If(ones_off_diagonal > 0):
            relation_attention(nc, mem, a, x1_dram, x2_dram, r_act, c_sup)
        attention(nc, mem, a, x2_dram, out)


def kernel(**inputs):
    import concourse.bacc as bacc
    from concourse.bass_utils import run_bass_kernel_spmd

    def column(v):
        return np.ascontiguousarray(np.asarray(v).reshape(K4, P).T)

    x, adj = np.asarray(inputs["x"]), np.asarray(inputs["adj"])
    pairs_in = np.asarray(inputs["L1_gnn_rel_pair_index"])
    padded = np.full((2, ET * P), -1, pairs_in.dtype)
    padded[:, :EDGES] = pairs_in.T
    edges = np.ascontiguousarray(padded.reshape(2 * ET, P).T)
    scalars = [inputs[n] for n in ("L2_gnn_act_alpha", "L2_gnn_wgt_alpha", "L2_gnn_act_alpha2",
                                   "L2_gnn_adj_scaling_factor")]
    arrays = {
        "x": x, "adj": adj, "adjT": np.ascontiguousarray(adj.T),
        "scalars": np.tile(np.stack([np.asarray(v).reshape(()) for v in scalars]), (P, 1)),
        "L2_w": np.asarray(inputs["L2_gnn_weight"]),
        "W_q": np.asarray(inputs["L3_gnn_W_q"]), "W_k": np.asarray(inputs["L3_gnn_W_k"]),
        "W_vT": np.ascontiguousarray(np.asarray(inputs["L3_gnn_W_v"]).T),
        "b_q": column(inputs["L3_gnn_b_q"]), "b_k": column(inputs["L3_gnn_b_k"]),
        "b_v": np.asarray(inputs["L3_gnn_b_v"]).reshape(1, D),
        "L1_wqT": np.ascontiguousarray(np.asarray(inputs["L1_gnn_Wq"]).T),
        "L1_wkT": np.ascontiguousarray(np.asarray(inputs["L1_gnn_Wk"]).T),
        "L1_bq": column(inputs["L1_gnn_bq"]), "L1_bk": column(inputs["L1_gnn_bk"]),
        "edges": edges, "iota": np.tile(np.arange(N, dtype=np.float32), (P, 1)),
    }
    nc = bacc.Bacc("TRN2", target_bir_lowering=False, num_devices=1)
    args = {n: nc.dram_tensor(f"in_{n}", v.shape, mybir.dt.from_np(v.dtype), kind="ExternalInput").ap()
            for n, v in arrays.items()}
    out = nc.dram_tensor("out_x", [N, D], FP32, kind="ExternalOutput").ap()
    gnn_stack(nc, args, out)
    result = run_bass_kernel_spmd(nc, [{f"in_{n}": v for n, v in arrays.items()}], core_ids=[0])
    return result.results[0]["out_x"]
```

```python
from contextlib import ExitStack

import numpy as np

import concourse.bass as bass
import concourse.mybir as mybir

FP32 = mybir.dt.float32
FP16 = mybir.dt.float16
INT32 = mybir.dt.int32
ALU = mybir.AluOpType
ACT = mybir.ActivationFunctionType
AX = mybir.AxisListType

P = 128
N = 2048
D = 512
T = N // P
K4 = D // P
HALF = N // 2
HT = HALF // P
HEADS = 8
DK = D // HEADS
EDGES = 10000
ET = -(-EDGES // P)
EPS = 1e-5
S64 = 64.0
SUMS = 128.0
PSCALE = 1024.0
ZS = 4.0
SCALE = ZS / float(np.sqrt(D))
MASKED = -10000.0
MAGIC = 12582912.0
ACT_STEPS = 15.0
WGT_STEPS = 7.0
ARENA = 79872


def ds(i, n):
    return bass.ds(i, n)


def pairs(eng, start, end):
    return eng.Fori(start, end - 1, 2)


def fours(eng, start, end):
    return eng.Fori(start, end - 3, 4)


def wait_apart(eng, semaphore, n, waited):
    eng.wait_ge(semaphore, n)
    eng.sem_inc(waited, 1)


def convolve(pe, mem, m, b, tiles):
    for k in tiles:
        for h in range(2):
            w = mem.big[:, ds(m, 1), (h * T + k) * P:(h * T + k + 1) * P].rearrange("p a b -> p (a b)")
            last = pe.matmul(mem.psum[:, b, :], w, mem.sup[:, k, :], start=(k == 0 and h == 0),
                             stop=(k == T - 1 and h == 1), skip_group_check=True)
    return last


def load_weights(eng, mem, a):
    for v, n in zip(mem.raw, ("W_q", "W_k", "W_vT")):
        eng.dma_start(v, a[n].rearrange("(k p) d -> p k d", p=P)).then_inc(mem.sem("weights_in"), 16)


def weights_high(act, mem, loaded):
    act.wait_ge(mem.sem("weights_in"), loaded)
    for v, pair in zip(mem.raw, mem.weight_pairs):
        act.activation(pair[:, 0], v, ACT.Copy, scale=S64).then_inc(mem.sem("weights_high"), 1)


def weights_low(dve, mem, pairs_before):
    for i, (v, pair) in enumerate(zip(mem.raw, mem.weight_pairs)):
        dve.wait_ge(mem.sem("weights_high"), pairs_before + i + 1)
        high, low = (pair[:, h].rearrange("p a b -> p (a b)") for h in range(2))
        dve.scalar_tensor_tensor(low, v.rearrange("p a b -> p (a b)"), S64, high, ALU.mult, ALU.subtract)\
            .then_inc(mem.sem("weights_low"), 1)


class Memory:

    def __init__(self, nc, ctx):
        self.nc, self.ctx, self.sems = nc, ctx, {}
        self.big = ctx.enter_context(nc.sbuf_tensor("big", [P, T, 4096], FP16))
        self.arena = ctx.enter_context(nc.sbuf_tensor("arena", [P, ARENA // 4], FP32))
        self.psum = ctx.enter_context(nc.psum_tensor("psum", [P, 8, 512], FP32))
        self.ident = ctx.enter_context(nc.sbuf_tensor("ident", [P, P], FP16))
        self.mean_matrix = ctx.enter_context(nc.sbuf_tensor("mean_matrix", [P, P], FP32))
        self.scal = ctx.enter_context(nc.sbuf_tensor("scal", [P, 4], FP32))
        self.small = ctx.enter_context(nc.sbuf_tensor("small", [P, 240], FP32))
        self.sup = self.carve(32768, [T, D], FP16)
        self.raw = [self.carve(8192 * i, [K4, D], FP32) for i in range(3)]
        self.weight_pairs = [self.carve(at, [2, K4, D], FP16) for at in (57344, 24576)]
        self.at = 0
        self.minus_half = self.col()
        self.f_out = self.col()
        self.relation_cols = self.col(13)

    def sem(self, name):
        if name not in self.sems:
            self.sems[name] = self.ctx.enter_context(self.nc.semaphore(name))
        return self.sems[name]

    def col(self, n=1):
        self.at += n
        assert self.at <= 240
        return self.small[:, self.at - n:self.at]

    def carve(self, at, dims, dt):
        size = int(np.prod(dims)) * (2 if dt == FP16 else 4)
        assert at % 4 == 0 and at + size <= ARENA, (at, size)
        v = self.arena[:, at // 4:(at + size) // 4]
        if dt != FP32:
            v = v.bitcast(dt)
        if len(dims) > 1:
            n = "abcd"[:len(dims)]
            v = v.rearrange(f"p ({' '.join(n)}) -> p {' '.join(n)}", **dict(zip(n, dims)))
        return v

    def bank16(self, b, n=8):
        nb = n // 8
        return self.psum[:, b:b + nb, :].rearrange("p a b -> p (a b)").bitcast(FP16)\
            .rearrange("p (a b) -> p a b", a=n)


def propagation(nc, mem, a, x1_dram, x2_dram, flag):
    big, psum, ident, S, carve = mem.big, mem.psum, mem.ident, mem.sem, mem.carve
    u = carve(0, [2, T, D], FP16)
    rows = [carve(32768 + 8192 * b, [2, HALF], FP32) for b in range(2)]
    rows0 = [carve(8192 * b, [2, HALF], FP32) for b in range(4)]
    rows2 = rows + [rows0[1], rows0[3]]
    rows2_in = ["rows_in0", "rows_in1", "rows0_in1", "rows0_in3"]
    mpair = [carve(49152 + 4096 * b, [2, HALF], FP16) for b in range(2)]
    zpair = [carve(57344 + 2048 * b, [2, D], FP16) for b in range(2)]
    xbuf = [carve(61440 + 2048 * b, [D], FP32) for b in range(2)]
    wq8 = carve(65536, [K4, D], FP16)
    wraw = carve(69632, [K4, D], FP32)
    sup = mem.sup
    qpair = [carve(49152 + 2048 * b, [2, D], FP16) for b in range(2)]
    qT = [carve(53248 + 2048 * b, [2 * K4, P], FP16) for b in range(2)]
    hbuf = carve(57344, [D], FP32)
    qbuf = carve(59392, [D], FP32)
    x1buf = [carve(69632 + 2048 * b, [D], FP32) for b in range(2)]
    x2buf = [carve(73728 + 2048 * b, [D], FP32) for b in range(2)]
    sbuf2 = carve(77824, [D], FP32)

    col = mem.col
    sum_m, sum_a, sum_t = col(T), col(T), col(T)
    dz, dm = col(T), col(T)
    deg = [col() for _ in range(4)]
    stats, mv, mv2, rs1, rs2 = col(6), col(2), col(2), col(), col()
    wstats, wmv, wmean, wvar, wscale, wtmp = col(24), col(2), col(), col(), col(), [col() for _ in range(4)]
    r_act, c_sup = col(), col()
    ones_seen, ones_diag, ones_tmp = col(2 * T), col(T), col(4)
    below_one = col()
    sums_scale, diagonal = col(), col()

    def regions(part, half, k):
        if isinstance(k, int):
            at = slice((part * T + k) * P, (part * T + k + 1) * P)
        else:
            at = ds((k + part * T) * P, P)
        return big[:, HT * half:HT * half + HT, at]

    def rows2_count(k, b4):
        return (k - b4) * 8 + ((T // 2 if b4 < 2 else T // 4) * 32 + 32)

    def blocks(v):
        return v.rearrange("p (a b) -> p a b", b=P)

    with nc.Block() as block:
        @block.sync
        def _(sp):
            sp.dma_start(mem.scal[:], a["scalars"]).then_inc(S("scalars_in"), 16)

            def load_first(k, b4):
                r, b = ds(k * P, P), b4 % 2
                sp.wait_ge(S("rows0_free"), k + 1)
                sp.dma_start(rows0[b4][:, 0, :], a["adj"][r, 0:HALF]).then_inc(S(f"rows0_in{b4}"), 16)
                sp.dma_start(rows0[b4][:, 1, :], a["adjT"][r, 0:HALF]).then_inc(S(f"rows0_in{b4}"), 16)
                sp.wait_ge(S("sums_at"), k + 1)
                sp.dma_start(rows[b][:, 1, :], a["adjT"][r, HALF:N]).then_inc(S(f"rows_in{b}"), 16)
                sp.dma_start(rows[b][:, 0, :], a["adj"][r, HALF:N]).then_inc(S(f"rows_in{b}"), 16)
                sp.wait_ge(S("x_free"), k + 1)
                sp.dma_start(xbuf[b], a["x"][r, :]).then_inc(S(f"x_in{b}"), 16)

            with fours(sp, 0, T) as k:
                for b in range(4):
                    load_first(k + b, b)

            def load_second(k, b4):
                r, b = ds(k * P, P), b4 % 2
                sp.dma_start(rows2[b4][:, 0, :], a["adj"][r, HALF:N]).then_inc(S(rows2_in[b4]), 16)
                sp.dma_start(rows2[b4][:, 1, :], a["adjT"][r, HALF:N]).then_inc(S(rows2_in[b4]), 16)
                sp.wait_ge(S("x_free"), k + T + 1)
                sp.dma_start(xbuf[b], a["x"][r, :]).then_inc(S(f"x_in{b}"), 16)

            sp.wait_ge(S("sums_at"), T + 1)
            load_second(0, 0)
            sp.wait_ge(S("sums_at"), T + 2)
            load_second(1, 1)
            sp.wait_ge(S("rows0_free"), T + 2)
            load_second(2, 2)
            sp.wait_ge(S("rows0_free"), T + 4)
            load_second(3, 3)
            sp.dma_start(wraw, a["L2_w"].rearrange("(k p) d -> p k d", p=P)).then_inc(S("w_in"), 16)

            with fours(sp, 4, T) as k:
                for b in range(4):
                    sp.wait_ge(S("rows_free"), k + b - 3)
                    load_second(k + b, b)

            with pairs(sp, 0, T) as m:
                for b in range(2):
                    r = ds((m + b) * P, P)
                    sp.wait_ge(S("x_free"), m + b + 2 * T + 1)
                    sp.dma_start(xbuf[b], a["x"][r, :]).then_inc(S(f"x_in{b}"), 16)
                    sp.wait_ge(S("x1_made"), m + b + 1)
                    sp.dma_start(x1_dram[r, :], x1buf[b]).then_inc(S(f"x1_kept{b}"), 16)
                    sp.wait_ge(S("x2_made"), m + b + 1)
                    sp.dma_start(x2_dram[r, :], x2buf[b]).then_inc(S(f"x2_kept{b}"), 16)
            for b in range(2):
                sp.wait_ge(S(f"x1_kept{b}"), 16 * (T // 2 + 1))
                sp.wait_ge(S(f"x2_kept{b}"), 16 * (T // 2 + 1))

        @block.gpsimd
        def _(pool):
            pool.memset(ident[:], 0.0).then_inc(S("setup"), 1)
            pool.memset(mem.mean_matrix[:], 1.0 / P).then_inc(S("setup"), 1)
            pool.memset(mem.minus_half, -0.5).then_inc(S("setup"), 1)
            pool.memset(sums_scale, SUMS).then_inc(S("setup"), 1)
            pool.memset(diagonal, 2.0 * SUMS).then_inc(S("setup"), 1)
            pool.memset(below_one, -(S64 - 2.0 ** -6)).then_inc(S("setup"), 1)
            pool.wait_ge(S("setup"), 6)
            pool.affine_select(out=ident[:], in_=ident[:], compare_op=ALU.not_equal, fill=1.0, base=0,
                               pattern=[[-1, P]], channel_multiplier=1).then_inc(S("setup"), 1)

            def degree(k, b):
                c = ds(k, 1)
                pool.wait_ge(S("sums_at"), k + 3)
                pool.tensor_tensor(deg[0], sum_a[:, c], sum_t[:, c], ALU.add).then_inc(S("deg_a"), 1)
                pool.wait_ge(S("deg_a"), k * 2 + 1)
                pool.tensor_tensor(deg[1], deg[0], diagonal, ALU.add).then_inc(S("deg_a"), 1)
                pool.wait_ge(S("sum_m"), k + 1)
                pool.tensor_tensor(deg[2], sum_m[:, c], sums_scale, ALU.mult).then_inc(S("deg_b"), 1)
                pool.wait_ge(S("deg_a"), k * 2 + 2)
                pool.wait_ge(S("deg_b"), k + 1)
                pool.tensor_tensor(deg[3], deg[2], deg[1], ALU.add).then_inc(S("deg_c"), 1)
                wait_apart(pool, S("deg_c"), k + 1, S("waited_pool"))
                pool.tensor_scalar(deg[0], deg[3], 1e-37, None, ALU.max).then_inc(S("deg_d"), 1)
                pool.tensor_scalar(deg[1], deg[3], 0.0, S64 * (2.0 * SUMS) ** 0.5, ALU.is_gt, ALU.mult)\
                    .then_inc(S("deg_d"), 1)
                pool.wait_ge(S("deg_d"), k * 2 + 2)
                pool.tensor_tensor(deg[2], deg[0], mem.minus_half, ALU.pow).then_inc(S("deg_e"), 1)
                pool.wait_ge(S("deg_e"), k + 1)
                pool.tensor_tensor(dz[:, c], deg[2], deg[1], ALU.mult).then_inc(S("dz"), 1)

            with pairs(pool, 0, T) as k:
                for b in range(2):
                    degree(k + b, b)
            pool.wait_ge(S("dz"), T)
            pool.tensor_scalar(dm, dz, 0.5 / (S64 * S64), None, ALU.mult).then_inc(S("dm"), 1)

            pool.wait_ge(S("w_var"), 1)
            pool.tensor_tensor(wtmp[2], wvar, mem.minus_half, ALU.pow).then_inc(S("w_rstd"), 1)

            with pool.Fori(0, T) as m:
                wait_apart(pool, S("aggr1"), m + 1, S("waited_pool"))
                pool.tensor_scalar(deg[0], mv[:, 1:2], EPS, None, ALU.add).then_inc(S("ve1"), 1)
                pool.wait_ge(S("ve1"), m + 1)
                pool.tensor_tensor(rs1, deg[0], mem.minus_half, ALU.pow).then_inc(S("rstd1"), 1)
                wait_apart(pool, S("aggr2"), m + 1, S("waited_pool"))
                pool.tensor_scalar(deg[1], mv2[:, 1:2], 4.0, EPS, ALU.mult, ALU.add).then_inc(S("ve2"), 1)
                pool.wait_ge(S("ve2"), m + 1)
                pool.tensor_tensor(deg[2], deg[1], mem.minus_half, ALU.pow).then_inc(S("pw2"), 1)
                wait_apart(pool, S("pw2"), m + 1, S("waited_pool"))
                pool.tensor_scalar(rs2, deg[2], 2.0, None, ALU.mult).then_inc(S("rstd2"), 1)

        @block.scalar
        def _(act):
            def m_high(k, b, src, n):
                act.wait_ge(S("m_sum"), n)
                act.wait_ge(S("m_free"), n)
                act.activation(mpair[b][:, 0, :], src[:, 0, :], ACT.Copy, scale=S64).then_inc(S("m_high"), 1)

            def z_high(k, b, n, xn):
                act.wait_ge(S(f"x_in{b}"), xn)
                act.wait_ge(S("m_free"), n)
                act.activation(zpair[b][:, 0, :], xbuf[b], ACT.Copy, scale=dz[:, ds(k, 1)]).then_inc(S("z_high"), 1)

            def rows_first(k, b4):
                c, b = ds(k, 1), b4 % 2
                act.wait_ge(S(f"rows_in{b}"), (k - b) * 16 + 32)
                act.activation(rows[b][:, 1, :], rows[b][:, 1, :], ACT.Copy, scale=SUMS, accum_out=sum_t[:, c])
                act.activation(rows[b][:, 0, :], rows[b][:, 0, :], ACT.Copy, scale=SUMS,
                               accum_out=sum_a[:, c]).then_inc(S("sums_at"), 1)
                act.wait_ge(S(f"rows0_in{b4}"), (k - b4) * 8 + 32)
                act.activation(regions(0, 0, k), blocks(rows0[b4][:, 1, :]), ACT.Copy, scale=S64).then_inc(S("t_high"), 1)
                m_high(k, b, rows0[b4], k + 1)
                act.wait_ge(S("dz"), k + 1)
                z_high(k, b, k + 1, (k - b) * 8 + 16)

            act.sem_inc(S("m_free"), 2)
            act.sem_inc(S("sums_at"), 2)
            rows_first(0, 0)
            with fours(act, 1, T - 3) as k:
                for j in range(4):
                    rows_first(k + j, (1 + j) % 4)
            for k in range(T - 3, T):
                rows_first(k, k % 4)

            def u_high(half):
                def one(j):
                    if j < HT - 1:
                        act.wait_ge(S("sweep_done"), half * (HT - 1) + j + 1)
                    else:
                        act.wait_ge(S("m_free"), (half + 1) * T + 2)
                    act.activation(u[:, 0, HT * half + j, :], psum[:, j, :], ACT.Copy,
                                   scale=dm[:, HT * half + j:HT * half + j + 1]).then_inc(S("u_high"), 1)
                act.wait_ge(S("dm"), 1)
                for j in range(HT):
                    one(j)

            def t_high(k, b4):
                act.wait_ge(S(rows2_in[b4]), rows2_count(k, b4))
                act.activation(regions(0, 1, k), blocks(rows2[b4][:, 1, :]), ACT.Copy, scale=S64).then_inc(S("t_high"), 1)

            def m_and_z(k, b4):
                z_high(k, b4 % 2, k + T + 1, (k - b4 % 2) * 8 + 16 * (T // 2) + 16)
                m_high(k, b4 % 2, rows2[b4], k + T + 1)

            t_high(0, 0)
            m_and_z(0, 0)
            t_high(1, 1)
            u_high(0)
            m_and_z(1, 1)
            for k in (2, 3):
                t_high(k, k)
                m_and_z(k, k)
            with fours(act, 4, T) as k:
                for b in range(4):
                    t_high(k + b, b)
                    m_and_z(k + b, b)
            u_high(1)

            def ones(m):
                for h in range(2):
                    act.activation(psum[:, 6:8, :].rearrange("p a b -> p (a b)"),
                                   big[:, ds(m, 1), HALF * h:HALF * (h + 1)].rearrange("p a b -> p (a b)"), ACT.Sign,
                                   bias=below_one, accum_out=ones_seen[:, ds(m + h * T, 1)]).then_inc(S("ones"), 1)
                    act.wait_ge(S("ones"), m * 2 + (h + 1))

            def qT_out(m, b):
                act.wait_ge(S("qT_psum"), m + 3)
                act.wait_ge(S("sup_psum"), m + 1)
                act.activation(qT[b], mem.bank16(2 + b), ACT.Copy).then_inc(S("qT_made"), 1)

            act.wait_ge(S("u_low"), T)
            ones(0)
            ones(1)
            with pairs(act, 2, T) as m:
                for b in range(2):
                    ones(m + b)
                    qT_out(m + b - 2, b)
            act.wait_ge(S("au_done"), T)
            load_weights(act, mem, a)
            qT_out(T - 2, 0)
            act.wait_ge(S("q_made"), T)
            weights_high(act, mem, 48)
            qT_out(T - 1, 1)

        @block.vector
        def _(dve):
            dve.sem_inc(S("rows0_free"), 4)
            dve.sem_inc(S("x_free"), 2)
            dve.sem_inc(S("qT_psum"), 2)
            dve.sem_inc(S("sup_psum"), 2)
            dve.sem_inc(S("sup_free"), 2)
            dve.sem_inc(S("au_free"), 2)
            for b in range(2):
                dve.sem_inc(S(f"x1_kept{b}"), 16)
                dve.sem_inc(S(f"x2_kept{b}"), 16)
            step = [0]

            def chained(ins):
                step[0] += 1
                ins.then_inc(S("w_chain"), 1)
                dve.wait_ge(S("w_chain"), step[0])

            act_alpha, wgt_alpha, act_alpha2, adj_scale = (mem.scal[:, i:i + 1] for i in range(4))

            def quantise_weight():
                dve.wait_ge(S("scalars_in"), 16)
                dve.wait_ge(S("w_in"), 16)
                for k in range(K4):
                    last = dve.bn_stats(wstats[:, 6 * k:6 * k + 6], wraw[:, k, :])
                chained(last)
                chained(dve.bn_aggr(wmv, wstats))
                dve.engine_nop().then_inc(S("w_part_mean"), 1)
                dve.wait_ge(S("w_mean"), 1)
                chained(dve.tensor_copy(wmean, psum[:, 5, 0:1]))
                chained(dve.tensor_tensor(wtmp[0], wmv[:, 0:1], wmean, ALU.subtract))
                chained(dve.tensor_tensor(wtmp[1], wtmp[0], wtmp[0], ALU.mult))
                dve.tensor_tensor(wtmp[3], wtmp[1], wmv[:, 1:2], ALU.add).then_inc(S("w_part_var"), 1)
                dve.wait_ge(S("w_pvar"), 1)
                dve.tensor_scalar(wvar, psum[:, 5, 1:2], D * D / (D * D - 1.0), None, ALU.mult).then_inc(S("w_var"), 1)
                chained(dve.reciprocal(wtmp[1], wgt_alpha))
                dve.wait_ge(S("w_rstd"), 1)
                chained(dve.tensor_tensor(wscale, wtmp[2], wtmp[1], ALU.mult))
                chained(dve.tensor_scalar(wraw, wraw, wmean, wscale, ALU.subtract, ALU.mult))
                chained(dve.tensor_scalar(wraw, wraw, 1.0, -1.0, ALU.min, ALU.max))
                chained(dve.tensor_scalar(wraw, wraw, WGT_STEPS, MAGIC, ALU.mult, ALU.add))
                dve.tensor_scalar(wq8, wraw, MAGIC, None, ALU.subtract).then_inc(S("wq8"), 1)
                dve.wait_ge(S("wq8"), 1)

            def constants():
                chained(dve.reciprocal(r_act, act_alpha))
                chained(dve.reciprocal(wtmp[1], act_alpha2))
                chained(dve.tensor_scalar(wtmp[0], act_alpha, 1.0 / ACT_STEPS, 1.0 / WGT_STEPS, ALU.mult, ALU.mult))
                chained(dve.tensor_tensor(wtmp[2], wtmp[0], wgt_alpha, ALU.mult))
                chained(dve.tensor_tensor(c_sup, wtmp[2], wtmp[1], ALU.mult))
                chained(dve.reciprocal(wtmp[0], adj_scale))
                chained(dve.tensor_tensor(wtmp[1], wtmp[0], adj_scale, ALU.mult))
                chained(dve.tensor_tensor(wtmp[2], wtmp[1], act_alpha2, ALU.mult))
                chained(dve.tensor_scalar(mem.f_out, wtmp[2], 1.0 / (ACT_STEPS * S64), None, ALU.mult))

            def m_rows(k, b, r, n, diag, accum):
                if accum:
                    dve.scalar_tensor_tensor(r[:, 0, :], r[:, 0, :], 1.0, r[:, 1, :], ALU.mult, ALU.add,
                                             accum_out=sum_m[:, ds(k, 1)]).then_inc(S("sum_m"), 1)
                else:
                    dve.tensor_tensor(r[:, 0, :], r[:, 0, :], r[:, 1, :], ALU.add).then_inc(S("sum_m"), 1)
                dve.wait_ge(S("sum_m"), n)
                if diag is not None:
                    d = r[:, 0, ds(diag * P, P)]
                    dve.scalar_tensor_tensor(d, ident[:], 2.0, d, ALU.mult, ALU.add).then_inc(S("m_sum"), 1)
                else:
                    dve.sem_inc(S("m_sum"), 1)

            def m_low(k, b, r, n):
                dve.wait_ge(S("m_high"), n)
                dve.wait_ge(S("m_sum"), n)
                dve.scalar_tensor_tensor(mpair[b][:, 1, :], r[:, 0, :], S64, mpair[b][:, 0, :],
                                         ALU.mult, ALU.subtract).then_inc(S("m_low"), 1)

            def z_low(k, b, n):
                dve.wait_ge(S("z_high"), n)
                dve.scalar_tensor_tensor(zpair[b][:, 1, :], xbuf[b], dz[:, ds(k, 1)], zpair[b][:, 0, :],
                                         ALU.mult, ALU.subtract).then_inc(S("z_low"), 1)

            def z_ready(k, b, n):
                z_low(k, b, n)
                dve.wait_ge(S("z_low"), n)
                dve.sem_inc(S("x_free"), 1)

            def t_low(k, half, r):
                dve.scalar_tensor_tensor(regions(1, half, k), blocks(r[:, 1, :]), S64, regions(0, half, k),
                                         ALU.mult, ALU.subtract).then_inc(S("t_low"), 1)

            def rows_first(k, b4, diag):
                b, r0 = b4 % 2, rows0[b4]
                dve.wait_ge(S(f"rows0_in{b4}"), (k - b4) * 8 + 32)
                m_rows(k, b, r0, k + 1, diag, True)
                dve.wait_ge(S("t_high"), k + 1)
                t_low(k, 0, r0)
                m_low(k, b, r0, k + 1)
                dve.wait_ge(S("m_low"), k + 1)
                dve.wait_ge(S("t_low"), k + 1)
                dve.sem_inc(S("rows0_free"), 1)
                z_ready(k, b, k + 1)

            dve.wait_ge(S("setup"), 7)
            with fours(dve, 0, HT) as k:
                for b in range(4):
                    rows_first(k + b, b, k + b)
            with fours(dve, HT, T) as k:
                for b in range(4):
                    rows_first(k + b, b, None)

            def u_low(half):
                for j in range(HT):
                    i = HT * half + j
                    dve.wait_ge(S("u_high"), i + 1)
                    dve.scalar_tensor_tensor(u[:, 1, i, :], psum[:, j, :], dm[:, i:i + 1], u[:, 0, i, :],
                                             ALU.mult, ALU.subtract).then_inc(S("u_low"), 1)

            def gather_second(k, b4, diag):
                dve.wait_ge(S(rows2_in[b4]), rows2_count(k, b4))
                m_rows(k, b4 % 2, rows2[b4], k + T + 1, diag, False)

            def t_second(k, b4):
                dve.wait_ge(S("t_high"), k + T + 1)
                t_low(k, 1, rows2[b4])

            def m_second(k, b4):
                m_low(k, b4 % 2, rows2[b4], k + T + 1)
                dve.wait_ge(S("m_low"), k + T + 1)
                dve.wait_ge(S("t_low"), k + T + 1)
                dve.sem_inc(S("rows_free"), 1)

            def rows_second(k, b4, diag):
                gather_second(k, b4, diag)
                t_second(k, b4)
                z_ready(k, b4 % 2, k + T + 1)
                m_second(k, b4)

            for k in range(2):
                gather_second(k, k, None)
                z_ready(k, k, T + k + 1)
                m_low(k, k, rows2[k], T + k + 1)
                if k == 0:
                    u_low(0)
            for k in range(2):
                t_second(k, k)
                dve.wait_ge(S("m_low"), T + k + 1)
                dve.wait_ge(S("t_low"), T + k + 1)
                dve.sem_inc(S("rows_free"), 1)
            rows_second(2, 2, None)
            rows_second(3, 3, None)
            with fours(dve, 4, HT) as k:
                for b in range(4):
                    rows_second(k + b, b, None)
            with fours(dve, HT, T) as k:
                for b in range(4):
                    rows_second(k + b, b, k + b - HT)
            u_low(1)
            quantise_weight()
            constants()

            def normed(m, b):
                n = m + 1
                dve.wait_ge(S("au_done"), n)
                dve.wait_ge(S(f"x_in{b}"), (m - b) * 8 + 16 * T + 16)
                dve.scalar_tensor_tensor(hbuf, psum[:, b, :], 1.0 / (S64 * S64), xbuf[b], ALU.mult,
                                         ALU.add).then_inc(S("h1"), 1)
                dve.wait_ge(S("h1"), n)
                dve.sem_inc(S("x_free"), 1)
                dve.sem_inc(S("au_free"), 1)
                dve.bn_stats(stats, hbuf).then_inc(S("stats1"), 1)
                wait_apart(dve, S("stats1"), n, S("waited_dve"))
                dve.bn_aggr(mv, stats).then_inc(S("aggr1"), 1)
                dve.scalar_tensor_tensor(sbuf2[:, 0:P], big[:, ds(m, 1), ds(m * P, P)].rearrange("p a b -> p (a b)"),
                                         S64, ident[:], ALU.is_ge, ALU.mult,
                                         accum_out=ones_diag[:, ds(m, 1)]).then_inc(S("ones_diag"), 1)
                dve.wait_ge(S("ones_diag"), n)
                dve.wait_ge(S("rstd1"), n)
                dve.wait_ge(S(f"x1_kept{b}"), (m - b) * 8 + 16)
                dve.tensor_scalar(x1buf[b], hbuf, mv[:, 0:1], rs1, ALU.subtract, ALU.mult).then_inc(S("x1_made"), 1)
                dve.wait_ge(S("x1_made"), n)
                dve.bn_stats(stats, x1buf[b]).then_inc(S("stats2"), 1)
                wait_apart(dve, S("stats2"), n, S("waited_dve"))
                dve.bn_aggr(mv2, stats).then_inc(S("aggr2"), 1)

            def quantised(m, b):
                n = m + 1
                dve.wait_ge(S("rstd2"), n)
                dve.wait_ge(S(f"x2_kept{b}"), (m - b) * 8 + 16)
                dve.tensor_scalar(x2buf[b], x1buf[b], mv2[:, 0:1], rs2, ALU.subtract, ALU.mult).then_inc(S("x2_made"), 1)
                dve.wait_ge(S("x2_made"), n)
                dve.tensor_scalar(qbuf, x2buf[b], r_act, 1.0, ALU.mult, ALU.min).then_inc(S("q_a"), 1)
                dve.wait_ge(S("q_a"), n)
                dve.tensor_scalar(qbuf, qbuf, ACT_STEPS, MAGIC, ALU.mult, ALU.add).then_inc(S("q_b"), 1)
                dve.wait_ge(S("q_b"), n)
                dve.wait_ge(S("qT_psum"), n)
                dve.tensor_scalar(qpair[b][:, 0, :], qbuf, MAGIC, None, ALU.subtract).then_inc(S("q_c"), 1)
                dve.wait_ge(S("q_c"), n)
                dve.scalar_tensor_tensor(qpair[b][:, 1, :], qbuf, MAGIC, qpair[b][:, 0, :], ALU.subtract,
                                         ALU.subtract).then_inc(S("q_made"), 1)

            def support(m, b):
                n = m + 1
                dve.wait_ge(S("sup_psum"), n + 2)
                dve.tensor_scalar(sbuf2, psum[:, 4 + b, :], c_sup, 0.0, ALU.mult, ALU.max).then_inc(S("s_a"), 1)
                dve.wait_ge(S("s_a"), n)
                dve.sem_inc(S("sup_free"), 1)
                dve.tensor_scalar(sbuf2, sbuf2, 1.0, ACT_STEPS, ALU.min, ALU.mult).then_inc(S("s_b"), 1)
                dve.wait_ge(S("s_b"), n)
                dve.tensor_scalar(sup[:, ds(m, 1), :].rearrange("p a b -> p (a b)"), sbuf2, MAGIC, MAGIC, ALU.add,
                                  ALU.subtract).then_inc(S("sup_made"), 1)
                dve.wait_ge(S("sup_made"), n)

            normed(0, 0)
            quantised(0, 0)
            normed(1, 1)
            quantised(1, 1)
            with pairs(dve, 2, T) as m:
                for b in range(2):
                    normed(m + b, b)
                    support(m + b - 2, b)
                    quantised(m + b, b)
            dve.wait_ge(S("ones"), 2 * T)
            dve.reduce_sum(ones_tmp[:, 0:1], ones_seen, axis=AX.X).then_inc(S("ones_sums"), 1)
            dve.reduce_sum(ones_tmp[:, 1:2], ones_diag, axis=AX.X).then_inc(S("ones_sums"), 1)
            dve.wait_ge(S("ones_sums"), 2)
            dve.tensor_scalar(ones_tmp[:, 3:4], ones_tmp[:, 0:1], 0.5, 0.5 * T * N, ALU.mult, ALU.add)\
                .then_inc(S("ones_sums"), 1)
            dve.wait_ge(S("ones_sums"), 3)
            dve.tensor_tensor(ones_tmp[:, 2:3], ones_tmp[:, 3:4], ones_tmp[:, 1:2], ALU.subtract)\
                .then_inc(S("ones_row"), 1)
            support(T - 2, 0)
            weights_low(dve, mem, 0)
            dve.wait_ge(S("ones_all"), 1)
            dve.tensor_scalar(flag[0:1, 0:1], psum[0:1, 7, 0:1], float(P), None, ALU.mult).then_inc(S("flag"), 1)
            support(T - 1, 1)
            dve.wait_ge(S("flag"), 1)

        @block.tensor
        def _(pe):
            def sweep(half):
                def body(k, b, start=False, stop=False):
                    n = k + (T * half + 1)
                    pe.wait_ge(S("m_low"), n)
                    pe.wait_ge(S("z_low"), n)
                    for j in range(HT):
                        if start and half:
                            pe.wait_ge(S("u_low"), j + 1)
                        high, low = (mpair[b][:, h, j * P:(j + 1) * P] for h in range(2))
                        pe.matmul(psum[:, j, :], high, zpair[b][:, 0, :], start=start, stop=False)
                        pe.matmul(psum[:, j, :], high, zpair[b][:, 1, :], start=False, stop=False)
                        last = pe.matmul(psum[:, j, :], low, zpair[b][:, 0, :], start=False, stop=stop)
                        if stop and j < HT - 1:
                            last.then_inc(S("sweep_done"), 1)
                    last.then_inc(S("m_free"), 1)

                body(0, 0, start=True)
                body(1, 1)
                with pairs(pe, 2, T - 2) as k:
                    for b in range(2):
                        body(k + b, b)
                body(T - 2, 0)
                body(T - 1, 1, stop=True)
            sweep(0)
            sweep(1)

            def transposes(m, b):
                pe.wait_ge(S("q_made"), m + 1)
                for h in range(2):
                    for k in range(K4):
                        last = pe.transpose(mem.bank16(2 + b)[:, h * K4 + k, :], qpair[b][:, h, k * P:(k + 1) * P],
                                            ident[:])
                last.then_inc(S("qT_psum"), 1)

            def au(m, b, prev, first=False):
                pe.wait_ge(S("au_free"), m + 1)
                for k in range(T):
                    if first:
                        pe.wait_ge(S("u_low"), k + 1 if k >= b + 1 else HT + b + 1)
                    if k == T // 2 and prev:
                        transposes(m - 2, b)
                    if first and k == T // 2:
                        pe.wait_ge(S("w_part_mean"), 1)
                        pe.matmul(psum[:, 5, 0:1], mem.mean_matrix[:], wmv[:, 0:1], start=True,
                                  stop=True).then_inc(S("w_mean"), 1)
                    if first and k == T - 3:
                        pe.wait_ge(S("w_part_var"), 1)
                        pe.matmul(psum[:, 5, 1:2], mem.mean_matrix[:], wtmp[3], start=True,
                                  stop=True).then_inc(S("w_pvar"), 1)
                    high, low = (big[:, ds(m, 1), (h * T + k) * P:(h * T + k + 1) * P].rearrange("p a b -> p (a b)")
                                 for h in range(2))
                    pe.matmul(psum[:, b, :], high, u[:, 0, k, :], start=(k == 0), stop=False, skip_group_check=True)
                    pe.matmul(psum[:, b, :], high, u[:, 1, k, :], start=False, stop=False, skip_group_check=True)
                    last = pe.matmul(psum[:, b, :], low, u[:, 0, k, :], start=False, stop=(k == T - 1),
                                     skip_group_check=True)
                last.then_inc(S("au_done"), 1)

            def support(m, b):
                pe.wait_ge(S("qT_made"), m + 1)
                pe.wait_ge(S("sup_free"), m + 1)
                for h in range(2):
                    for k in range(K4):
                        last = pe.matmul(psum[:, 4 + b, :], qT[b][:, h * K4 + k, :], wq8[:, k, :],
                                         start=(h == 0 and k == 0), stop=(h == 1 and k == K4 - 1))
                last.then_inc(S("sup_psum"), 1)

            pe.wait_ge(S("u_low"), HT + 6)
            au(0, 0, False, first=True)
            au(1, 1, False)
            pe.wait_ge(S("wq8"), 1)
            with pairs(pe, 2, T) as m:
                for b in range(2):
                    au(m + b, b, True)
                    support(m + b - 2, b)
            transposes(T - 2, 0)
            pe.wait_ge(S("sup_made"), T - 3)
            pe.wait_ge(S("au_free"), T + 1)
            convolve(pe, mem, 0, 0, range(T - 3))
            support(T - 2, 0)
            pe.wait_ge(S("sup_made"), T - 2)
            convolve(pe, mem, 0, 0, range(T - 3, T - 2))
            pe.wait_ge(S("au_free"), T + 2)
            convolve(pe, mem, 1, 1, range(T - 2))
            pe.wait_ge(S("ones_row"), 1)
            pe.matmul(psum[0:1, 7, 0:1], ones_tmp[:, 2:3], mem.mean_matrix[:, 0:1], start=True,
                      stop=True).then_inc(S("ones_all"), 1)
            transposes(T - 1, 1)
            pe.wait_ge(S("sup_made"), T - 1)
            for m in range(2):
                convolve(pe, mem, m, m, range(T - 2, T - 1))
            support(T - 1, 1)
    return r_act, c_sup


def relation_attention(nc, mem, a, x1_dram, x2_dram, r_act, c_sup):
    big, psum, ident, S, carve = mem.big, mem.psum, mem.ident, mem.sem, mem.carve
    floats = big[:].rearrange("p a b -> p (a b)").bitcast(FP32)

    def room(at, dims):
        v = floats[:, at:at + int(np.prod(dims))]
        return v.rearrange("p (a b) -> p a b", a=dims[0]) if len(dims) > 1 else v

    x1 = room(0, [T, D])
    x1T = room(T * D, [K4, N])
    related, masked, score, shares = (room(T * D + N * i, [N]) for i in range(4))
    q, k_ = room(2 * T * D, [K4, N]), room(3 * T * D, [K4, N])
    w = [carve(8192 * i, [K4, D], FP32) for i in range(2)]
    iota = carve(0, [N], FP32)
    edge_one, node_one = carve(8192, [N], FP16), carve(12288, [P], FP16)
    q_tile = carve(12544, [K4, P], FP32)
    sharesT = carve(14592, [T, P], FP32)
    edges, edges_f = carve(22784, [2 * ET], FP32).bitcast(INT32), carve(24064, [2 * ET], FP32)
    ident_f, not_ident = carve(25344, [P], FP32), carve(25856, [P], FP32)
    biases = carve(26368, [2 * K4], FP32)
    hbuf, qbuf = carve(49152, [D], FP32), carve(51200, [D], FP32)
    qpair, qT, sbuf = carve(53248, [2, D], FP16), carve(55296, [2 * K4, P], FP16), carve(57344, [D], FP32)
    x2buf = carve(59392, [D], FP32)
    sup = mem.sup
    wq8 = carve(65536, [K4, D], FP16)
    rows = carve(0, [N], FP32)
    top, total, inv, stats, mv, ve, rstd = (mem.relation_cols[:, i:j] for i, j in
                                            ((0, 1), (1, 2), (2, 3), (3, 9), (9, 11), (11, 12), (12, 13)))

    EDGE, MASKS, HEAD, AFTER = 2, 2 + 3 * ET, 8 + 3 * ET, 8 + 3 * ET + 9 * HEADS
    TILE = AFTER + 20
    START = 9
    END = START + T * TILE

    def at(i, step):
        return i * TILE + (START + step)

    with nc.Block() as block:
        @block.sync
        def _(sp):
            sp.wait_ge(S("weights_in"), 48)
            loads = [(x1, x1_dram.rearrange("(t p) d -> p t d", p=P)),
                     (w[0], a["L1_wqT"].rearrange("(k p) d -> p k d", p=P)),
                     (w[1], a["L1_wkT"].rearrange("(k p) d -> p k d", p=P)),
                     (biases[:, 0:K4], a["L1_bq"]), (biases[:, K4:2 * K4], a["L1_bk"]), (edges, a["edges"])]
            for dst, src in loads:
                sp.dma_start(dst, src).then_inc(S("relation_in"), 16)
            sp.wait_ge(S("relation_in"), 16 * len(loads))
            sp.sem_inc(S("turn"), 1)
            sp.wait_ge(S("turn"), 8)
            sp.dma_start(iota, a["iota"]).then_inc(S("relation_in"), 16)
            sp.wait_ge(S("relation_in"), 16 * len(loads) + 16)
            sp.sem_inc(S("turn"), 1)
            with sp.Fori(0, T) as i:
                r = ds(i * P, P)
                sp.wait_ge(S("turn"), at(i, 0))
                sp.dma_start(masked, a["adj"][r, :]).then_inc(S("relation_adj"), 16)
                sp.wait_ge(S("relation_adj"), i * 16 + 16)
                sp.sem_inc(S("turn"), 1)
                sp.wait_ge(S("turn"), at(i, AFTER + 9))
                sp.dma_start(x2_dram[r, :], x2buf).then_inc(S("relation_x2"), 16)
                sp.wait_ge(S("relation_x2"), i * 16 + 16)
                sp.sem_inc(S("turn"), 1)
            with sp.Fori(0, T) as k:
                sp.wait_ge(S("turn"), k * 3 + END)
                sp.dma_start(rows, a["adjT"][ds(k * P, P), :]).then_inc(S("relation_rows"), 16)
                sp.wait_ge(S("relation_rows"), k * 16 + 16)
                sp.sem_inc(S("turn"), 1)
            sp.wait_ge(S("turn"), END + 3 * T)
            load_weights(sp, mem, a)
            sp.wait_ge(S("weights_in"), 96)

        @block.gpsimd
        def _(pool):
            with pool.Fori(0, T) as i:
                wait_apart(pool, S("turn"), at(i, AFTER + 6), S("waited_pool"))
                pool.tensor_scalar(ve, mv[:, 1:2], EPS, None, ALU.add).then_inc(S("turn"), 1)
                pool.wait_ge(S("turn"), at(i, AFTER + 7))
                pool.tensor_tensor(rstd, ve, mem.minus_half, ALU.pow).then_inc(S("turn"), 1)

        @block.scalar
        def _(act):
            act.wait_ge(S("turn"), 5)
            for k in range(K4):
                for b in range(2):
                    act.wait_ge(S("relation_x1T"), 2 * k + b + 1)
                    last = act.activation(x1T[:, k, HALF * b:HALF * (b + 1)],
                                          psum[:, 2 * b:2 * b + 2, :].rearrange("p a b -> p (a b)"), ACT.Copy)
                    last.then_inc(S("relation_x1T_out"), 1)
            act.wait_ge(S("relation_x1T_out"), 2 * K4)
            act.sem_inc(S("turn"), 1)
            with act.Fori(0, T) as i:
                for h in range(HEADS):
                    act.wait_ge(S("turn"), at(i, HEAD + 9 * h + 5))
                    act.activation(score, score, ACT.Exp, bias=top, accum_out=total).then_inc(S("turn"), 1)
                act.wait_ge(S("turn"), at(i, AFTER + 1))
                act.activation(sharesT.rearrange("p a b -> p (a b)"),
                               psum[:, 4:8, :].rearrange("p a b -> p (a b)"), ACT.Copy).then_inc(S("turn"), 1)
                act.wait_ge(S("turn"), at(i, AFTER + 15))
                act.activation(qT, mem.bank16(2), ACT.Copy).then_inc(S("turn"), 1)
            with act.Fori(0, T) as k:
                act.wait_ge(S("turn"), k * 3 + (END + 1))
                act.activation(big[:, :, ds(k * P, P)], rows.rearrange("p (a b) -> p a b", b=P), ACT.Copy,
                               scale=S64).then_inc(S("turn"), 1)
            weights_high(act, mem, 96)

        @block.vector
        def _(dve):
            dve.wait_ge(S("turn"), 1)
            dve.tensor_copy(edges_f, edges).then_inc(S("turn"), 1)
            dve.tensor_copy(ident_f, ident[:]).then_inc(S("turn"), 1)
            dve.wait_ge(S("turn"), 3)
            dve.tensor_scalar(not_ident, ident_f, -1.0, 1.0, ALU.mult, ALU.add).then_inc(S("turn"), 1)
            dve.wait_ge(S("turn"), 4)
            dve.sem_inc(S("turn"), 1)
            for n in range(2 * K4 * 4):
                side, d, c = n // (K4 * 4), n // 4 % K4, n % 4
                dve.wait_ge(S("relation_qk"), n + 1)
                dve.tensor_scalar((q, k_)[side][:, d, c * 512:(c + 1) * 512], psum[:, 4 + n % 4, :],
                                  biases[:, side * K4 + d:side * K4 + d + 1], None, ALU.add)\
                    .then_inc(S("relation_qk_out"), 1)
            dve.wait_ge(S("relation_qk_out"), 8 * K4)
            dve.sem_inc(S("turn"), 1)
            dve.sem_inc(S("turn"), 1)
            with dve.Fori(0, T) as i:
                diag = ds(i * P, P)
                dve.wait_ge(S("turn"), at(i, 1))
                dve.tensor_copy(q_tile, q[:, :, diag]).then_inc(S("turn"), 1)
                with dve.Fori(0, ET) as e:
                    dve.wait_ge(S("turn"), i * TILE + e * 3 + (START + EDGE))
                    dve.tensor_scalar(node_one, iota[:, diag], edges_f[:, ds(e, 1)], None, ALU.is_equal)\
                        .then_inc(S("turn"), 1)
                    dve.tensor_scalar(edge_one, iota, edges_f[:, ds(e + ET, 1)], None, ALU.is_equal)\
                        .then_inc(S("turn"), 1)
                dve.wait_ge(S("turn"), at(i, MASKS))
                dve.tensor_scalar(related, psum[:, 0:4, :].rearrange("p a b -> p (a b)"), 1.0, float(DK) ** -0.5,
                                  ALU.min, ALU.mult).then_inc(S("turn"), 1)
                dve.wait_ge(S("turn"), at(i, MASKS + 1))
                dve.tensor_tensor(related[:, diag], related[:, diag], not_ident, ALU.mult).then_inc(S("turn"), 1)
                dve.tensor_scalar(masked, masked, 1.0, 3.0e38, ALU.is_equal, ALU.mult).then_inc(S("turn"), 1)
                dve.wait_ge(S("turn"), at(i, MASKS + 3))
                dve.tensor_scalar(masked, masked, 3.0e38, None, ALU.subtract).then_inc(S("turn"), 1)
                dve.wait_ge(S("turn"), at(i, MASKS + 4))
                dve.tensor_tensor(masked[:, diag], masked[:, diag], not_ident, ALU.mult).then_inc(S("turn"), 1)
                dve.wait_ge(S("turn"), at(i, MASKS + 5))
                dve.scalar_tensor_tensor(masked[:, diag], ident_f, 1e-7, masked[:, diag], ALU.mult, ALU.add)\
                    .then_inc(S("turn"), 1)
                for h in range(HEADS):
                    first = HEAD + 9 * h
                    dve.wait_ge(S("turn"), at(i, first + 1))
                    dve.tensor_tensor(score, psum[:, 0:4, :].rearrange("p a b -> p (a b)"), related, ALU.mult)\
                        .then_inc(S("turn"), 1)
                    dve.wait_ge(S("turn"), at(i, first + 2))
                    dve.tensor_tensor(score, score, masked, ALU.add).then_inc(S("turn"), 1)
                    dve.wait_ge(S("turn"), at(i, first + 3))
                    dve.tensor_reduce(inv, score, axis=AX.X, op=ALU.max).then_inc(S("turn"), 1)
                    dve.wait_ge(S("turn"), at(i, first + 4))
                    dve.tensor_scalar(top, inv, -1.0, None, ALU.mult).then_inc(S("turn"), 1)
                    dve.wait_ge(S("turn"), at(i, first + 6))
                    dve.reciprocal(inv, total).then_inc(S("turn"), 1)
                    dve.wait_ge(S("turn"), at(i, first + 7))
                    dve.tensor_scalar(ve, inv, 1.0 / HEADS, None, ALU.mult).then_inc(S("turn"), 1)
                    dve.wait_ge(S("turn"), at(i, first + 8))
                    if h == 0:
                        dve.tensor_scalar(shares, score, ve, None, ALU.mult).then_inc(S("turn"), 1)
                    else:
                        dve.scalar_tensor_tensor(shares, score, ve, shares, ALU.mult, ALU.add).then_inc(S("turn"), 1)
                dve.wait_ge(S("turn"), at(i, AFTER + 3))
                dve.tensor_tensor(hbuf, psum[:, 0, :], x1[:, ds(i, 1), :].rearrange("p a b -> p (a b)"), ALU.add)\
                    .then_inc(S("turn"), 1)
                dve.wait_ge(S("turn"), at(i, AFTER + 4))
                dve.bn_stats(stats, hbuf).then_inc(S("turn"), 1)
                wait_apart(dve, S("turn"), at(i, AFTER + 5), S("waited_dve"))
                dve.bn_aggr(mv, stats).then_inc(S("turn"), 1)
                dve.wait_ge(S("turn"), at(i, AFTER + 8))
                dve.tensor_scalar(x2buf, hbuf, mv[:, 0:1], rstd, ALU.subtract, ALU.mult).then_inc(S("turn"), 1)
                dve.wait_ge(S("turn"), at(i, AFTER + 10))
                dve.tensor_scalar(qbuf, x2buf, r_act, 1.0, ALU.mult, ALU.min).then_inc(S("turn"), 1)
                dve.wait_ge(S("turn"), at(i, AFTER + 11))
                dve.tensor_scalar(qbuf, qbuf, ACT_STEPS, MAGIC, ALU.mult, ALU.add).then_inc(S("turn"), 1)
                dve.wait_ge(S("turn"), at(i, AFTER + 12))
                dve.tensor_scalar(qpair[:, 0, :], qbuf, MAGIC, None, ALU.subtract).then_inc(S("turn"), 1)
                dve.wait_ge(S("turn"), at(i, AFTER + 13))
                dve.scalar_tensor_tensor(qpair[:, 1, :], qbuf, MAGIC, qpair[:, 0, :], ALU.subtract, ALU.subtract)\
                    .then_inc(S("turn"), 1)
                dve.wait_ge(S("turn"), at(i, AFTER + 17))
                dve.tensor_scalar(sbuf, psum[:, 4, :], c_sup, 0.0, ALU.mult, ALU.max).then_inc(S("turn"), 1)
                dve.wait_ge(S("turn"), at(i, AFTER + 18))
                dve.tensor_scalar(sbuf, sbuf, 1.0, ACT_STEPS, ALU.min, ALU.mult).then_inc(S("turn"), 1)
                dve.wait_ge(S("turn"), at(i, AFTER + 19))
                dve.tensor_scalar(sup[:, ds(i, 1), :].rearrange("p a b -> p (a b)"), sbuf, MAGIC, MAGIC, ALU.add,
                                  ALU.subtract).then_inc(S("turn"), 1)
            with dve.Fori(0, T) as k:
                dve.wait_ge(S("turn"), k * 3 + (END + 2))
                dve.scalar_tensor_tensor(big[:, :, ds(k * P + N, P)], rows.rearrange("p (a b) -> p a b", b=P), S64,
                                         big[:, :, ds(k * P, P)], ALU.mult, ALU.subtract).then_inc(S("turn"), 1)
            weights_low(dve, mem, 2)

        @block.tensor
        def _(pe):
            pe.wait_ge(S("turn"), 5)
            for k in range(K4):
                for b in range(2):
                    if k:
                        pe.wait_ge(S("relation_x1T_out"), 2 * (k - 1) + b + 1)
                    for t in range(HT):
                        last = pe.transpose(psum[:, 2 * b + t // 4, t % 4 * P:(t % 4 + 1) * P],
                                            x1[:, HT * b + t, k * P:(k + 1) * P], ident_f)
                    last.then_inc(S("relation_x1T"), 1)
            pe.wait_ge(S("turn"), 6)
            for n in range(2 * K4 * 4):
                side, d, c = n // (K4 * 4), n // 4 % K4, n % 4
                if n >= 4:
                    pe.wait_ge(S("relation_qk_out"), n - 3)
                for k in range(K4):
                    last = pe.matmul(psum[:, 4 + n % 4, :], w[side][:, k, d * P:(d + 1) * P],
                                     x1T[:, k, c * 512:(c + 1) * 512], start=(k == 0), stop=(k == K4 - 1))
                last.then_inc(S("relation_qk"), 1)
            with pe.Fori(0, T) as i:
                def count(e, start=False, stop=False):
                    pe.wait_ge(S("turn"), i * TILE + e * 3 + (START + EDGE + 2))
                    for c in range(4):
                        last = pe.matmul(psum[:, c, :], node_one, edge_one[:, c * 512:(c + 1) * 512],
                                         start=start, stop=stop)
                    last.then_inc(S("turn"), 1)
                count(0, start=True)
                with pe.Fori(1, ET - 1) as e:
                    count(e)
                count(ET - 1, stop=True)
                for h in range(HEADS):
                    pe.wait_ge(S("turn"), at(i, HEAD + 9 * h))
                    r = slice(DK * (h % 2), DK * (h % 2) + DK)
                    for c in range(4):
                        last = pe.matmul(psum[:, c, :], q_tile[r, h // 2, :], k_[r, h // 2, c * 512:(c + 1) * 512],
                                         start=True, stop=True)
                    last.then_inc(S("turn"), 1)
                pe.wait_ge(S("turn"), at(i, AFTER))
                for t in range(T):
                    last = pe.transpose(psum[:, 4 + t // 4, t % 4 * P:(t % 4 + 1) * P], shares[:, t * P:(t + 1) * P],
                                        ident_f)
                last.then_inc(S("turn"), 1)
                pe.wait_ge(S("turn"), at(i, AFTER + 2))
                for t in range(T):
                    last = pe.matmul(psum[:, 0, :], sharesT[:, t, :], x1[:, t, :], start=(t == 0), stop=(t == T - 1))
                last.then_inc(S("turn"), 1)
                pe.wait_ge(S("turn"), at(i, AFTER + 14))
                for h in range(2):
                    for k in range(K4):
                        last = pe.transpose(mem.bank16(2)[:, h * K4 + k, :], qpair[:, h, k * P:(k + 1) * P], ident[:])
                last.then_inc(S("turn"), 1)
                pe.wait_ge(S("turn"), at(i, AFTER + 16))
                for h in range(2):
                    for k in range(K4):
                        last = pe.matmul(psum[:, 4, :], qT[:, h * K4 + k, :], wq8[:, k, :],
                                         start=(h == 0 and k == 0), stop=(h == 1 and k == K4 - 1))
                last.then_inc(S("turn"), 1)
            pe.wait_ge(S("turn"), END + 3 * T)
            for m in range(2):
                convolve(pe, mem, m, m, range(T - 1))


def attention(nc, mem, a, x2_dram, out):
    big, psum, ident, S, carve = mem.big, mem.psum, mem.ident, mem.sem, mem.carve
    x3 = carve(0, [T, D], FP32)
    sup = mem.sup
    wvt = mem.raw[2]
    (wq, wk) = mem.weight_pairs
    g = carve(49152, [2, K4, D], FP16)
    wv = carve(57344, [2, K4, D], FP16)
    x2in = [carve(65536 + 2048 * b, [D], FP32) for b in range(2)]
    hbuf = carve(69632, [D], FP32)
    x3pair = [carve(71680, [2, D], FP16), carve(75776, [2, D], FP16)]
    v_sum = carve(73728, [D], FP32)
    t_sum = [v_sum, hbuf]
    bk_wide = carve(73728, [2, K4, P], FP16)
    T_BANK = (6, 7, 0, 1)
    bv = carve(77824, [D], FP32)
    rows = [carve(32768 + 8192 * b, [N], FP32) for b in range(2)]
    mask = carve(49152, [N], FP16)
    ppair = [carve(53248 + 8192 * b, [2, N], FP16) for b in range(2)]
    attended = [carve(69632 + 2048 * b, [D], FP32) for b in range(2)]

    mem.at = 15
    col = mem.col
    biases = col(2 * K4)
    bias_high, bias_low = (col(K4).bitcast(FP16) for _ in range(2))
    gk, c0, tmpc = col(K4), col(), col(K4)
    ci, ci_part = col(T), col(T)
    biases64 = col(2 * K4)
    bqk_sum = col()
    stats, mv, ve, rstd = col(6), col(2), col(), col()
    top, bias, total, inv = col(2), col(2), col(2), col(2)

    def xT(tiles, part, k):
        return big[:, tiles, (part * K4 + k) * P:(part * K4 + k + 1) * P]

    def tT(tiles, part, k):
        return big[:, tiles, 1024 + (part * K4 + k) * P:1024 + (part * K4 + k + 1) * P]

    def value(tile, part):
        return big[:, tile, 2048 + part * D:2048 + (part + 1) * D].rearrange("p a b -> p (a b)")

    def pT(b, part, tiles):
        return big[:, tiles, 3072 + (2 * b + part) * P:3072 + (2 * b + part + 1) * P]

    with nc.Block() as block:
        @block.sync
        def _(sp):
            def load_x2(m, b):
                sp.wait_ge(S("x2_free"), m + 1)
                sp.dma_start(x2in[b], x2_dram[ds(m * P, P), :]).then_inc(S(f"x2_in{b}"), 16)

            sp.dma_start(biases[:, 0:K4], a["b_q"]).then_inc(S("biases_in"), 16)
            sp.dma_start(biases[:, K4:2 * K4], a["b_k"]).then_inc(S("biases_in"), 16)
            load_x2(0, 0)
            load_x2(1, 1)
            sp.dma_start(bv, a["b_v"].to_broadcast([P, D])).then_inc(S("bv_in"), 16)
            with pairs(sp, 2, T) as m:
                for b in range(2):
                    load_x2(m + b, b)
            sp.wait_ge(S("l3_psum"), T)
            with pairs(sp, 0, T) as i:
                for b in range(2):
                    sp.wait_ge(S("adj_free"), i + b + 1)
                    sp.dma_start(rows[b], a["adj"][ds((i + b) * P, P), :]).then_inc(S(f"adj_in{b}"), 16)
            with sp.Fori(0, T) as i:
                sp.wait_ge(S("out_made"), i + 1)
                sp.dma_start(out[ds(i * P, P), :], x3[:, ds(i, 1), :].rearrange("p a b -> p (a b)"))\
                    .then_inc(S("stored"), 16)
            sp.wait_ge(S("stored"), 16 * T)

        @block.gpsimd
        def _(pool):
            def inverse_deviation(n, made, ve_sem, rstd_sem):
                wait_apart(pool, S(made), n, S("waited_pool"))
                pool.tensor_scalar(ve, mv[:, 1:2], EPS, None, ALU.add).then_inc(S(ve_sem), 1)
                pool.wait_ge(S(ve_sem), n)
                pool.tensor_tensor(rstd, ve, mem.minus_half, ALU.pow).then_inc(S(rstd_sem), 1)

            with pool.Fori(0, T) as m:
                inverse_deviation(m + 1, "aggr3", "ve3", "rstd3")

            with pool.Fori(0, T) as i:
                inverse_deviation(i + 1, "aggr4", "ve4", "rstd4")

        @block.scalar
        def _(act):
            def x_side(m, b):
                act.wait_ge(S("x3_made"), m + 1)
                act.wait_ge(S("xT_psum"), m + 1)
                act.activation(x3pair[b][:, 0, :], x3[:, ds(m, 1), :].rearrange("p a b -> p (a b)"),
                               ACT.Copy).then_inc(S("x3_high"), 1)

            x_side(0, 0)
            x_side(1, 1)
            for k in range(K4):
                act.wait_ge(S("g_psum"), k + 1)
                act.activation(g[:, 0, k, :], psum[:, 4 + k, :], ACT.Copy, scale=1.0 / S64).then_inc(S("g_high"), 1)
            act.wait_ge(S("small_psum"), 1)
            act.activation(wv[:, 0, :, :], wvt, ACT.Copy, scale=S64).then_inc(S("wv_high"), 1)

            def v_high(m):
                act.wait_ge(S("v_sum"), m + 1)
                act.activation(value(ds(m, 1), 0), v_sum, ACT.Copy, scale=S64).then_inc(S("v_high"), 1)

            def xT_out(m):
                act.wait_ge(S("xT_psum"), m + 3)
                act.activation(big[:, ds(m, 1), 0:1024].rearrange("p a (k c) -> p (a k) c", c=P),
                               mem.bank16(2), ACT.Copy).then_inc(S("xT_made"), 1)

            with pairs(act, 2, T) as m:
                for b in range(2):
                    xT_out(m + b - 2)
                    x_side(m + b, b)
                    v_high(m + b - 2)
            def turned_out(c):
                for e in range(K4):
                    act.wait_ge(S("t_sum"), c * K4 + e + 1)
                    act.activation(tT(slice(4 * c, 4 * c + 4), 0, e),
                                   t_sum[e % 2].rearrange("p (a b) -> p a b", b=P), ACT.Copy).then_inc(S("t_high4"), 1)

            xT_out(T - 2)
            turned_out(0)
            v_high(T - 2)
            xT_out(T - 1)
            turned_out(1)
            v_high(T - 1)
            turned_out(2)
            turned_out(3)

            def numerators(i, b, parts=1):
                act.wait_ge(S("bias"), i + 1)
                act.activation(rows[b], rows[b], ACT.Exp, bias=bias[:, b:b + 1], scale=1.0 / ZS,
                               accum_out=total[:, b:b + 1]).then_inc(S("exp"), 1)
                act.wait_ge(S("exp"), i + 1)
                act.wait_ge(S("pT_l"), i * 2 + 2)
                for h in range(parts):
                    half = slice(h * N // parts, (h + 1) * N // parts)
                    act.activation(ppair[b][:, 0, half], rows[b][:, half], ACT.Copy).then_inc(S("p_high"), 1)

            def evacuate(i, b):
                for q in range(2):
                    act.wait_ge(S("pT_h"), i * 2 + (q + 1))
                    if q == 0:
                        act.wait_ge(S("pv"), i + 1)
                    act.activation(pT(b, 0, slice(8 * q, 8 * q + 8)), mem.bank16(4 + q), ACT.Copy)\
                        .then_inc(S("pT_high"), 1)

            def weighted(i, b):
                act.wait_ge(S("pv"), i + 3)
                act.wait_ge(S("inv"), i + 1)
                act.activation(attended[b], psum[:, 7, :], ACT.Relu, scale=inv[:, b:b + 1]).then_inc(S("relu"), 1)

            numerators(0, 0)
            evacuate(0, 0)
            with pairs(act, 0, T - 2) as i:
                for b in range(2):
                    numerators(i + b + 1, 1 - b)
                    weighted(i + b, b)
                    evacuate(i + b + 1, 1 - b)
            numerators(T - 1, 1, parts=2)
            weighted(T - 2, 0)
            evacuate(T - 1, 1)
            weighted(T - 1, 1)

        @block.vector
        def _(dve):
            dve.sem_inc(S("x2_free"), 2)
            dve.sem_inc(S("l3_free"), 2)
            dve.sem_inc(S("xT_psum"), 2)
            dve.sem_inc(S("adj_free"), 2)
            dve.sem_inc(S("pT_l"), 4)
            dve.sem_inc(S("pv"), 2)
            def convolved(m, b):
                n = m + 1
                xm = x3[:, ds(m, 1), :].rearrange("p a b -> p (a b)")
                dve.wait_ge(S("l3_psum"), n)
                dve.wait_ge(S(f"x2_in{b}"), (m - b) * 8 + 16)
                dve.scalar_tensor_tensor(hbuf, psum[:, b, :], mem.f_out, x2in[b], ALU.mult, ALU.add)\
                    .then_inc(S("h3"), 1)
                dve.wait_ge(S("h3"), n)
                dve.sem_inc(S("x2_free"), 1)
                dve.sem_inc(S("l3_free"), 1)
                dve.bn_stats(stats, hbuf).then_inc(S("stats3"), 1)
                wait_apart(dve, S("stats3"), n, S("waited_dve"))
                dve.bn_aggr(mv, stats).then_inc(S("aggr3"), 1)
                dve.wait_ge(S("rstd3"), n)
                dve.tensor_scalar(xm, hbuf, mv[:, 0:1], rstd, ALU.subtract, ALU.mult).then_inc(S("x3_made"), 1)
                dve.wait_ge(S("x3_high"), n)
                dve.tensor_tensor(x3pair[b][:, 1, :], xm, x3pair[b][:, 0, :], ALU.subtract).then_inc(S("x3_low"), 1)

            def row_constant(m):
                dve.scalar_tensor_tensor(psum[:, 5, :], x3[:, ds(m, 1), :].rearrange("p a b -> p (a b)"),
                                         SCALE / (S64 * S64), psum[:, 3, :], ALU.mult, ALU.mult,
                                         accum_out=ci_part[:, ds(m, 1)]).then_inc(S("ci"), 1)
                dve.wait_ge(S("ci"), m + 1)

            def valued(m):
                n = m + 1
                dve.wait_ge(S("v_psum"), n)
                dve.scalar_tensor_tensor(v_sum, psum[:, 4, :], 1.0 / S64, bv, ALU.mult, ALU.add).then_inc(S("v_sum"), 1)
                dve.wait_ge(S("v_high"), n)
                dve.scalar_tensor_tensor(value(ds(m, 1), 1), v_sum, S64, value(ds(m, 1), 0), ALU.mult,
                                         ALU.subtract).then_inc(S("v_low"), 1)
                dve.wait_ge(S("v_low"), n)

            dve.wait_ge(S("biases_in"), 32)
            dve.tensor_scalar(biases64, biases, S64, None, ALU.mult).then_inc(S("bias_pairs"), 1)
            dve.wait_ge(S("bias_pairs"), 1)
            dve.tensor_copy(bias_high, biases64).then_inc(S("bias_pairs"), 1)
            for o in range(K4):
                dve.tensor_scalar(bk_wide[:, 0, o, :], ident[:], 0.0, biases64[:, K4 + o:K4 + o + 1], ALU.mult,
                                  ALU.add).then_inc(S("bias_pairs"), 1)
            dve.wait_ge(S("bias_pairs"), 2 + K4)
            dve.tensor_tensor(bias_low, biases64, bias_high, ALU.subtract).then_inc(S("bias_pairs"), 1)
            for o in range(K4):
                dve.tensor_scalar(bk_wide[:, 1, o, :], bk_wide[:, 0, o, :], -1.0, biases64[:, K4 + o:K4 + o + 1],
                                  ALU.mult, ALU.add).then_inc(S("bias_pairs"), 1)
            dve.tensor_tensor(tmpc, biases[:, 0:K4], biases[:, K4:2 * K4], ALU.mult).then_inc(S("bqk"), 1)
            dve.wait_ge(S("bqk"), 1)
            dve.reduce_sum(bqk_sum, tmpc, axis=AX.X).then_inc(S("bqk"), 1)
            convolved(0, 0)
            convolved(1, 1)
            dve.wait_ge(S("small_psum"), 1)
            dve.tensor_scalar(gk, psum[:, 2, 0:K4], SCALE / (S64 * S64), None, ALU.mult).then_inc(S("gk"), 1)
            dve.tensor_scalar(c0, psum[:, 2, K4:K4 + 1], SCALE * P, None, ALU.mult).then_inc(S("c0"), 1)
            for k in range(K4):
                dve.wait_ge(S("g_high"), k + 1)
                dve.scalar_tensor_tensor(g[:, 1, k, :], psum[:, 4 + k, :], 1.0 / S64, g[:, 0, k, :], ALU.mult,
                                         ALU.subtract).then_inc(S("g_low"), 1)
            dve.wait_ge(S("g_low"), K4)
            row_constant(0)
            row_constant(1)
            dve.wait_ge(S("wv_high"), 1)
            dve.scalar_tensor_tensor(wv[:, 1, :, :].rearrange("p a b -> p (a b)"), wvt.rearrange("p a b -> p (a b)"), S64,
                                     wv[:, 0, :, :].rearrange("p a b -> p (a b)"), ALU.mult, ALU.subtract)\
                .then_inc(S("wv_low"), 1)
            dve.wait_ge(S("wv_low"), 1)
            dve.wait_ge(S("bv_in"), 16)

            with pairs(dve, 2, T) as m:
                for b in range(2):
                    convolved(m + b, b)
                    row_constant(m + b)
                    valued(m + b - 2)
            def turned_out(c):
                for e in range(K4):
                    n = c * K4 + e + 1
                    dve.wait_ge(S("t_psum"), n)
                    dve.tensor_scalar(t_sum[e % 2], psum[:, T_BANK[e], :], SCALE / S64, gk[:, e:e + 1], ALU.mult,
                                      ALU.add).then_inc(S("t_sum"), 1)
                    dve.wait_ge(S("t_high4"), n)
                    tiles = slice(4 * c, 4 * c + 4)
                    dve.tensor_tensor(tT(tiles, 1, e), t_sum[e % 2].rearrange("p (a b) -> p a b", b=P),
                                      tT(tiles, 0, e), ALU.subtract).then_inc(S("t_made"), 1)

            turned_out(0)
            valued(T - 2)
            turned_out(1)
            valued(T - 1)
            turned_out(2)
            turned_out(3)
            dve.wait_ge(S("c0"), 1)
            dve.tensor_scalar(ci, ci_part, c0, None, ALU.add).then_inc(S("ci"), 1)
            dve.wait_ge(S("ci"), T + 1)

            def scored(i, b):
                dve.wait_ge(S(f"adj_in{b}"), (i - b) * 8 + 16)
                for h in range(2):
                    dve.wait_ge(S("z"), i * 2 + (h + 1))
                    part = rows[b][:, h * HALF:(h + 1) * HALF]
                    dve.scalar_tensor_tensor(part, psum[:, 2 * h:2 * h + 2, :].rearrange("p a b -> p (a b)"),
                                             ci[:, ds(i, 1)], part, ALU.add, ALU.mult).then_inc(S("scored"), 1)

            def maximum(i, b):
                dve.wait_ge(S("scored"), i * 2 + 2)
                dve.tensor_scalar(mask, rows[b], 0.0, ZS * MASKED, ALU.is_equal, ALU.mult).then_inc(S("mask"), 1)
                wait_apart(dve, S("mask"), i + 1, S("waited_dve"))
                dve.tensor_tensor_reduce(out=rows[b], in0=rows[b], in1=mask, scale=1.0, scalar=-3.0e38,
                                         op0=ALU.add, op1=ALU.max, accum_out=top[:, b:b + 1]).then_inc(S("top"), 1)
                dve.wait_ge(S("top"), i + 1)
                dve.tensor_scalar(bias[:, b:b + 1], top[:, b:b + 1], -1.0 / ZS, float(np.log(PSCALE)), ALU.mult,
                                  ALU.add).then_inc(S("bias"), 1)

            def p_low(i, b, parts=1):
                for h in range(parts):
                    half = slice(h * N // parts, (h + 1) * N // parts)
                    dve.wait_ge(S("p_high"), i + (h + 1))
                    dve.tensor_tensor(ppair[b][:, 1, half], rows[b][:, half], ppair[b][:, 0, half],
                                      ALU.subtract).then_inc(S("p_low"), 1)
                dve.reciprocal(top[:, b:b + 1], total[:, b:b + 1]).then_inc(S("recip"), 1)
                dve.wait_ge(S("recip"), i + 1)
                dve.tensor_scalar(inv[:, b:b + 1], top[:, b:b + 1], 1.0 / S64, None, ALU.mult).then_inc(S("inv"), 1)
                dve.wait_ge(S("p_low"), i + 1)
                dve.sem_inc(S("adj_free"), 1)

            def evacuate(i, b):
                for q in range(2):
                    dve.wait_ge(S("pT_l"), i * 2 + (q + 5))
                    if q == 0:
                        dve.wait_ge(S("pv"), i + 1)
                    dve.tensor_copy(pT(b, 1, slice(8 * q, 8 * q + 8)), mem.bank16(6 if q == 0 else 4))\
                        .then_inc(S("pT_low"), 1)

            def finished(i, b):
                n = i + 1
                xi = x3[:, ds(i, 1), :].rearrange("p a b -> p (a b)")
                dve.wait_ge(S("relu"), n)
                dve.tensor_tensor(attended[b], attended[b], xi, ALU.add).then_inc(S("h4"), 1)
                dve.wait_ge(S("h4"), n)
                dve.bn_stats(stats, attended[b]).then_inc(S("stats4"), 1)
                wait_apart(dve, S("stats4"), n, S("waited_dve"))
                dve.bn_aggr(mv, stats).then_inc(S("aggr4"), 1)
                dve.wait_ge(S("rstd4"), n)
                dve.tensor_scalar(xi, attended[b], mv[:, 0:1], rstd, ALU.subtract, ALU.mult).then_inc(S("out_made"), 1)

            scored(0, 0)
            maximum(0, 0)
            p_low(0, 0)
            evacuate(0, 0)
            with pairs(dve, 0, T - 2) as i:
                for b in range(2):
                    scored(i + b + 1, 1 - b)
                    maximum(i + b + 1, 1 - b)
                    p_low(i + b + 1, 1 - b)
                    finished(i + b, b)
                    evacuate(i + b + 1, 1 - b)
            scored(T - 1, 1)
            maximum(T - 1, 1)
            p_low(T - 1, 1, parts=2)
            evacuate(T - 1, 1)
            finished(T - 2, 0)
            finished(T - 1, 1)

        @block.tensor
        def _(pe):
            def sums(m, b):
                pe.wait_ge(S("l3_free"), m + 1)
                convolve(pe, mem, m, b, range(T // 2))
                transposes(m - 2, b)
                convolve(pe, mem, m, b, range(T // 2, T)).then_inc(S("l3_psum"), 1)

            def transposes(m, b):
                pe.wait_ge(S("x3_low"), m + 1)
                for h in range(2):
                    for k in range(K4):
                        last = pe.transpose(mem.bank16(2)[:, h * K4 + k, :], x3pair[b][:, h, k * P:(k + 1) * P], ident[:])
                last.then_inc(S("xT_psum"), 1)

            def project(m):
                pe.wait_ge(S("xT_made"), m + 1)
                if not isinstance(m, int) or m > 0:
                    pe.wait_ge(S("v_low"), m)
                for part, other in ((0, 0), (0, 1), (1, 0)):
                    for k in range(K4):
                        last = pe.matmul(psum[:, 4, :], xT(ds(m, 1), part, k).rearrange("p a b -> p (a b)"),
                                         wv[:, other, k, :], start=((part, other, k) == (0, 0, 0)),
                                         stop=((part, k) == (1, K4 - 1)))
                last.then_inc(S("v_psum"), 1)

            for m in range(2):
                convolve(pe, mem, m, m, range(T - 1, T)).then_inc(S("l3_psum"), 1)
            pe.wait_ge(S("weights_low"), 2)
            for d in range(K4):
                for part, other in ((0, 0), (0, 1), (1, 0)):
                    for o in range(K4):
                        last = pe.matmul(psum[:, 4 + d, :], wq[:, part, o, d * P:(d + 1) * P], wk[:, other, o, :],
                                         start=((part, other, o) == (0, 0, 0)), stop=((part, o) == (1, K4 - 1)))
                last.then_inc(S("g_psum"), 1)
            pe.wait_ge(S("bias_pairs"), 3 + 2 * K4)
            for d in range(K4):
                for part, bias_col in ((0, bias_high), (0, bias_low), (1, bias_high)):
                    for o in range(K4):
                        pe.matmul(psum[:, 2, d:d + 1], wk[:, part, o, d * P:(d + 1) * P], bias_col[:, o:o + 1],
                                  start=((part, o) == (0, 0) and bias_col is bias_high),
                                  stop=((part, o) == (1, K4 - 1)))
            pe.wait_ge(S("bqk"), 2)
            pe.matmul(psum[:, 2, K4:K4 + 1], mem.mean_matrix[:], bqk_sum, start=True, stop=True)
            for part, other in ((0, 0), (0, 1), (1, 0)):
                for o in range(K4):
                    last = pe.matmul(psum[:, 3, :], bk_wide[:, part, o, :], wq[:, other, o, :],
                                     start=((part, other, o) == (0, 0, 0)), stop=((part, o) == (1, K4 - 1)))
            last.then_inc(S("small_psum"), 1)
            pe.wait_ge(S("gk"), 1)
            pe.wait_ge(S("c0"), 1)
            sums(2, 0)
            pe.wait_ge(S("g_low"), K4)
            pe.wait_ge(S("wv_low"), 1)
            project(0)
            sums(3, 1)
            project(1)
            with pairs(pe, 4, T) as m:
                for b in range(2):
                    sums(m + b, b)
                    project(m + b - 2)
            def turn_x(c):
                for e in range(K4):
                    if c:
                        pe.wait_ge(S("t_sum"), (c - 1) * K4 + e + 1)
                    elif e == 2:
                        pe.wait_ge(S("h3"), T)
                    for part, other in ((0, 0), (0, 1), (1, 0)):
                        for k in range(K4):
                            last = pe.matmul(psum[:, T_BANK[e], :], g[:, part, k, e * P:(e + 1) * P],
                                             xT(slice(4 * c, 4 * c + 4), other, k),
                                             start=((part, other, k) == (0, 0, 0)), stop=((part, k) == (1, K4 - 1)))
                    last.then_inc(S("t_psum"), 1)

            transposes(T - 2, 0)
            turn_x(0)
            project(T - 2)
            transposes(T - 1, 1)
            turn_x(1)
            project(T - 1)
            turn_x(2)
            turn_x(3)

            def scores(i, first=False, turning=None):
                for c in range(4):
                    if c == 3 and turning is not None:
                        turned(i - 1, turning)
                    if first:
                        if c < 2:
                            pe.wait_ge(S("t_sum"), 3 * K4 + T_BANK.index(c) + 1)
                    elif c % 2 == 0:
                        pe.wait_ge(S("scored"), i * 2 - 1 + c // 2)
                    for part, other in ((0, 0), (0, 1), (1, 0)):
                        for k in range(K4):
                            last = pe.matmul(psum[:, c, :], tT(ds(i, 1), part, k).rearrange("p a b -> p (a b)"),
                                             xT(slice(4 * c, 4 * c + 4), other, k),
                                             start=((part, other, k) == (0, 0, 0)), stop=((part, k) == (1, K4 - 1)))
                    if c % 2:
                        last.then_inc(S("z"), 1)

            def turn(b, part, q, bank, done):
                for j in range(8):
                    last = pe.transpose(mem.bank16(bank)[:, j, :],
                                        ppair[b][:, part, (8 * q + j) * P:(8 * q + j + 1) * P], ident[:])
                last.then_inc(S(done), 1)

            def turned(i, b, last_tile=False):
                pe.wait_ge(S("p_high"), i + 1)
                turn(b, 0, 0, 4, "pT_h")
                pe.wait_ge(S("p_low"), i + 1)
                turn(b, 1, 0, 6, "pT_l")
                if last_tile:
                    pe.wait_ge(S("p_high"), T + 1)
                turn(b, 0, 1, 5, "pT_h")

            def weigh(i, b, first=False, last_tile=False):
                pe.wait_ge(S("pT_high"), i * 2 + 1)
                if last_tile:
                    pe.wait_ge(S("p_low"), T + 1)
                turn(b, 1, 1, 4, "pT_l")
                if not first:
                    pe.wait_ge(S("relu"), i)
                for j in range(T):
                    if j % 8 == 0:
                        pe.wait_ge(S("pT_high"), i * 2 + (j // 8 + 1))
                        pe.wait_ge(S("pT_low"), i * 2 + (j // 8 + 1))
                    high, low = (pT(b, h, slice(j, j + 1)).rearrange("p a b -> p (a b)") for h in range(2))
                    pe.matmul(psum[:, 7, :], high, value(slice(j, j + 1), 0), start=(j == 0), stop=False)
                    pe.matmul(psum[:, 7, :], high, value(slice(j, j + 1), 1), start=False, stop=False)
                    last = pe.matmul(psum[:, 7, :], low, value(slice(j, j + 1), 0), start=False, stop=(j == T - 1))
                last.then_inc(S("pv"), 1)

            pe.wait_ge(S("t_made"), K4)
            scores(0, first=True)
            pe.wait_ge(S("t_made"), 4 * K4)
            scores(1)
            turned(0, 0)
            weigh(0, 0, first=True)
            scores(2, turning=1)
            with pairs(pe, 1, T - 3) as i:
                for j in range(2):
                    weigh(i + j, 1 - j)
                    scores(i + j + 2, turning=j)
            weigh(T - 3, 1)
            scores(T - 1, turning=0)
            weigh(T - 2, 0)
            turned(T - 1, 1, last_tile=True)
            weigh(T - 1, 1, last_tile=True)


def gnn_stack(nc, a, out):
    with ExitStack() as ctx:
        mem = Memory(nc, ctx)
        x1_dram = nc.dram_tensor("x1_scratch", [N, D], FP32, kind="Internal").ap()
        x2_dram = nc.dram_tensor("x2_scratch", [N, D], FP32, kind="Internal").ap()
        flag = ctx.enter_context(nc.sbuf_tensor("flag", [1, 1], INT32))
        r_act, c_sup = propagation(nc, mem, a, x1_dram, x2_dram, flag)
        ones_off_diagonal = nc.values_load(flag[0:1, 0:1],
                                           skip_runtime_bounds_check_because="it is only compared with 0")
        with nc.If(ones_off_diagonal > 0):
            relation_attention(nc, mem, a, x1_dram, x2_dram, r_act, c_sup)
        attention(nc, mem, a, x2_dram, out)


def kernel(**inputs):
    import concourse.bacc as bacc
    from concourse.bass_utils import run_bass_kernel_spmd

    def column(v):
        return np.ascontiguousarray(np.asarray(v).reshape(K4, P).T)

    x, adj = np.asarray(inputs["x"]), np.asarray(inputs["adj"])
    pairs_in = np.asarray(inputs["L1_gnn_rel_pair_index"])
    padded = np.full((2, ET * P), -1, pairs_in.dtype)
    padded[:, :EDGES] = pairs_in.T
    edges = np.ascontiguousarray(padded.reshape(2 * ET, P).T)
    scalars = [inputs[n] for n in ("L2_gnn_act_alpha", "L2_gnn_wgt_alpha", "L2_gnn_act_alpha2",
                                   "L2_gnn_adj_scaling_factor")]
    arrays = {
        "x": x, "adj": adj, "adjT": np.ascontiguousarray(adj.T),
        "scalars": np.tile(np.stack([np.asarray(v).reshape(()) for v in scalars]), (P, 1)),
        "L2_w": np.asarray(inputs["L2_gnn_weight"]),
        "W_q": np.asarray(inputs["L3_gnn_W_q"]), "W_k": np.asarray(inputs["L3_gnn_W_k"]),
        "W_vT": np.ascontiguousarray(np.asarray(inputs["L3_gnn_W_v"]).T),
        "b_q": column(inputs["L3_gnn_b_q"]), "b_k": column(inputs["L3_gnn_b_k"]),
        "b_v": np.asarray(inputs["L3_gnn_b_v"]).reshape(1, D),
        "L1_wqT": np.ascontiguousarray(np.asarray(inputs["L1_gnn_Wq"]).T),
        "L1_wkT": np.ascontiguousarray(np.asarray(inputs["L1_gnn_Wk"]).T),
        "L1_bq": column(inputs["L1_gnn_bq"]), "L1_bk": column(inputs["L1_gnn_bk"]),
        "edges": edges, "iota": np.tile(np.arange(N, dtype=np.float32), (P, 1)),
    }
    nc = bacc.Bacc("TRN2", target_bir_lowering=False, num_devices=1)
    args = {n: nc.dram_tensor(f"in_{n}", v.shape, mybir.dt.from_np(v.dtype), kind="ExternalInput").ap()
            for n, v in arrays.items()}
    out = nc.dram_tensor("out_x", [N, D], FP32, kind="ExternalOutput").ap()
    gnn_stack(nc, args, out)
    result = run_bass_kernel_spmd(nc, [{f"in_{n}": v for n, v in arrays.items()}], core_ids=[0])
    return result.results[0]["out_x"]
```
